# Optimizing a Trainium2 kernel written in Bass

```python
import numpy as np
import jax
import jax.numpy as jnp

def _softmax(x, axis=-1):
    return jax.nn.softmax(x, axis=axis)

def _gelu(x):
    return jax.nn.gelu(x, approximate=True)

def _silu(x):
    return jax.nn.silu(x)

def _sigmoid(x):
    return jax.nn.sigmoid(x)

def _layernorm(x, axis=-1, eps=1e-05):
    m = jnp.mean(x, axis=axis, keepdims=True)
    v = jnp.var(x, axis=axis, keepdims=True)
    return (x - m) / jnp.sqrt(v + eps)

def _scatter_add(tgt, idx, src, axis=0):
    return tgt.at[idx].add(src)

def _segment_sum(src, seg, n):
    return jax.ops.segment_sum(src, seg, n)
kernel_name = 'mk_early_fusion_d1_tok_img256_r4_1adbbe'

def setup_inputs(seed: int=0):
    np.random.seed(seed)
    _w = jnp.asarray

    def _rec_inputs():
        import jax
        import jax.numpy as jnp
        _rk = jax.random.key(seed)
        x = -0.000392918 + 0.999932 * jax.random.normal(jax.random.fold_in(_rk, 1), (8, 64, 64, 64), jnp.float32)
        txt = 0.0132895 + 1.06584 * jax.random.normal(jax.random.fold_in(_rk, 2), (8, 128, 64), jnp.float32)
        return (x, txt)
    x, txt = _rec_inputs()

    def _L0_tok_setup():
        import jax, jax.numpy as jnp
        import numpy as np
        from jax import lax
        BN_EPS = 1e-05
        key = jax.random.key(seed)
        ks = jax.random.split(key, 9)
        B, H, W, C = (16, 64, 64, 64)
        return {'x': jax.random.normal(ks[0], (B, H, W, C), dtype=jnp.float32), 'bn_gamma': jax.random.uniform(ks[1], (C,), dtype=jnp.float32, minval=0.5, maxval=1.5), 'bn_beta': jax.random.normal(ks[2], (C,), dtype=jnp.float32) * 0.1, 'bn_mean': jax.random.normal(ks[3], (C,), dtype=jnp.float32) * 0.1, 'bn_var': jax.random.uniform(ks[4], (C,), dtype=jnp.float32, minval=0.5, maxval=1.5), 'conv_w': jax.random.normal(ks[5], (C, 1, 3, 3), dtype=jnp.float32) * (1.0 / 3.0), 'conv_b': jax.random.normal(ks[6], (C,), dtype=jnp.float32) * 0.1, 'lin_w': jax.random.normal(ks[7], (C, C), dtype=jnp.float32) * (1.0 / np.sqrt(C)), 'lin_b': jax.random.normal(ks[8], (C,), dtype=jnp.float32) * 0.1}
    _L0_tok_all = _L0_tok_setup()
    _L0_tok_in = {k: v for k, v in _L0_tok_all.items() if k in ('bn_gamma', 'bn_beta', 'bn_mean', 'bn_var', 'conv_w', 'conv_b', 'lin_w', 'lin_b')}
    del _L0_tok_all

    def _L0_attn_setup():
        import jax, jax.numpy as jnp
        import numpy as np
        import math
        EMBED_DIM = 64
        SEQ_LEN = 1024
        BATCH = 4
        NUM_SCALES = (24.0, 720.0)
        key = jax.random.key(seed)
        ks = jax.random.split(key, 8)
        d = EMBED_DIM
        x = jax.random.normal(ks[0], (BATCH, SEQ_LEN, d), dtype=jnp.float32)
        s = 1.0 / math.sqrt(d)
        Wq = jax.random.uniform(ks[1], (d, d), jnp.float32, -s, s)
        bq = jax.random.uniform(ks[2], (d,), jnp.float32, -s, s)
        Wk = jax.random.uniform(ks[3], (d, d), jnp.float32, -s, s)
        bk = jax.random.uniform(ks[4], (d,), jnp.float32, -s, s)
        Wv = jax.random.uniform(ks[5], (d, d), jnp.float32, -s, s)
        bv = jax.random.uniform(ks[6], (d,), jnp.float32, -s, s)
        beta = jnp.ones((len(NUM_SCALES),), dtype=jnp.float32)
        return {'x': x, 'Wq': Wq, 'bq': bq, 'Wk': Wk, 'bk': bk, 'Wv': Wv, 'bv': bv, 'beta': beta}
    _L0_attn_all = _L0_attn_setup()
    _L0_attn_in = {k: v for k, v in _L0_attn_all.items() if k in ('Wq', 'bq', 'Wk', 'bk', 'Wv', 'bv', 'beta')}
    del _L0_attn_all

    def _L0_ffn_setup():
        import jax, jax.numpy as jnp
        import numpy as np
        B, S, H, F, E, K = (8, 1024, 64, 128, 16, 2)
        EPS = 1e-05
        key = jax.random.key(seed)
        ks = jax.random.split(key, 9)
        sc = 0.02
        return {'x': jax.random.normal(ks[0], (B, S, H), dtype=jnp.float32), 'gate_w': jax.random.normal(ks[1], (H, E), dtype=jnp.float32) * sc, 'gate_b': jnp.zeros((E,), dtype=jnp.float32), 'w1': jax.random.normal(ks[2], (E, H, F), dtype=jnp.float32) * sc, 'b1': jnp.zeros((E, F), dtype=jnp.float32), 'w2': jax.random.normal(ks[3], (E, F, H), dtype=jnp.float32) * sc, 'b2': jnp.zeros((E, H), dtype=jnp.float32), 'gamma': jnp.ones((H,), dtype=jnp.float32), 'beta': jnp.zeros((H,), dtype=jnp.float32)}
    _L0_ffn_all = _L0_ffn_setup()
    _L0_ffn_in = {k: v for k, v in _L0_ffn_all.items() if k in ('gate_w', 'gate_b', 'w1', 'b1', 'w2', 'b2', 'gamma', 'beta')}
    del _L0_ffn_all
    return {'x': x, 'txt': txt, 'L0_tok_bn_gamma': _L0_tok_in['bn_gamma'], 'L0_tok_bn_beta': _L0_tok_in['bn_beta'], 'L0_tok_bn_mean': _L0_tok_in['bn_mean'], 'L0_tok_bn_var': _L0_tok_in['bn_var'], 'L0_tok_conv_w': _L0_tok_in['conv_w'], 'L0_tok_conv_b': _L0_tok_in['conv_b'], 'L0_tok_lin_w': _L0_tok_in['lin_w'], 'L0_tok_lin_b': _L0_tok_in['lin_b'], 'L0_attn_Wq': _L0_attn_in['Wq'], 'L0_attn_bq': _L0_attn_in['bq'], 'L0_attn_Wk': _L0_attn_in['Wk'], 'L0_attn_bk': _L0_attn_in['bk'], 'L0_attn_Wv': _L0_attn_in['Wv'], 'L0_attn_bv': _L0_attn_in['bv'], 'L0_attn_beta': _L0_attn_in['beta'], 'L0_ffn_gate_w': _L0_ffn_in['gate_w'], 'L0_ffn_gate_b': _L0_ffn_in['gate_b'], 'L0_ffn_w1': _L0_ffn_in['w1'], 'L0_ffn_b1': _L0_ffn_in['b1'], 'L0_ffn_w2': _L0_ffn_in['w2'], 'L0_ffn_b2': _L0_ffn_in['b2'], 'L0_ffn_gamma': _L0_ffn_in['gamma'], 'L0_ffn_beta': _L0_ffn_in['beta']}

def reference(x, txt, L0_tok_bn_gamma, L0_tok_bn_beta, L0_tok_bn_mean, L0_tok_bn_var, L0_tok_conv_w, L0_tok_conv_b, L0_tok_lin_w, L0_tok_lin_b, L0_attn_Wq, L0_attn_bq, L0_attn_Wk, L0_attn_bk, L0_attn_Wv, L0_attn_bv, L0_attn_beta, L0_ffn_gate_w, L0_ffn_gate_b, L0_ffn_w1, L0_ffn_b1, L0_ffn_w2, L0_ffn_b2, L0_ffn_gamma, L0_ffn_beta):
    import jax
    import jax.numpy as jnp

    def _L0_tok_ref(x, bn_gamma, bn_beta, bn_mean, bn_var, conv_w, conv_b, lin_w, lin_b):
        import jax, jax.numpy as jnp
        import numpy as np
        from jax import lax
        BN_EPS = 1e-05
        x = jnp.transpose(x, (0, 3, 1, 2))
        B, C, H, W = x.shape
        scale = bn_gamma / jnp.sqrt(bn_var + BN_EPS)
        shift = bn_beta - bn_mean * scale
        xn = x * scale[None, :, None, None] + shift[None, :, None, None]
        y = lax.conv_general_dilated(xn, conv_w, window_strides=(1, 1), padding='SAME', feature_group_count=C, dimension_numbers=('NCHW', 'OIHW', 'NCHW')) + conv_b[None, :, None, None]
        y = jnp.transpose(y.reshape(B, C, H * W), (0, 2, 1))
        return jnp.einsum('bnc,dc->bnd', y, lin_w) + lin_b

    def _L0_attn_ref(x, Wq, bq, Wk, bk, Wv, bv, beta):
        import jax, jax.numpy as jnp
        import numpy as np
        import math
        EMBED_DIM = 64
        SEQ_LEN = 1024
        BATCH = 4
        NUM_SCALES = (24.0, 720.0)
        d = x.shape[-1]
        seq_len = x.shape[1]
        sqrt_d = jnp.asarray(math.sqrt(d), x.dtype)
        Q = jnp.einsum('bsd,ed->bse', x, Wq) + bq
        K = jnp.einsum('bsd,ed->bse', x, Wk) + bk
        V = jnp.einsum('bsd,ed->bse', x, Wv) + bv
        attn = jnp.einsum('bse,bte->bst', Q, K) / sqrt_d
        idx = jnp.arange(seq_len, dtype=jnp.float32)
        absdiff = jnp.abs(idx[:, None] - idx[None, :])
        two_pi = jnp.asarray(2.0 * math.pi, jnp.float32)
        bias = jnp.zeros((seq_len, seq_len), dtype=jnp.float32)
        for n, T in enumerate(NUM_SCALES):
            bias = bias + beta[n] * jnp.cos(two_pi * absdiff / T)
        scores = jax.nn.softmax(attn + bias[None, :, :], axis=-1)
        return jnp.einsum('bst,bte->bse', scores, V)

    def _L0_ffn_ref(x, gate_w, gate_b, w1, b1, w2, b2, gamma, beta):
        import jax, jax.numpy as jnp
        import numpy as np
        B, S, H, F, E, K = (8, 1024, 64, 128, 16, 2)
        EPS = 1e-05
        gate_logits = x @ gate_w + gate_b
        topk_vals, topk_idx = jax.lax.top_k(gate_logits, K)
        topk_w = jax.nn.softmax(topk_vals, axis=-1)
        h = jax.nn.relu(jnp.einsum('bsh,ehf->bsef', x, w1) + b1)
        expert_out = jnp.einsum('bsef,efh->bseh', h, w2) + b2
        sel = jnp.take_along_axis(expert_out, topk_idx[:, :, :, None], axis=2)
        moe = jnp.sum(topk_w[..., None] * sel, axis=2)
        y = x + moe
        mu = jnp.mean(y, axis=-1, keepdims=True)
        var = jnp.var(y, axis=-1, keepdims=True)
        return (y - mu) / jnp.sqrt(var + EPS) * gamma + beta
    h = _L0_tok_ref(x, L0_tok_bn_gamma, L0_tok_bn_beta, L0_tok_bn_mean, L0_tok_bn_var, L0_tok_conv_w, L0_tok_conv_b, L0_tok_lin_w, L0_tok_lin_b)
    h = jnp.concatenate([h, txt], axis=1)
    h = h + _L0_attn_ref(_layernorm(h, axis=-1), L0_attn_Wq, L0_attn_bq, L0_attn_Wk, L0_attn_bk, L0_attn_Wv, L0_attn_bv, L0_attn_beta)
    h = h + _L0_ffn_ref(_layernorm(h, axis=-1), L0_ffn_gate_w, L0_ffn_gate_b, L0_ffn_w1, L0_ffn_b1, L0_ffn_w2, L0_ffn_b2, L0_ffn_gamma, L0_ffn_beta)
    return h

_drawn_inputs = setup_inputs


def setup_inputs(seed=0):
    import zlib

    import numpy as np

    out = dict(_drawn_inputs(seed))
    spreads = {'L0_attn_beta': (1.0, 0.6),
     'L0_ffn_gate_b': (0.0, 0.1),
     'L0_ffn_b1': (0.0, 0.8),
     'L0_ffn_b2': (0.0, 0.304),
     'L0_ffn_gamma': (1.0, 0.2),
     'L0_ffn_beta': (0.0, 0.1)}
    factors = {'L0_attn_bq': 8.0, 'L0_attn_bk': 64.0, 'L0_ffn_w1': 7.334, 'L0_ffn_w2': 5.518}
    for name, (base, spread) in spreads.items():
        noise = np.random.default_rng([zlib.crc32(name.encode()), seed]).standard_normal(out[name].shape)
        drawn = base * np.exp(spread * noise) if base else spread * noise
        out[name] = jnp.asarray(drawn.astype(out[name].dtype))
    for name, factor in factors.items():
        out[name] = (out[name] * factor).astype(out[name].dtype)
    return out
```

```python
from contextlib import ExitStack

import concourse.bass as bass
import numpy as np
from concourse import mybir

F32 = mybir.dt.float32
F32R = mybir.dt.float32r
U32 = mybir.dt.uint32
ALU = mybir.AluOpType
ACT = mybir.ActivationFunctionType
AX = mybir.AxisListType

P = 128
BATCH, SIDE, CH = 8, 64, 64
IMAGE = SIDE * SIDE
TEXT = 128
SEQ = IMAGE + TEXT
TILES = SEQ // P
IMAGE_TILES = IMAGE // P
ALL_TILES = BATCH * TILES
EXPERTS, HIDDEN = 16, 128
EPS = 1e-5
PERIODS = (24.0, 720.0)
PAD = SIDE + 2
BANK = 512
ds = bass.ds

CHUNK_TILES = 3
CHUNK = CHUNK_TILES * P
CHUNKS = TILES // CHUNK_TILES
STEPS = BATCH * CHUNKS
UNITS = (TILES + 1) // 2
BIAS_ROWS = 2 * len(PERIODS)
EXTRA = 1 + 3 * BIAS_ROWS
ROWS1 = CH + EXTRA
P_SLOTS = 3
PIECES = [(a, min(BANK, SEQ - a)) for a in range(0, SEQ, BANK)]
MAXES = CHUNK_TILES * len(PIECES)


def constants():
    s = np.arange(SEQ, dtype=np.float64)
    waves = []
    for period in PERIODS:
        waves += [np.cos(2 * np.pi * s / period), np.sin(2 * np.pi * s / period)]
    waves = np.stack(waves)
    rows = np.concatenate([np.ones((1, SEQ)), waves, waves, waves]).astype(np.float32)
    masks = np.zeros((EXTRA, 4), np.float32)
    n = BIAS_ROWS
    masks[:1 + 2 * n, 0] = 1
    masks[1 + 2 * n:, 1] = 1
    masks[1:1 + n, 2] = masks[1 + 2 * n:, 2] = 1
    masks[1 + n:1 + 2 * n, 3] = 1
    ones_col = np.zeros((P, 1), np.float32)
    ones_col[CH - 1] = ones_col[2 * CH - 1] = 1
    eye = np.eye(P, dtype=np.float32)
    pick = np.zeros((48, EXPERTS, P), np.float32)
    for e in range(EXPERTS):
        pick[e, e] = pick[32 + e, e] = 1
    iota = np.broadcast_to(np.arange(EXPERTS, dtype=np.float32), (P, EXPERTS)).copy()
    return {"waves": rows, "masks": masks, "sum_col": ones_col, "eye": eye,
            "pick": pick.reshape(48, EXPERTS * P), "iota": iota}


def col(ap, n=None):
    return ap.rearrange("(p a) -> p a", a=1)


def stand_alone(eng, passed):
    eng.sem_inc(passed, 1)


def tokenise(nc, d, residual, eye):
    PAIRS = BATCH // 2
    GROUP = 4
    GROUPS = IMAGE_TILES // GROUP
    ROWS = GROUP * P // SIDE
    PARTS = 4
    PART = IMAGE // PARTS
    with ExitStack() as ctx:
        def sb(name, shape, dt=F32):
            return ctx.enter_context(nc.sbuf_tensor(name, shape, dt))

        def sem(name):
            return ctx.enter_context(nc.semaphore(name))

        tokens = sb("tokens", [P, 2, IMAGE_TILES, 2, CH])
        padded = sb("padded", [P, 2, PAD, PAD])
        conv = sb("conv", [P, 2, IMAGE])
        lin_rows = sb("lin_rows", [CH, CH])
        lin_both = sb("lin_both", [P, P])
        lin_bias = sb("lin_bias", [P, 2, CH])
        taps = sb("taps", [P, 9])
        vec = sb("vec", [P, 5])
        bn = sb("bn", [P, 4])
        shift = sb("shift", [P, 1])
        scale = sb("scale", [P, 1])
        ps_t = [ctx.enter_context(nc.psum_tensor(f"ps_t{i}", [P, BANK], F32)) for i in range(2)]
        ps_l = [ctx.enter_context(nc.psum_tensor(f"ps_l{i}", [P, BANK], F32)) for i in range(2)]
        ps_w = ctx.enter_context(nc.psum_tensor("ps_w", [P, BANK], F32))

        par_in, eye_in, text_in = sem("par_in"), sem("eye_in"), sem("text_in")
        x_in = [sem("x_in0"), sem("x_in1")]
        zeroed, bn_a, bn_b, bn_c = sem("zeroed"), sem("bn_a"), sem("bn_b"), sem("bn_c")
        lin_t, lin_c = sem("lin_t"), sem("lin_c")
        turned, padded_ready, conv_step, conv_ready = (
            sem("turned"), sem("padded_ready"), sem("conv_step"), sem("conv_ready"))
        lin_ready, lin_used = sem("lin_ready"), sem("lin_used")

        block = ctx.enter_context(nc.Block())

        @block.sync
        def _(sp):
            sp.dma_start(eye[:], d["eye"]).then_inc(eye_in, 16)
            n = 0
            for half in range(2):
                rows = slice(half * CH, half * CH + CH)
                for i, name in enumerate(["bn_gamma", "bn_beta", "bn_mean", "bn_var", "conv_b"]):
                    sp.dma_start(vec[rows, i:i + 1], col(d["L0_tok_" + name])).then_inc(par_in, 16)
                sp.dma_start(taps[rows, :], d["L0_tok_conv_w"].rearrange("c a h w -> c (a h w)")).then_inc(par_in, 16)
                sp.dma_start(lin_bias[:, half, :],
                             d["L0_tok_lin_b"].partition_broadcast(P)).then_inc(par_in, 16)
            sp.dma_start(lin_rows[:], d["L0_tok_lin_w"]).then_inc(par_in, 16)
            for q in range(PAIRS):
                if q >= 2:
                    sp.wait_ge(turned, (q - 1) * GROUPS)
                for i in range(2):
                    src = d["x"][2 * q + i].rearrange("(t r) w c -> (r w) t c", r=P // SIDE)
                    sp.dma_start(tokens[:, q % 2, :, i, :], src).then_inc(x_in[q % 2], 16)
            for b in range(BATCH):
                sp.dma_start(residual[:, b * TILES + IMAGE_TILES, :], d["txt"][b]).then_inc(text_in, 16)
            sp.wait_ge(text_in, 16 * BATCH)

        PARAMS = 16 * 15

        @block.gpsimd
        def _(pool):
            nc.gpsimd.memset(padded[:, 0], 0.0).then_inc(zeroed, 1)
            nc.gpsimd.memset(padded[:, 1], 0.0).then_inc(zeroed, 1)

        @block.scalar
        def _(act):
            act.wait_ge(bn_a, 1)
            nc.scalar.activation(bn[:, 1:2], bn[:, 0:1], ACT.Sqrt).then_inc(bn_b, 1)
            act.wait_ge(bn_c, 3)
            act.wait_ge(zeroed, 2)
            for q in range(PAIRS):
                for g in range(GROUPS):
                    k = q * GROUPS + g
                    act.wait_ge(turned, k + 1)
                    if g == 0 and q >= 2:
                        act.wait_ge(conv_ready, (q - 1) * PARTS)
                    nc.scalar.activation(
                        padded[:, q % 2, 1 + g * ROWS:1 + (g + 1) * ROWS, 1:1 + SIDE],
                        ps_t[k % 2][:, :].rearrange("p (r w) -> p r w", w=SIDE),
                        ACT.Identity, bias=shift[:, 0:1], scale=scale[:, 0:1]).then_inc(padded_ready, 1)

        @block.tensor
        def _(pe):
            pe.wait_ge(eye_in, 16)
            pe.wait_ge(par_in, PARAMS)
            nc.tensor.transpose(ps_w[0:CH, 0:CH], lin_rows[:], eye[0:CH, 0:CH]).then_inc(lin_t, 1)

            def turn(q):
                pe.wait_ge(x_in[q % 2], 32 * (q // 2 + 1))
                for g in range(GROUPS):
                    k = q * GROUPS + g
                    if k >= 2:
                        pe.wait_ge(padded_ready, k - 1)
                    for j in range(GROUP):
                        mm = nc.tensor.transpose(ps_t[k % 2][:, j * P:(j + 1) * P],
                                                 tokens[:, q % 2, g * GROUP + j, :, :], eye[:])
                    mm.then_inc(turned, 1)

            def linear(q):
                for g in range(GROUPS):
                    k = q * GROUPS + g
                    pe.wait_ge(conv_ready, q * PARTS + g * PARTS // GROUPS + 1)
                    if k >= 2:
                        pe.wait_ge(lin_used, k - 1)
                    for j in range(GROUP):
                        t = g * GROUP + j
                        mm = nc.tensor.matmul(ps_l[k % 2][:, j * P:(j + 1) * P],
                                              conv[:, q % 2, t * P:(t + 1) * P], lin_both[:],
                                              start=True, stop=True)
                    mm.then_inc(lin_ready, 1)

            turn(0)
            pe.wait_ge(lin_c, 3)
            for q in range(PAIRS):
                if q + 1 < PAIRS:
                    turn(q + 1)
                linear(q)

        @block.vector
        def _(dve):
            dve.wait_ge(par_in, PARAMS)
            nc.vector.tensor_scalar(bn[:, 0:1], vec[:, 3:4], EPS, None, ALU.add).then_inc(bn_a, 1)
            nc.vector.memset(lin_both[:], 0.0).then_inc(lin_c, 1)
            dve.wait_ge(lin_t, 1)
            dve.wait_ge(lin_c, 1)
            for h in range(2):
                nc.vector.tensor_copy(lin_both[h * CH:h * CH + CH, h * CH:h * CH + CH],
                                      ps_w[0:CH, 0:CH]).then_inc(lin_c, 1)
            dve.wait_ge(bn_b, 1)
            nc.vector.reciprocal(bn[:, 2:3], bn[:, 1:2]).then_inc(bn_c, 1)
            dve.wait_ge(bn_c, 1)
            nc.vector.tensor_tensor(scale[:], bn[:, 2:3], vec[:, 0:1], ALU.mult).then_inc(bn_c, 1)
            dve.wait_ge(bn_c, 2)
            nc.vector.scalar_tensor_tensor(out=bn[:, 3:4], in0=vec[:, 2:3], scalar=scale[:, 0:1],
                                           in1=vec[:, 1:2], op0=ALU.mult, op1=ALU.subtract).then_inc(bn_a, 1)
            dve.wait_ge(bn_a, 2)
            nc.vector.tensor_scalar(shift[:], bn[:, 3:4], -1.0, None, ALU.mult).then_inc(bn_c, 1)

            steps = [0]

            def convolve(q, part):
                r0 = part * SIDE // PARTS
                n = SIDE // PARTS
                acc = conv[:, q % 2, part * PART:(part + 1) * PART].rearrange("p (r w) -> p r w", w=SIDE)
                groups = min(GROUPS, (r0 + n) // ROWS + 1)
                dve.wait_ge(padded_ready, q * GROUPS + groups)
                if q >= 2 and part == 0:
                    dve.wait_ge(lin_ready, (q - 1) * GROUPS)
                for k in range(9):
                    window = padded[:, q % 2, r0 + k // 3:r0 + k // 3 + n, k % 3:k % 3 + SIDE]
                    if k == 0:
                        ins = nc.vector.tensor_scalar(acc, window, taps[:, 0:1], vec[:, 4:5], ALU.mult, ALU.add)
                    else:
                        dve.wait_ge(conv_step, steps[0])
                        ins = nc.vector.scalar_tensor_tensor(out=acc, in0=window, scalar=taps[:, k:k + 1],
                                                             in1=acc, op0=ALU.mult, op1=ALU.add)
                    if k < 8:
                        steps[0] += 1
                        ins.then_inc(conv_step, 1)
                    else:
                        ins.then_inc(conv_ready, 1)

            def store(q, g):
                k = q * GROUPS + g
                dve.wait_ge(lin_ready, k + 1)
                for i in range(2):
                    t0 = (2 * q + i) * TILES + g * GROUP
                    ins = nc.vector.tensor_tensor(
                        residual[:, t0:t0 + GROUP, :],
                        ps_l[k % 2][:, :].rearrange("p (t i c) -> p i t c", t=GROUP, i=2)[:, i],
                        lin_bias[:, i:i + 1, :].broadcast_to([P, GROUP, CH]), ALU.add)
                ins.then_inc(lin_used, 1)

            for q in range(PAIRS):
                for part in range(PARTS):
                    convolve(q, part)
                    if part:
                        for g in range((part - 1) * GROUPS // PARTS, part * GROUPS // PARTS):
                            store(q, g)
                for g in range((PARTS - 1) * GROUPS // PARTS, GROUPS):
                    store(q, g)


def statistics(nc, residual, mean, rstd):
    with ExitStack() as ctx:
        def sb(name, shape, dt=F32):
            return ctx.enter_context(nc.sbuf_tensor(name, shape, dt))

        def sem(name):
            return ctx.enter_context(nc.semaphore(name))

        total = sb("total", [P, ALL_TILES])
        centred = sb("centred", [P, 2, TILES, CH])
        squared = sb("squared", [P, 2, TILES, CH])
        squares = sb("squares", [P, ALL_TILES])
        power = sb("power", [P, ALL_TILES])
        s_sum, s_mean, s_cent, s_sq, s_ss, s_var, s_pow = (
            sem(n) for n in ("s_sum", "s_mean", "s_cent", "s_sq", "s_ss", "s_var", "s_pow"))
        block = ctx.enter_context(nc.Block())

        def tiles(b):
            return slice(b * TILES, (b + 1) * TILES)

        @block.vector
        def _(dve):
            def square_sums(b):
                dve.wait_ge(s_sq, b + 1)
                nc.vector.tensor_reduce(squares[:, tiles(b)], squared[:, b % 2], AX.X, ALU.add).then_inc(s_ss, 1)

            for b in range(BATCH):
                nc.vector.tensor_reduce(total[:, tiles(b)], residual[:, tiles(b), :], AX.X, ALU.add).then_inc(s_sum, 1)
                dve.wait_ge(s_sum, b + 1)
                nc.vector.tensor_scalar(mean[:, tiles(b)], total[:, tiles(b)], 1.0 / CH, None,
                                        ALU.mult).then_inc(s_mean, 1)
                if b:
                    square_sums(b - 1)
            square_sums(BATCH - 1)
            dve.wait_ge(s_ss, BATCH)
            nc.vector.tensor_scalar(total[:], squares[:], 1.0 / CH, EPS, ALU.mult, ALU.add).then_inc(s_var, 1)

        @block.gpsimd
        def _(pool):
            nc.gpsimd.memset(power[:], -0.5).then_inc(s_pow, 1)
            for b in range(BATCH):
                pool.wait_ge(s_mean, b + 1)
                if b >= 2:
                    pool.wait_ge(s_sq, b - 1)
                nc.gpsimd.tensor_tensor(centred[:, b % 2], residual[:, tiles(b), :],
                                        mean[:, tiles(b)].unsqueeze(2).broadcast_to([P, TILES, CH]),
                                        ALU.subtract).then_inc(s_cent, 1)
            pool.wait_ge(s_pow, 1)
            pool.wait_ge(s_var, 1)
            nc.gpsimd.tensor_tensor(rstd[:], total[:], power[:], ALU.pow).then_inc(s_pow, 1)

        @block.scalar
        def _(act):
            for b in range(BATCH):
                act.wait_ge(s_cent, b + 1)
                if b >= 2:
                    act.wait_ge(s_ss, b - 1)
                nc.scalar.activation(squared[:, b % 2], centred[:, b % 2], ACT.Square).then_inc(s_sq, 1)


def attend(nc, d, residual, mean, rstd, eye):
    with ExitStack() as ctx:
        def sb(name, shape, dt=F32):
            return ctx.enter_context(nc.sbuf_tensor(name, shape, dt))

        def sem(name):
            return ctx.enter_context(nc.semaphore(name))

        def psum(name, shape):
            return ctx.enter_context(nc.psum_tensor(name, shape, F32))

        keys1 = sb("keys1", [P, 2 * SEQ], F32R)
        keys2 = sb("keys2", [P, 2 * SEQ], F32R)
        values = sb("values", [P, 2, TILES, CH])
        waves_q = sb("waves_q", [P, SEQ], F32R)
        next_q = sb("next_q", [P, CHUNK], F32R)
        query1 = sb("query1", [P, 2 * CHUNK], F32R)
        query2 = sb("query2", [P, 2 * CHUNK], F32R)
        normed = sb("normed", [P, CHUNK_TILES, CH])
        centred = sb("centred_x", [P, CHUNK_TILES, CH])
        probs = sb("probs", [P, P_SLOTS, 2, CHUNK])
        summed = sb("summed", [P, CHUNK])
        maxima = sb("maxima", [P, CHUNK_TILES, len(PIECES)])
        maximum = sb("maximum", [P, CHUNK_TILES])
        recip = sb("recip", [P, CHUNK_TILES])
        update = sb("update", [P, CHUNK_TILES, CH])
        wq2 = sb("wq2", [CH, 2, CH])
        wkb = sb("wkb", [CH, CH + 1])
        bq = sb("bq", [CH, 1])
        wv = sb("wv", [CH, CH])
        wvd = sb("wvd", [CH, 2, CH])
        w_query = sb("w_query", [P, CH + 1])
        b_query = sb("b_query", [CH + 1, 1])
        w_value = sb("w_value", [P, CH + 1])
        beta_col = sb("beta_col", [P, 1])
        masks = sb("masks", [P, 4])

        scores = [psum(f"scores{i}", [P, 2, BANK]) for i in range(2)]
        acc = psum("acc", [P, BANK])
        misc = psum("misc", [P, BANK])
        tops = [psum(f"tops{i}", [P, BANK]) for i in range(2)]

        names = ("pe_passed", "pool_passed", "dve_passed", "par_in", "wave_in", "set_a", "set_b", "set_c", "set_w", "w_mm",
                 "x_centred", "x_ready", "v_ready", "ext_ready", "q_copied",
                 "t_ready", "t_high", "t_used", "g_ready", "g_high", "g_used",
                 "top_done", "top_used", "max_done", "row_mm", "row_used",
                 "s_done", "p_done", "pv_done", "acc_used", "o_ready", "o_used", "o_scaled", "o_mul", "o_rec")
        S = {n: sem(n) for n in names}
        block = ctx.enter_context(nc.Block())

        E0, E1 = CH, CH + EXTRA
        HALF = SEQ // 2

        def steps(eng, step):
            with eng.Fori(0, BATCH // 2 - 1) as i:
                for p in range(2):
                    n0 = i * (2 * CHUNKS) + p * CHUNKS
                    with eng.Fori(0, CHUNKS - 1) as c:
                        step(n0 + c, p, c, (p, c + 1), True)
                    step(n0 + (CHUNKS - 1), p, CHUNKS - 1, (1 - p, 0), True)
            for p in range(2):
                n0 = (BATCH - 2 + p) * CHUNKS
                with eng.Fori(0, CHUNKS - 1) as c:
                    step(n0 + c, p, c, (p, c + 1), p == 0)
                step(n0 + CHUNKS - 1, p, CHUNKS - 1, (1, 0) if p == 0 else None, p == 0)

        def unit_count(n, u):
            return n * UNITS + (u + 1 + UNITS)

        def before_unit(n, u, ring):
            if u >= ring:
                return unit_count(n, u - ring)
            last = max(v for v in range(UNITS) if v % ring == u % ring)
            return n * UNITS + (last + 1)

        def tiles_of(u):
            return [t for t in (2 * u, 2 * u + 1) if t < TILES]

        G_AT, T_AT, TOP_FROM, TOP_TO, ROW_AT = 0, 2, 1, 13, 14
        tops_at = {}
        for k in range(MAXES):
            tops_at.setdefault(TOP_FROM + k * (TOP_TO - TOP_FROM + 1) // MAXES, []).append(k)
        T_LOW_AFTER = 6

        @block.sync
        def _(sp):
            sp.dma_start(wq2[:, 0, :], d["L0_attn_Wq"]).then_inc(S["par_in"], 16)
            sp.dma_start(wq2[:, 1, :], d["L0_attn_Wq"]).then_inc(S["par_in"], 16)
            sp.dma_start(wkb[:, 0:CH], d["L0_attn_Wk"]).then_inc(S["par_in"], 16)
            sp.dma_start(wkb[:, CH:CH + 1], col(d["L0_attn_bk"])).then_inc(S["par_in"], 16)
            sp.dma_start(bq[:], col(d["L0_attn_bq"])).then_inc(S["par_in"], 16)
            sp.dma_start(wv[:], d["L0_attn_Wv"]).then_inc(S["par_in"], 16)
            sp.dma_start(wvd[:, 0, CH - 1:CH], col(d["L0_attn_bv"])).then_inc(S["par_in"], 16)
            sp.dma_start(wvd[:, 1, CH - 1:CH], col(d["L0_attn_bv"])).then_inc(S["par_in"], 16)
            sp.dma_start(w_value[:, CH:CH + 1], d["sum_col"]).then_inc(S["par_in"], 16)
            sp.dma_start(masks[E0:E1, :], d["masks"]).then_inc(S["par_in"], 16)
            sp.dma_start(beta_col[E0:E0 + 1, :], d["waves"][0:1, 0:1]).then_inc(S["par_in"], 16)
            for r in range(3):
                for w in range(len(PERIODS)):
                    at = E0 + 1 + r * BIAS_ROWS + 2 * w
                    sp.dma_start(beta_col[at:at + 2, :],
                                 d["L0_attn_beta"][w:w + 1].partition_broadcast(2)).then_inc(S["par_in"], 16)
            raw = values[:].rearrange("p a t c -> p (a t c)")
            sp.dma_start(raw[E0:E1, :], d["waves"]).then_inc(S["wave_in"], 16)

        PARAMS = 16 * (11 + 3 * len(PERIODS))

        @block.gpsimd
        def _(pool):
            def normalise(j, p, c):
                stat = (ds(j * CHUNK_TILES, CHUNK_TILES))
                pool.wait_ge(S["t_ready"], j + 1)
                nc.gpsimd.tensor_tensor(centred[:], residual[:, stat, :],
                                        mean[:, stat].unsqueeze(2).broadcast_to([P, CHUNK_TILES, CH]),
                                        ALU.subtract).then_inc(S["x_centred"], 1)
                pool.wait_ge(S["x_centred"], j + 1)
                nc.gpsimd.tensor_tensor(normed[:], centred[:],
                                        rstd[:, stat].unsqueeze(2).broadcast_to([P, CHUNK_TILES, CH]),
                                        ALU.mult).then_inc(S["x_ready"], 1)
                pool.wait_ge(S["x_ready"], j + 1)
                stand_alone(pool, S["pool_passed"])
                nc.gpsimd.tensor_copy(values[:, p, ds(c * CHUNK_TILES, CHUNK_TILES), 0:CH - 1],
                                      normed[:, :, 0:CH - 1]).then_inc(S["v_ready"], 1)

            def extra_rows(r, c, prepared):
                pool.wait_ge(S["v_ready"], prepared)
                pool.wait_ge(S["row_used"], r + 1)
                stand_alone(pool, S["pool_passed"])
                nc.gpsimd.tensor_copy(next_q[E0:E1, :], waves_q[E0:E1, ds(c * CHUNK, CHUNK)]).then_inc(S["ext_ready"], 1)
                nc.gpsimd.tensor_copy(query1[E0:E1, ds((r % 2) * CHUNK, CHUNK)],
                                      waves_q[E0:E1, ds(c * CHUNK, CHUNK)]).then_inc(S["ext_ready"], 1)

            def high_rows(r):
                pool.wait_ge(S["ext_ready"], 2 * r + 2)
                pool.wait_ge(S["g_high"], r + 1)
                stand_alone(pool, S["pool_passed"])
                for to in (query1, query2):
                    nc.gpsimd.tensor_copy(to[0:CH, ds((r % 2) * CHUNK, CHUNK)],
                                          next_q[0:CH, :]).then_inc(S["q_copied"], 1)

            pool.wait_ge(S["set_c"], 2)
            nc.gpsimd.memset(values[:, :, :, CH - 1:CH], 1.0)
            with pool.Fori(0, CHUNKS) as c:
                normalise(c, 0, c)
            extra_rows(0, 0, CHUNKS)
            high_rows(0)

            def step(n, p, c, nxt, prep):
                if nxt:
                    pool.wait_ge(S["pv_done"], n * UNITS + UNITS)
                    extra_rows(n + 1, nxt[1], n + CHUNKS if prep else STEPS)
                    high_rows(n + 1)
                if prep:
                    normalise(n + CHUNKS, 1 - p, c)

            steps(pool, step)

        @block.scalar
        def _(act):
            def keys_high(j, p, c):
                act.wait_ge(S["t_ready"], j + 2)
                at = ds(p * SEQ + c * CHUNK, CHUNK)
                nc.scalar.activation(keys1[0:CH, at], misc[0:CH, 0:CHUNK], ACT.Identity).then_inc(S["t_high"], 1)
                nc.scalar.activation(keys2[CH:P, at], misc[0:CH, 0:CHUNK], ACT.Identity).then_inc(S["t_high"], 1)

            def query_high(r):
                act.wait_ge(S["g_ready"], r + 1)
                act.wait_ge(S["ext_ready"], 2 * r + 2)
                nc.scalar.activation(next_q[0:CH + 1, :], misc[0:CH + 1, 0:CHUNK], ACT.Identity,
                                     bias=b_query[:, 0:1]).then_inc(S["g_high"], 1)

            def exponential(n, u):
                act.wait_ge(S["s_done"], n * UNITS + (u + 1))
                act.wait_ge(S["pv_done"], before_unit(n, u, P_SLOTS))
                k = len(tiles_of(u))
                nc.scalar.activation(probs[:, u % P_SLOTS, 0:k, :], scores[u % 2][:, 0:k, 0:CHUNK],
                                     ACT.Exp).then_inc(S["p_done"], 1)

            def take_sums(n):
                act.wait_ge(S["pv_done"], unit_count(n, UNITS - 1))
                nc.scalar.activation(summed[:], acc[:, 0:CHUNK], ACT.Identity).then_inc(S["acc_used"], 1)

            act.wait_ge(S["set_b"], 4)
            with act.Fori(0, CHUNKS) as c:
                keys_high(c, 0, c)
            query_high(0)

            def step(n, p, c, nxt, prep):
                for u in range(UNITS):
                    exponential(n, u)
                    if u == G_AT and nxt:
                        query_high(n + 1)
                    if u == T_AT and prep:
                        keys_high(n + CHUNKS, 1 - p, c)
                take_sums(n)

            steps(act, step)

        @block.tensor
        def _(pe):
            pe.sem_inc(S["t_ready"], 1)
            pe.sem_inc(S["pv_done"], UNITS)

            pe.wait_ge(S["par_in"], PARAMS)
            nc.tensor.matmul(misc[:, 0:CH + 1], wq2[:].rearrange("e a j -> e (a j)"), wkb[:],
                             start=True, stop=True).then_inc(S["w_mm"], 1)
            nc.tensor.matmul(tops[0][0:CH + 1, 0:1], wkb[:], bq[:], start=True, stop=True).then_inc(S["w_mm"], 1)
            pe.wait_ge(S["set_a"], 3)
            nc.tensor.matmul(tops[1][:, 0:CH], wvd[:].rearrange("e a j -> e (a j)"), eye[0:CH, 0:CH],
                             start=True, stop=True).then_inc(S["w_mm"], 1)

            def turn(j):
                pe.wait_ge(S["x_ready"], j + 1)
                stand_alone(pe, S["pe_passed"])
                for t in range(CHUNK_TILES):
                    mm = nc.tensor.transpose(misc[0:CH, t * P:(t + 1) * P], normed[:, t, :], eye[:])
                mm.then_inc(S["t_ready"], 1)

            def queries(r, p, c):
                nc.tensor.matmul(misc[0:CH + 1, 0:CHUNK], w_query[:],
                                 keys2[:, ds(p * SEQ + c * CHUNK, CHUNK)].bitcast(F32),
                                 start=True, stop=True).then_inc(S["g_ready"], 1)

            def top(r, k, p):
                t, (a, n) = k // len(PIECES), PIECES[k % len(PIECES)]
                if k >= 2:
                    pe.wait_ge(S["top_used"], r * MAXES + (k - 1))
                nc.tensor.matmul(tops[k % 2][:, 0:n], next_q[0:E1, t * P:(t + 1) * P],
                                 keys1[0:E1, p * SEQ + a:p * SEQ + a + n],
                                 start=True, stop=True).then_inc(S["top_done"], 1)

            def row(r):
                pe.wait_ge(S["max_done"], r + 1)
                for t in range(CHUNK_TILES):
                    mm = nc.tensor.matmul(tops[1][0:1, t * P:(t + 1) * P], maximum[:, t:t + 1], eye[:],
                                          start=True, stop=True)
                mm.then_inc(S["row_mm"], 1)

            def score(n, u, p):
                if u < 2:
                    pe.wait_ge(S["row_used"], n + 2)
                    pe.wait_ge(S["q_copied"], 2 * n + 2)
                    pe.wait_ge(S["g_used"], n + 1)
                pe.wait_ge(S["p_done"], before_unit(n, u, 2))
                at = ds((n % 2) * CHUNK, CHUNK)
                for i, t in enumerate(tiles_of(u)):
                    cols = slice(p * SEQ + t * P, p * SEQ + (t + 1) * P)
                    nc.tensor.matmul(scores[u % 2][:, i, 0:CHUNK], keys1[0:E1, cols], query1[0:E1, at],
                                     start=True, stop=False)
                    mm = nc.tensor.matmul(scores[u % 2][:, i, 0:CHUNK], keys2[:, cols], query2[:, at],
                                          start=False, stop=True)
                mm.then_inc(S["s_done"], 1)

            def weigh(n, u, p):
                pe.wait_ge(S["p_done"], unit_count(n, u))
                if u == 0:
                    pe.wait_ge(S["acc_used"], n + 1)
                for i, t in enumerate(tiles_of(u)):
                    mm = nc.tensor.matmul(acc[i * CH:(i + 1) * CH, 0:CHUNK], values[:, p, t, :],
                                          probs[:, u % P_SLOTS, i, :],
                                          start=(u == 0), stop=(t >= TILES - 2))
                mm.then_inc(S["pv_done"], 1)

            def project(n):
                pe.wait_ge(S["acc_used"], n + 2)
                pe.wait_ge(S["o_used"], n + 1)
                for t in range(CHUNK_TILES):
                    mm = nc.tensor.matmul(tops[0][:, t * (CH + 1):(t + 1) * (CH + 1)],
                                          summed[:, t * P:(t + 1) * P], w_value[:], start=True, stop=True)
                mm.then_inc(S["o_ready"], 1)

            pe.wait_ge(S["set_b"], 4)
            with pe.Fori(0, CHUNKS) as c:
                pe.wait_ge(S["t_used"], c + 1)
                turn(c)
            pe.wait_ge(S["t_used"], CHUNKS + 1)
            queries(0, 0, 0)
            pe.wait_ge(S["g_high"], 1)
            for k in range(MAXES):
                top(0, k, 0)
            pe.wait_ge(S["top_used"], MAXES)
            row(0)
            score(0, 0, 0)
            score(0, 1, 0)

            def step(n, p, c, nxt, prep):
                for u in range(UNITS):
                    if u + 2 < UNITS:
                        score(n, u + 2, p)
                    elif nxt:
                        score(n + 1, u + 2 - UNITS, nxt[0])
                    if nxt and u == G_AT:
                        pe.wait_ge(S["t_used"], (n + CHUNKS if prep else STEPS) + 1)
                        queries(n + 1, *nxt)
                    if prep and u == T_AT:
                        pe.wait_ge(S["g_used"], n + 2)
                        turn(n + CHUNKS)
                    if nxt:
                        for k in tops_at.get(u, ()):
                            if k == 0:
                                pe.wait_ge(S["g_high"], n + 2)
                                pe.wait_ge(S["o_used"], n + 1)
                            if k == 1:
                                pe.wait_ge(S["row_used"], n + 2)
                            if prep and k == len(PIECES) - 2:
                                pe.wait_ge(S["t_high"], (n + CHUNKS) * 2 + 2)
                            top(n + 1, k, nxt[0])
                        if u == ROW_AT:
                            row(n + 1)
                    weigh(n, u, p)
                project(n)

            steps(pe, step)

        @block.vector
        def _(dve):
            dve.sem_inc(S["t_used"], 1)
            dve.sem_inc(S["row_used"], 1)
            dve.sem_inc(S["o_used"], 1)
            dve.sem_inc(S["p_done"], UNITS)
            dve.sem_inc(S["acc_used"], 1)

            dve.wait_ge(S["par_in"], PARAMS)
            for a in range(2):
                nc.vector.tensor_scalar(wvd[:, a, 0:CH - 1], wv[:, 0:CH - 1], wv[:, CH - 1:CH], None,
                                        ALU.subtract).then_inc(S["set_a"], 1)
            nc.vector.memset(maximum[:], 0.0).then_inc(S["set_a"], 1)
            dve.wait_ge(S["w_mm"], 1)
            nc.vector.tensor_scalar(w_query[:], misc[:, 0:CH + 1], CH ** -0.5, None, ALU.mult).then_inc(S["set_b"], 1)
            dve.wait_ge(S["w_mm"], 2)
            nc.vector.tensor_scalar(b_query[:], tops[0][0:CH + 1, 0:1], CH ** -0.5, None, ALU.mult).then_inc(S["set_b"], 1)
            dve.wait_ge(S["w_mm"], 3)
            nc.vector.tensor_copy(w_value[:, 0:CH], tops[1][:, 0:CH]).then_inc(S["set_b"], 1)

            raw = values[:].rearrange("p a t c -> p (a t c)")
            tmp = probs[:].rearrange("p a b c -> p (a b c)")
            dve.wait_ge(S["wave_in"], 16)
            count = [0]

            def link(ins):
                count[0] += 1
                ins.then_inc(S["set_w"], 1)
                dve.wait_ge(S["set_w"], count[0])

            rows = slice(E0, E1)
            for side in range(2):
                for h in range(2):
                    at = slice(h * HALF, (h + 1) * HALF)
                    target = keys1 if side else waves_q
                    if side:
                        link(nc.vector.tensor_scalar(raw[rows, at], raw[rows, at], beta_col[rows, 0:1], None, ALU.mult))
                    link(nc.vector.tensor_copy(target[rows, at], raw[rows, at]))
                    low = tmp[rows, 0:HALF]
                    link(nc.vector.tensor_tensor(low, raw[rows, at], target[rows, at].bitcast(F32), ALU.subtract))
                    m = 0 if side else 2
                    link(nc.vector.tensor_scalar(low, low, masks[rows, m + 1:m + 2], None, ALU.mult))
                    link(nc.vector.scalar_tensor_tensor(out=target[rows, at], in0=target[rows, at].bitcast(F32),
                                                        scalar=masks[rows, m:m + 1], in1=low,
                                                        op0=ALU.mult, op1=ALU.add))
                    if side:
                        link(nc.vector.tensor_copy(keys1[rows, SEQ + h * HALF:SEQ + (h + 1) * HALF],
                                                   keys1[rows, at].bitcast(F32)))
            nc.vector.memset(recip[:], 0.0).then_inc(S["set_c"], 1)
            nc.vector.memset(maxima[:], 0.0).then_inc(S["set_c"], 1)
            nc.vector.memset(update[:], 0.0).then_inc(S["set_b"], 1)

            def keys_low(j, p, c):
                at = ds(p * SEQ + c * CHUNK, CHUNK)
                dve.wait_ge(S["t_high"], j * 2 + 2)
                nc.vector.tensor_tensor(keys2[0:CH, at], misc[0:CH, 0:CHUNK], keys1[0:CH, at].bitcast(F32),
                                        ALU.subtract).then_inc(S["t_used"], 1)

            def query_low(r):
                dve.wait_ge(S["g_high"], r + 1)
                nc.vector.scalar_tensor_tensor(
                    out=query2[CH:P, ds((r % 2) * CHUNK, CHUNK)], in0=misc[0:CH, 0:CHUNK],
                    scalar=b_query[0:CH, 0:1], in1=next_q[0:CH, :].bitcast(F32),
                    op0=ALU.add, op1=ALU.subtract).then_inc(S["g_used"], 1)

            def reduce(r, k):
                t, j = divmod(k, len(PIECES))
                dve.wait_ge(S["top_done"], r * MAXES + (k + 1))
                nc.vector.tensor_reduce(maxima[:, t, j:j + 1], tops[k % 2][:, 0:PIECES[j][1]], AX.X,
                                        ALU.max).then_inc(S["top_used"], 1)

            def shift_row(r):
                dve.wait_ge(S["top_used"], r * MAXES + MAXES)
                nc.vector.tensor_reduce(maximum[:], maxima[:], AX.X, ALU.max).then_inc(S["max_done"], 1)
                dve.wait_ge(S["row_mm"], r + 1)
                dve.wait_ge(S["ext_ready"], 2 * r + 2)
                nc.vector.tensor_tensor(query1[E0:E0 + 1, ds((r % 2) * CHUNK, CHUNK)],
                                        next_q[E0:E0 + 1, :].bitcast(F32), tops[1][0:1, 0:CHUNK],
                                        ALU.subtract).then_inc(S["row_used"], 1)

            def add_update(n):
                out = tops[0][:, 0:CHUNK_TILES * (CH + 1)].rearrange("p (t c) -> p t c", c=CH + 1)
                at = ds(n * CHUNK_TILES, CHUNK_TILES)
                dve.wait_ge(S["o_ready"], n + 1)
                nc.vector.reciprocal(recip[:], out[:, :, CH]).then_inc(S["o_rec"], 1)
                dve.wait_ge(S["o_rec"], n + 1)
                nc.vector.tensor_tensor(update[:], out[:, :, 0:CH],
                                        recip[:].unsqueeze(2).broadcast_to([P, CHUNK_TILES, CH]),
                                        ALU.mult).then_inc(S["o_used"], 1)
                dve.wait_ge(S["o_used"], n + 2)
                nc.vector.tensor_tensor(residual[:, at, :], residual[:, at, :], update[:], ALU.add).then_inc(S["o_mul"], 1)

            with dve.Fori(0, CHUNKS) as c:
                keys_low(c, 0, c)
            query_low(0)
            for k in range(MAXES):
                reduce(0, k)
            shift_row(0)

            def step(n, p, c, nxt, prep):
                if nxt:
                    query_low(n + 1)
                for k in range(MAXES):
                    if nxt:
                        reduce(n + 1, k)
                    if k == T_LOW_AFTER and prep:
                        keys_low(n + CHUNKS, 1 - p, c)
                if nxt:
                    shift_row(n + 1)
                add_update(n)

            steps(dve, step)


def experts(nc, d, residual, eye, out):
    GROUP = 4
    GROUPS = ALL_TILES // GROUP
    COLS = GROUP * P
    with ExitStack() as ctx:
        def sb(name, shape, dt=F32):
            return ctx.enter_context(nc.sbuf_tensor(name, shape, dt))

        def sem(name):
            return ctx.enter_context(nc.semaphore(name))

        w1_raw = sb("w1_raw", [P, EXPERTS, HIDDEN])
        w1_high = sb("w1_high", [P, EXPERTS, HIDDEN], F32R)
        w1_low = sb("w1_low", [P, EXPERTS, HIDDEN], F32R)
        b1 = sb("b1", [HIDDEN, EXPERTS])
        w2 = sb("w2", [HIDDEN, EXPERTS, CH])
        b2 = sb("b2", [48, CH])
        gate_raw = sb("gate_raw", [P, EXPERTS])
        gate_high = sb("gate_high", [P, EXPERTS], F32R)
        gate_low = sb("gate_low", [P, EXPERTS], F32R)
        gate_bias = sb("gate_bias", [P, 1, EXPERTS])
        pick_raw = sb("pick_raw", [48, EXPERTS * P])
        pick = sb("pick", [48, EXPERTS * P], F32R)
        iota = sb("iota", [P, 1, EXPERTS])
        gamma = sb("gamma", [P, 1, CH])
        beta = sb("beta", [P, 1, CH])
        half = sb("half", [P, GROUP])

        z = sb("z", [P, 2, GROUP, CH])
        halves = sb("halves", [P, 2, COLS], F32R)
        gates_t = sb("gates_t", [48, 2, COLS], F32R)
        hidden = sb("hidden", [P, 2, COLS])
        gated = sb("gated", [P, 2, COLS])
        moe = sb("moe", [P, COLS])
        n1 = {k: sb("n1_" + k, s) for k, s in (("sum", [P, GROUP]), ("mean", [P, GROUP]), ("cent", [P, GROUP, CH]),
                                             ("sq", [P, GROUP, CH]), ("ss", [P, GROUP]), ("var", [P, GROUP]), ("rstd", [P, GROUP]))}
        n2 = {k: sb("n2_" + k, s) for k, s in (("sum", [P, GROUP]), ("mean", [P, GROUP]), ("cent", [P, GROUP, CH]),
                                             ("sq", [P, GROUP, CH]), ("ss", [P, GROUP]), ("var", [P, GROUP]), ("rstd", [P, GROUP]))}
        y0 = sb("y0", [P, GROUP, CH])
        y = sb("y", [P, GROUP, CH])
        o1, o2, o3 = (sb(f"o{i}", [P, GROUP, CH]) for i in (1, 2, 3))
        result = sb("result", [P, 2, GROUP, CH])
        logits = sb("logits", [P, GROUP, EXPERTS])
        best = sb("best", [P, GROUP, 8])
        where = sb("where", [P, GROUP, 8], U32)
        where_f = sb("where_f", [P, GROUP, 2])
        gap = sb("gap", [P, GROUP])
        ratio = sb("ratio", [P, GROUP])
        one_up = sb("one_up", [P, GROUP])
        weight = sb("weight", [P, 2, GROUP])
        is0 = sb("is0", [P, GROUP, EXPERTS])
        is1 = sb("is1", [P, GROUP, EXPERTS])
        by0 = sb("by0", [P, GROUP, EXPERTS])
        by1 = sb("by1", [P, GROUP, EXPERTS])
        gates = sb("gates", [P, GROUP, EXPERTS])

        def psum(name):
            return ctx.enter_context(nc.psum_tensor(name, [P, BANK], F32))

        ps_hid = [psum(f"ps_hid{i}") for i in range(2)]
        ps_gate = [psum(f"ps_gate{i}") for i in range(2)]
        ps_moe, ps_z, ps_log, ps_out = psum("ps_moe"), psum("ps_z"), psum("ps_log"), psum("ps_out")

        names = ("pe_passed", "pool_passed", "dve_passed", "w_in", "w_cast", "b2_zero", "power_set",
                 "p_dve", "p_cent", "p_sq", "p_rstd", "z_ready", "z_turned", "z_high", "z_low", "log_ready",
                 "ratio_ready", "gates_turned", "g_high", "g_low",
                 "hid_ready", "relu_ready", "gate_ready", "gated_ready", "moe_done", "moe_used",
                 "q_dve", "q_cent", "q_sq", "q_rstd", "out_turned", "y0_ready", "y_ready", "o_chain", "result_ready", "stored0", "stored1")
        S = {n: sem(n) for n in names}
        block = ctx.enter_context(nc.Block())

        P_NORM = 4
        P_CHOICE = 1 + 2 * GROUP + 2
        P_OPS = P_NORM + P_CHOICE + 3 + 5
        Q_OPS = 4

        def steps(eng, step):
            step(0, 0, True, False)
            with eng.Fori(0, (GROUPS - 2) // 2) as i:
                for k in range(2):
                    step(i * 2 + (1 + k), 1 - k, True, True)
            step(GROUPS - 1, 1, False, True)

        W_LOADS = 16 * 16

        @block.sync
        def _(sp):
            for k in range(2):
                rows = slice(k * CH, (k + 1) * CH)
                sp.dma_start(w1_raw[rows], d["L0_ffn_w1"].rearrange("e c f -> c e f")).then_inc(S["w_in"], 16)
                sp.dma_start(gate_raw[rows], d["L0_ffn_gate_w"]).then_inc(S["w_in"], 16)
            sp.dma_start(w2[:], d["L0_ffn_w2"].rearrange("e f c -> f e c")).then_inc(S["w_in"], 16)
            sp.dma_start(pick_raw[:], d["pick"]).then_inc(S["w_in"], 16)
            sp.dma_start(iota[:, 0, :], d["iota"]).then_inc(S["w_in"], 16)
            sp.dma_start(gate_bias[:, 0, :], d["L0_ffn_gate_b"].partition_broadcast(P)).then_inc(S["w_in"], 16)
            sp.dma_start(gamma[:, 0, :], d["L0_ffn_gamma"].partition_broadcast(P)).then_inc(S["w_in"], 16)
            sp.dma_start(beta[:, 0, :], d["L0_ffn_beta"].partition_broadcast(P)).then_inc(S["w_in"], 16)
            with nc.allow_non_contiguous_dma("a small transposed load"):
                for k in range(4):
                    sp.dma_start(b1[:, 4 * k:4 * k + 4],
                                 d["L0_ffn_b1"][4 * k:4 * k + 4].rearrange("e f -> f e")).then_inc(S["w_in"], 16)
            sp.wait_ge(S["b2_zero"], 1)
            for k in range(2):
                sp.dma_start(b2[32 * k:32 * k + EXPERTS, :], d["L0_ffn_b2"]).then_inc(S["w_in"], 16)

            flat = out.rearrange("b (t p) c -> (b t) p c", p=P)

            def store(g, p):
                sp.wait_ge(S["result_ready"], g + 1)
                sp.dma_start(flat[ds(g * GROUP, GROUP)].rearrange("t p c -> p t c"),
                             result[:, p]).then_inc(S[f"stored{p}"], 16)

            def step(g, p, prep, post):
                if post:
                    store(g - 1, 1 - p)

            steps(sp, step)
            store(GROUPS - 1, 1)
            sp.wait_ge(S["stored0"], 16 * (GROUPS // 2))
            sp.wait_ge(S["stored1"], 16 * (GROUPS // 2) + 16)

        def norm_on_pool(pool, n, x, r, pre):
            dve, ops = (S["p_dve"], P_OPS) if pre else (S["q_dve"], Q_OPS)
            cent, sq = (S["p_cent"], S["p_sq"]) if pre else (S["q_cent"], S["q_sq"])
            pool.wait_ge(dve, r * ops + 2)
            nc.gpsimd.tensor_tensor(n["cent"][:], x, n["mean"][:].unsqueeze(2).broadcast_to([P, GROUP, CH]),
                                    ALU.subtract).then_inc(cent, 1)
            pool.wait_ge(cent, r + 1)
            nc.gpsimd.tensor_tensor(n["sq"][:], n["cent"][:], n["cent"][:], ALU.mult).then_inc(sq, 1)

        def root_on_pool(pool, n, r, pre):
            dve, ops = (S["p_dve"], P_OPS) if pre else (S["q_dve"], Q_OPS)
            rstd = S["p_rstd"] if pre else S["q_rstd"]
            pool.wait_ge(dve, r * ops + 4)
            nc.gpsimd.tensor_tensor(n["rstd"][:], n["var"][:], half[:], ALU.pow).then_inc(rstd, 1)
            pool.wait_ge(rstd, r + 1)

        @block.gpsimd
        def _(pool):
            nc.gpsimd.memset(b2[:], 0.0).then_inc(S["b2_zero"], 1)
            nc.gpsimd.memset(half[:], -0.5).then_inc(S["power_set"], 1)
            pool.wait_ge(S["power_set"], 1)

            def rows_of(g):
                return residual[:, ds(g * GROUP, GROUP), :]

            def prep_a(r):
                norm_on_pool(pool, n1, rows_of(r), r, True)

            def prep_b(r, p):
                root_on_pool(pool, n1, r, True)
                pool.wait_ge(S["y_ready"], r)
                nc.gpsimd.tensor_tensor(z[:, p], n1["cent"][:], n1["rstd"][:].unsqueeze(2).broadcast_to([P, GROUP, CH]),
                                        ALU.mult).then_inc(S["z_ready"], 1)

            def post_a(r):
                norm_on_pool(pool, n2, y[:], r, False)

            def post_b(r, p):
                root_on_pool(pool, n2, r, False)
                chain = [(o1, n2["cent"][:], n2["rstd"][:].unsqueeze(2), ALU.mult),
                         (o2, o1[:], gamma[:], ALU.mult),
                         (o3, o2[:], beta[:], ALU.add)]
                for k, (to, a, b, op) in enumerate(chain):
                    nc.gpsimd.tensor_tensor(to[:], a, b.broadcast_to([P, GROUP, CH]), op).then_inc(S["o_chain"], 1)
                    pool.wait_ge(S["o_chain"], r * 3 + (k + 1))
                pool.wait_ge(S[f"stored{p}"], (r // 2) * 16 + 16)
                nc.gpsimd.tensor_tensor(result[:, p], o3[:], rows_of(r), ALU.add).then_inc(S["result_ready"], 1)

            prep_a(0)
            prep_b(0, 0)

            def step(g, p, prep, post):
                if prep:
                    prep_a(g + 1)
                if post:
                    post_a(g - 1)
                if prep:
                    prep_b(g + 1, 1 - p)
                if post:
                    post_b(g - 1, 1 - p)

            steps(pool, step)
            post_a(GROUPS - 1)
            post_b(GROUPS - 1, 1)

        @block.scalar
        def _(act):
            act.sem_inc(S["stored0"], 16)
            act.sem_inc(S["stored1"], 16)
            act.sem_inc(S["relu_ready"], EXPERTS)
            act.sem_inc(S["moe_used"], 1)

            def high_z(r, p):
                act.wait_ge(S["z_turned"], r + 1)
                nc.scalar.activation(halves[0:CH, p, :], ps_z[0:CH, :], ACT.Identity).then_inc(S["z_high"], 1)

            def exp_gap(r):
                act.wait_ge(S["p_dve"], r * P_OPS + P_NORM + P_CHOICE - 1)
                nc.scalar.activation(ratio[:], gap[:], ACT.Exp).then_inc(S["ratio_ready"], 1)

            def high_gates(r, p):
                act.wait_ge(S["gates_turned"], r + 1)
                nc.scalar.activation(gates_t[0:EXPERTS, p, :], ps_log[0:EXPERTS, :], ACT.Identity).then_inc(S["g_high"], 1)

            def relu(g, e):
                act.wait_ge(S["hid_ready"], g * EXPERTS + (e + 1))
                act.wait_ge(S["gated_ready"], g * EXPERTS + (e - 1 + EXPERTS))
                nc.scalar.activation(hidden[:, e % 2, :], ps_hid[e % 2][:, :], ACT.Relu,
                                     bias=b1[:, e:e + 1]).then_inc(S["relu_ready"], 1)

            act.wait_ge(S["w_cast"], 7)
            high_z(0, 0)
            exp_gap(0)
            high_gates(0, 0)

            def step(g, p, prep, post):
                for e in range(EXPERTS):
                    relu(g, e)
                    if prep and e == 5:
                        high_z(g + 1, 1 - p)
                    if prep and e == 9:
                        exp_gap(g + 1)
                    if prep and e == 12:
                        high_gates(g + 1, 1 - p)
                act.wait_ge(S["moe_done"], (g + 1) * EXPERTS)
                nc.scalar.activation(moe[:], ps_moe[:], ACT.Identity).then_inc(S["moe_used"], 1)

            steps(act, step)

        @block.tensor
        def _(pe):
            pe.wait_ge(S["w_in"], W_LOADS)
            pe.wait_ge(S["w_cast"], 7)

            def turn_z(r, p):
                pe.wait_ge(S["z_ready"], r + 1)
                stand_alone(pe, S["pe_passed"])
                for t in range(GROUP):
                    mm = nc.tensor.transpose(ps_z[0:CH, t * P:(t + 1) * P], z[:, p, t, :], eye[:])
                mm.then_inc(S["z_turned"], 1)

            def gate_logits(r, p):
                pe.wait_ge(S["z_low"], r + 1)
                for t in range(GROUP):
                    to = ps_log[:, t * EXPERTS:(t + 1) * EXPERTS]
                    zt = halves[:, p, t * P:(t + 1) * P]
                    nc.tensor.matmul(to, zt, gate_high[:], start=True, stop=False)
                    mm = nc.tensor.matmul(to, zt, gate_low[:], start=False, stop=True)
                mm.then_inc(S["log_ready"], 1)

            def turn_gates(r):
                pe.wait_ge(S["p_dve"], (r + 1) * P_OPS)
                for t in range(GROUP):
                    mm = nc.tensor.transpose(ps_log[0:EXPERTS, t * P:(t + 1) * P], gates[:, t, :], eye[:])
                mm.then_inc(S["gates_turned"], 1)

            def hid(g, e, p):
                if e == 0:
                    pe.wait_ge(S["z_low"], g + 1)
                pe.wait_ge(S["relu_ready"], g * EXPERTS + (e - 1 + EXPERTS))
                nc.tensor.matmul(ps_hid[e % 2][:, :], w1_high[:, e, :], halves[:, p, :], start=True, stop=False)
                nc.tensor.matmul(ps_hid[e % 2][:, :], w1_low[:, e, :], halves[:, p, :],
                                 start=False, stop=True).then_inc(S["hid_ready"], 1)

            def gate(g, e, p):
                if e == 0:
                    pe.wait_ge(S["g_low"], g + 1)
                pe.wait_ge(S["gated_ready"], g * EXPERTS + (e - 1 + EXPERTS))
                nc.tensor.matmul(ps_gate[e % 2][:, :], pick[:, e * P:(e + 1) * P], gates_t[:, p, :],
                                 start=True, stop=True).then_inc(S["gate_ready"], 1)

            def second(g, e, p):
                if e == 0:
                    pe.wait_ge(S["moe_used"], g + 1)
                    stand_alone(pe, S["pe_passed"])
                    nc.tensor.matmul(ps_moe[0:CH, :], b2[:], gates_t[:, p, :].bitcast(F32), start=True, stop=False)
                pe.wait_ge(S["gated_ready"], g * EXPERTS + (e + 1 + EXPERTS))
                h = e % 2
                nc.tensor.matmul(ps_moe[h * CH:(h + 1) * CH, :], w2[:, e, :], gated[:, e % 2, :],
                                 start=(e == 1), stop=(e >= EXPERTS - 2)).then_inc(S["moe_done"], 1)

            def turn_out(g):
                pe.wait_ge(S["moe_used"], g + 2)
                for t in range(GROUP):
                    mm = nc.tensor.transpose(ps_out[:, t * P:(t + 1) * P], moe[:, t * P:(t + 1) * P], eye[:])
                mm.then_inc(S["out_turned"], 1)

            turn_z(0, 0)
            gate_logits(0, 0)
            turn_gates(0)
            for e in range(2):
                hid(0, e, 0)
                gate(0, e, 0)

            def step(g, p, prep, post):
                for e in range(EXPERTS):
                    if e + 2 < EXPERTS:
                        hid(g, e + 2, p)
                        gate(g, e + 2, p)
                    elif prep:
                        hid(g + 1, e + 2 - EXPERTS, 1 - p)
                        gate(g + 1, e + 2 - EXPERTS, 1 - p)
                    if post and e == 0:
                        turn_out(g - 1)
                    if prep and e == 5:
                        turn_z(g + 1, 1 - p)
                    if prep and e == 7:
                        gate_logits(g + 1, 1 - p)
                    if prep and e == 11:
                        turn_gates(g + 1)
                    second(g, e, p)

            steps(pe, step)
            turn_out(GROUPS - 1)

        @block.vector
        def _(dve):
            dve.sem_inc(S["gated_ready"], EXPERTS)
            dve.sem_inc(S["y_ready"], 1)
            dve.wait_ge(S["w_in"], W_LOADS)
            nc.vector.tensor_copy(w1_high[:], w1_raw[:]).then_inc(S["w_cast"], 1)
            nc.vector.tensor_copy(gate_high[:], gate_raw[:]).then_inc(S["w_cast"], 1)
            nc.vector.tensor_copy(pick[:], pick_raw[:]).then_inc(S["w_cast"], 1)
            dve.wait_ge(S["w_cast"], 2)
            nc.vector.tensor_tensor(w1_low[:], w1_raw[:], w1_high[:].bitcast(F32), ALU.subtract).then_inc(S["w_cast"], 1)
            nc.vector.tensor_tensor(gate_low[:], gate_raw[:], gate_high[:].bitcast(F32), ALU.subtract).then_inc(S["w_cast"], 1)
            for p in range(2):
                nc.vector.memset(gates_t[:, p, :].bitcast(F32), 0.0).then_inc(S["w_cast"], 1)

            def linked(name, base):
                k = [0]

                def link(ins, wait=True):
                    k[0] += 1
                    ins.then_inc(S[name], 1)
                    if wait:
                        dve.wait_ge(S[name], base + k[0])
                return link

            def mean_of(link, n, x):
                link(nc.vector.tensor_reduce(n["sum"][:], x, AX.X, ALU.add))
                link(nc.vector.tensor_scalar(n["mean"][:], n["sum"][:], 1.0 / CH, None, ALU.mult), False)

            def prep_mean(r):
                link = linked("p_dve", r * P_OPS)
                if not (isinstance(r, int) and r == 0):
                    dve.wait_ge(S["z_ready"], r)
                mean_of(link, n1, residual[:, ds(r * GROUP, GROUP), :])

            def prep_var(r):
                dve.wait_ge(S["p_sq"], r + 1)
                link = linked("p_dve", r * P_OPS + 2)
                link(nc.vector.tensor_reduce(n1["ss"][:], n1["sq"][:], AX.X, ALU.add))
                link(nc.vector.tensor_scalar(n1["var"][:], n1["ss"][:], 1.0 / CH, EPS, ALU.mult, ALU.add), False)

            def low_z(r, p):
                dve.wait_ge(S["z_high"], r + 1)
                nc.vector.tensor_tensor(halves[CH:P, p, :], ps_z[0:CH, :], halves[0:CH, p, :].bitcast(F32),
                                        ALU.subtract).then_inc(S["z_low"], 1)

            def choose(r):
                dve.wait_ge(S["log_ready"], r + 1)
                link = linked("p_dve", r * P_OPS + P_NORM)
                link(nc.vector.tensor_tensor(logits[:], ps_log[:, 0:GROUP * EXPERTS].rearrange("p (t e) -> p t e", e=EXPERTS),
                                             gate_bias[:].broadcast_to([P, GROUP, EXPERTS]), ALU.add))
                stand_alone(dve, S["dve_passed"])
                for t in range(GROUP):
                    link(nc.vector.max(best[:, t, :], logits[:, t, :]), t == GROUP - 1)
                stand_alone(dve, S["dve_passed"])
                for t in range(GROUP):
                    link(nc.vector.max_index(where[:, t, :], best[:, t, :], logits[:, t, :]), False)
                link(nc.vector.tensor_tensor(gap[:], best[:, :, 1], best[:, :, 0], ALU.subtract))
                link(nc.vector.tensor_copy(where_f[:], where[:, :, 0:2]), False)

            def fill_gates(r):
                dve.wait_ge(S["ratio_ready"], r + 1)
                link = linked("p_dve", r * P_OPS + P_NORM + P_CHOICE)
                link(nc.vector.tensor_scalar(one_up[:], ratio[:], 1.0, None, ALU.add))
                link(nc.vector.reciprocal(weight[:, 0, :], one_up[:]))
                link(nc.vector.tensor_tensor(weight[:, 1, :], weight[:, 0, :], ratio[:], ALU.mult))
                full = [P, GROUP, EXPERTS]
                for k, to in enumerate((is0, is1)):
                    link(nc.vector.tensor_tensor(to[:], iota[:].broadcast_to(full),
                                                 where_f[:, :, k:k + 1].broadcast_to(full), ALU.is_equal), k == 1)
                for k, (to, src) in enumerate(((by0, is0), (by1, is1))):
                    link(nc.vector.tensor_tensor(to[:], src[:], weight[:, k, :].unsqueeze(2).broadcast_to(full),
                                                 ALU.mult), k == 1)
                link(nc.vector.tensor_tensor(gates[:], by0[:], by1[:], ALU.add), False)

            def low_gates(r, p):
                dve.wait_ge(S["g_high"], r + 1)
                nc.vector.tensor_tensor(gates_t[32:32 + EXPERTS, p, :], ps_log[0:EXPERTS, :],
                                        gates_t[0:EXPERTS, p, :].bitcast(F32), ALU.subtract).then_inc(S["g_low"], 1)

            def weigh(g, e):
                dve.wait_ge(S["relu_ready"], g * EXPERTS + (e + 1 + EXPERTS))
                dve.wait_ge(S["gate_ready"], g * EXPERTS + (e + 1))
                if not (isinstance(g, int) and g == 0 and e < 2):
                    dve.wait_ge(S["moe_done"], g * EXPERTS + (e - 1))
                nc.vector.tensor_tensor(gated[:, e % 2, :], hidden[:, e % 2, :], ps_gate[e % 2][:, :],
                                        ALU.mult).then_inc(S["gated_ready"], 1)

            def add_z(r, p):
                dve.wait_ge(S["out_turned"], r + 1)
                two = ps_out[:].rearrange("p (t h c) -> p t h c", t=GROUP, h=2)
                nc.vector.tensor_tensor(y0[:], two[:, :, 0], z[:, p], ALU.add).then_inc(S["y0_ready"], 1)
                dve.wait_ge(S["y0_ready"], r + 1)
                nc.vector.tensor_tensor(y[:], two[:, :, 1], y0[:], ALU.add).then_inc(S["y_ready"], 1)

            def post_mean(r):
                dve.wait_ge(S["y_ready"], r + 2)
                link = linked("q_dve", r * Q_OPS)
                mean_of(link, n2, y[:])

            def post_var(r):
                dve.wait_ge(S["q_sq"], r + 1)
                link = linked("q_dve", r * Q_OPS + 2)
                link(nc.vector.tensor_reduce(n2["ss"][:], n2["sq"][:], AX.X, ALU.add))
                link(nc.vector.tensor_scalar(n2["var"][:], n2["ss"][:], 1.0 / CH, EPS, ALU.mult, ALU.add), False)

            prep_mean(0)
            prep_var(0)
            low_z(0, 0)
            choose(0)
            fill_gates(0)
            low_gates(0, 0)

            def step(g, p, prep, post):
                for e in range(EXPERTS):
                    weigh(g, e)
                    if prep and e == 0:
                        prep_mean(g + 1)
                    if post and e == 1:
                        add_z(g - 1, 1 - p)
                        post_mean(g - 1)
                    if prep and e == 3:
                        prep_var(g + 1)
                    if post and e == 4:
                        post_var(g - 1)
                    if prep and e == 6:
                        low_z(g + 1, 1 - p)
                    if prep and e == 8:
                        choose(g + 1)
                    if prep and e == 10:
                        fill_gates(g + 1)
                    if prep and e == 13:
                        low_gates(g + 1, 1 - p)

            steps(dve, step)
            add_z(GROUPS - 1, 1)
            post_mean(GROUPS - 1)
            post_var(GROUPS - 1)


def early_fusion(nc, d, out, dump=None, stages=4):
    with ExitStack() as ctx:
        def sb(name, shape, dt=F32):
            return ctx.enter_context(nc.sbuf_tensor(name, shape, dt))

        residual = sb("residual", [P, ALL_TILES, CH])
        mean = sb("mean", [P, ALL_TILES])
        rstd = sb("rstd", [P, ALL_TILES])
        eye = sb("eye", [P, P])
        tokenise(nc, d, residual, eye)
        statistics(nc, residual, mean, rstd)
        if stages >= 2:
            attend(nc, d, residual, mean, rstd, eye)
        if stages >= 3:
            experts(nc, d, residual, eye, out)
        if dump is not None:
            with nc.semaphore("dumped") as dumped, nc.Block() as block:
                @block.sync
                def _(sp):
                    sp.dma_start(dump["h"], residual[:].rearrange("p t c -> p (t c)")).then_inc(dumped, 16)
                    sp.dma_start(dump["m"], mean[:]).then_inc(dumped, 16)
                    sp.dma_start(dump["r"], rstd[:]).then_inc(dumped, 16)
                    sp.wait_ge(dumped, 48)


def kernel(**inputs):
    import concourse.bacc as _bacc
    from concourse.bass_utils import run_bass_kernel_spmd as _run

    nc = _bacc.Bacc("TRN2", target_bir_lowering=False, num_devices=1)
    arrays, d = {}, {}
    for name, a in {**inputs, **constants()}.items():
        a = np.ascontiguousarray(a)
        arrays[f"in_{name}"] = a
        d[name] = nc.dram_tensor(f"in_{name}", a.shape, mybir.dt.from_np(a.dtype), kind="ExternalInput").ap()
    out = nc.dram_tensor("out_0", (BATCH, SEQ, CH), F32, kind="ExternalOutput").ap()
    early_fusion(nc, d, out)
    r = _run(nc, [arrays], core_ids=[0])
    return r.results[0]["out_0"]
```

```python
from contextlib import ExitStack

import concourse.bass as bass
import numpy as np
from concourse import mybir

F32 = mybir.dt.float32
F32R = mybir.dt.float32r
U32 = mybir.dt.uint32
ALU = mybir.AluOpType
ACT = mybir.ActivationFunctionType
AX = mybir.AxisListType

P = 128
BATCH, SIDE, CH = 8, 64, 64
IMAGE = SIDE * SIDE
TEXT = 128
SEQ = IMAGE + TEXT
TILES = SEQ // P
IMAGE_TILES = IMAGE // P
ALL_TILES = BATCH * TILES
EXPERTS, HIDDEN = 16, 128
EPS = 1e-5
PERIODS = (24.0, 720.0)
PAD = SIDE + 2
BANK = 512
ds = bass.ds

CHUNK_TILES = 3
CHUNK = CHUNK_TILES * P
CHUNKS = TILES // CHUNK_TILES
STEPS = BATCH * CHUNKS
UNITS = (TILES + 1) // 2
BIAS_ROWS = 2 * len(PERIODS)
EXTRA = 1 + 3 * BIAS_ROWS
ROWS1 = CH + EXTRA
P_SLOTS = 5
WHOLE, REST = divmod(SEQ, BANK)
MAXES = CHUNK_TILES * WHOLE + 1


def constants():
    s = np.arange(SEQ, dtype=np.float64)
    waves = []
    for period in PERIODS:
        waves += [np.cos(2 * np.pi * s / period), np.sin(2 * np.pi * s / period)]
    waves = np.stack(waves)
    rows = np.concatenate([np.ones((1, SEQ)), waves, waves, waves]).astype(np.float32)
    masks = np.zeros((EXTRA, 4), np.float32)
    n = BIAS_ROWS
    masks[:1 + 2 * n, 0] = 1
    masks[1 + 2 * n:, 1] = 1
    masks[1:1 + n, 2] = masks[1 + 2 * n:, 2] = 1
    masks[1 + n:1 + 2 * n, 3] = 1
    ones_col = np.zeros((P, 1), np.float32)
    ones_col[CH - 1] = ones_col[2 * CH - 1] = 1
    eye = np.eye(P, dtype=np.float32)
    pick = np.zeros((48, EXPERTS, P), np.float32)
    for e in range(EXPERTS):
        pick[e, e] = pick[32 + e, e] = 1
    iota = np.broadcast_to(np.arange(EXPERTS, dtype=np.float32), (P, EXPERTS)).copy()
    return {"waves": rows, "masks": masks, "sum_col": ones_col, "eye": eye,
            "pick": pick.reshape(48, EXPERTS * P), "iota": iota}


def col(ap, n=None):
    return ap.rearrange("(p a) -> p a", a=1)


def stand_alone(eng, passed):
    eng.sem_inc(passed, 1)


def tokenise(nc, d, residual, eye):
    PAIRS = BATCH // 2
    GROUP = 4
    GROUPS = IMAGE_TILES // GROUP
    ROWS = GROUP * P // SIDE
    PARTS = 4
    PART = IMAGE // PARTS
    with ExitStack() as ctx:
        def sb(name, shape, dt=F32):
            return ctx.enter_context(nc.sbuf_tensor(name, shape, dt))

        def sem(name):
            return ctx.enter_context(nc.semaphore(name))

        tokens = sb("tokens", [P, 2, IMAGE_TILES, 2, CH])
        padded = sb("padded", [P, 2, PAD, PAD])
        conv = sb("conv", [P, 2, IMAGE])
        lin_rows = sb("lin_rows", [CH, CH])
        lin_both = sb("lin_both", [P, P])
        lin_bias = sb("lin_bias", [P, 2, CH])
        taps = sb("taps", [P, 9])
        vec = sb("vec", [P, 5])
        bn = sb("bn", [P, 4])
        shift = sb("shift", [P, 1])
        scale = sb("scale", [P, 1])
        ps_t = [ctx.enter_context(nc.psum_tensor(f"ps_t{i}", [P, BANK], F32)) for i in range(2)]
        ps_l = [ctx.enter_context(nc.psum_tensor(f"ps_l{i}", [P, BANK], F32)) for i in range(2)]
        ps_w = ctx.enter_context(nc.psum_tensor("ps_w", [P, BANK], F32))

        par_in, eye_in, text_in = sem("par_in"), sem("eye_in"), sem("text_in")
        x_in = [sem("x_in0"), sem("x_in1")]
        zeroed, bn_a, bn_b, bn_c = sem("zeroed"), sem("bn_a"), sem("bn_b"), sem("bn_c")
        lin_t, lin_c = sem("lin_t"), sem("lin_c")
        turned, padded_ready, conv_step, conv_ready = (
            sem("turned"), sem("padded_ready"), sem("conv_step"), sem("conv_ready"))
        lin_ready, lin_used = sem("lin_ready"), sem("lin_used")

        block = ctx.enter_context(nc.Block())

        @block.sync
        def _(sp):
            sp.dma_start(eye[:], d["eye"]).then_inc(eye_in, 16)
            n = 0
            for half in range(2):
                rows = slice(half * CH, half * CH + CH)
                for i, name in enumerate(["bn_gamma", "bn_beta", "bn_mean", "bn_var", "conv_b"]):
                    sp.dma_start(vec[rows, i:i + 1], col(d["L0_tok_" + name])).then_inc(par_in, 16)
                sp.dma_start(taps[rows, :], d["L0_tok_conv_w"].rearrange("c a h w -> c (a h w)")).then_inc(par_in, 16)
                sp.dma_start(lin_bias[:, half, :],
                             d["L0_tok_lin_b"].partition_broadcast(P)).then_inc(par_in, 16)
            sp.dma_start(lin_rows[:], d["L0_tok_lin_w"]).then_inc(par_in, 16)
            for q in range(PAIRS):
                if q >= 2:
                    sp.wait_ge(turned, (q - 1) * GROUPS)
                for i in range(2):
                    src = d["x"][2 * q + i].rearrange("(t r) w c -> (r w) t c", r=P // SIDE)
                    sp.dma_start(tokens[:, q % 2, :, i, :], src).then_inc(x_in[q % 2], 16)
            for b in range(BATCH):
                sp.dma_start(residual[:, b * TILES + IMAGE_TILES, :], d["txt"][b]).then_inc(text_in, 16)
            sp.wait_ge(text_in, 16 * BATCH)

        PARAMS = 16 * 15

        @block.gpsimd
        def _(pool):
            nc.gpsimd.memset(padded[:, 0], 0.0).then_inc(zeroed, 1)
            nc.gpsimd.memset(padded[:, 1], 0.0).then_inc(zeroed, 1)

        @block.scalar
        def _(act):
            act.wait_ge(bn_a, 1)
            nc.scalar.activation(bn[:, 1:2], bn[:, 0:1], ACT.Sqrt).then_inc(bn_b, 1)
            act.wait_ge(bn_c, 3)
            act.wait_ge(zeroed, 2)
            for q in range(PAIRS):
                for g in range(GROUPS):
                    k = q * GROUPS + g
                    act.wait_ge(turned, k + 1)
                    if g == 0 and q >= 2:
                        act.wait_ge(conv_ready, (q - 1) * PARTS)
                    nc.scalar.activation(
                        padded[:, q % 2, 1 + g * ROWS:1 + (g + 1) * ROWS, 1:1 + SIDE],
                        ps_t[k % 2][:, :].rearrange("p (r w) -> p r w", w=SIDE),
                        ACT.Identity, bias=shift[:, 0:1], scale=scale[:, 0:1]).then_inc(padded_ready, 1)

        @block.tensor
        def _(pe):
            pe.wait_ge(eye_in, 16)
            pe.wait_ge(par_in, PARAMS)
            nc.tensor.transpose(ps_w[0:CH, 0:CH], lin_rows[:], eye[0:CH, 0:CH]).then_inc(lin_t, 1)

            def turn(q):
                pe.wait_ge(x_in[q % 2], 32 * (q // 2 + 1))
                for g in range(GROUPS):
                    k = q * GROUPS + g
                    if k >= 2:
                        pe.wait_ge(padded_ready, k - 1)
                    for j in range(GROUP):
                        mm = nc.tensor.transpose(ps_t[k % 2][:, j * P:(j + 1) * P],
                                                 tokens[:, q % 2, g * GROUP + j, :, :], eye[:])
                    mm.then_inc(turned, 1)

            def linear(q):
                for g in range(GROUPS):
                    k = q * GROUPS + g
                    pe.wait_ge(conv_ready, q * PARTS + g * PARTS // GROUPS + 1)
                    if k >= 2:
                        pe.wait_ge(lin_used, k - 1)
                    for j in range(GROUP):
                        t = g * GROUP + j
                        mm = nc.tensor.matmul(ps_l[k % 2][:, j * P:(j + 1) * P],
                                              conv[:, q % 2, t * P:(t + 1) * P], lin_both[:],
                                              start=True, stop=True)
                    mm.then_inc(lin_ready, 1)

            turn(0)
            pe.wait_ge(lin_c, 3)
            for q in range(PAIRS):
                if q + 1 < PAIRS:
                    turn(q + 1)
                linear(q)

        @block.vector
        def _(dve):
            dve.wait_ge(par_in, PARAMS)
            nc.vector.tensor_scalar(bn[:, 0:1], vec[:, 3:4], EPS, None, ALU.add).then_inc(bn_a, 1)
            nc.vector.memset(lin_both[:], 0.0).then_inc(lin_c, 1)
            dve.wait_ge(lin_t, 1)
            dve.wait_ge(lin_c, 1)
            for h in range(2):
                nc.vector.tensor_copy(lin_both[h * CH:h * CH + CH, h * CH:h * CH + CH],
                                      ps_w[0:CH, 0:CH]).then_inc(lin_c, 1)
            dve.wait_ge(bn_b, 1)
            nc.vector.reciprocal(bn[:, 2:3], bn[:, 1:2]).then_inc(bn_c, 1)
            dve.wait_ge(bn_c, 1)
            nc.vector.tensor_tensor(scale[:], bn[:, 2:3], vec[:, 0:1], ALU.mult).then_inc(bn_c, 1)
            dve.wait_ge(bn_c, 2)
            nc.vector.scalar_tensor_tensor(out=bn[:, 3:4], in0=vec[:, 2:3], scalar=scale[:, 0:1],
                                           in1=vec[:, 1:2], op0=ALU.mult, op1=ALU.subtract).then_inc(bn_a, 1)
            dve.wait_ge(bn_a, 2)
            nc.vector.tensor_scalar(shift[:], bn[:, 3:4], -1.0, None, ALU.mult).then_inc(bn_c, 1)

            steps = [0]

            def convolve(q, part):
                r0 = part * SIDE // PARTS
                n = SIDE // PARTS
                acc = conv[:, q % 2, part * PART:(part + 1) * PART].rearrange("p (r w) -> p r w", w=SIDE)
                groups = min(GROUPS, (r0 + n) // ROWS + 1)
                dve.wait_ge(padded_ready, q * GROUPS + groups)
                if q >= 2 and part == 0:
                    dve.wait_ge(lin_ready, (q - 1) * GROUPS)
                for k in range(9):
                    window = padded[:, q % 2, r0 + k // 3:r0 + k // 3 + n, k % 3:k % 3 + SIDE]
                    if k == 0:
                        ins = nc.vector.tensor_scalar(acc, window, taps[:, 0:1], vec[:, 4:5], ALU.mult, ALU.add)
                    else:
                        dve.wait_ge(conv_step, steps[0])
                        ins = nc.vector.scalar_tensor_tensor(out=acc, in0=window, scalar=taps[:, k:k + 1],
                                                             in1=acc, op0=ALU.mult, op1=ALU.add)
                    if k < 8:
                        steps[0] += 1
                        ins.then_inc(conv_step, 1)
                    else:
                        ins.then_inc(conv_ready, 1)

            def store(q, g):
                k = q * GROUPS + g
                dve.wait_ge(lin_ready, k + 1)
                for i in range(2):
                    t0 = (2 * q + i) * TILES + g * GROUP
                    ins = nc.vector.tensor_tensor(
                        residual[:, t0:t0 + GROUP, :],
                        ps_l[k % 2][:, :].rearrange("p (t i c) -> p i t c", t=GROUP, i=2)[:, i],
                        lin_bias[:, i:i + 1, :].broadcast_to([P, GROUP, CH]), ALU.add)
                ins.then_inc(lin_used, 1)

            for q in range(PAIRS):
                for part in range(PARTS):
                    convolve(q, part)
                    if part:
                        for g in range((part - 1) * GROUPS // PARTS, part * GROUPS // PARTS):
                            store(q, g)
                for g in range((PARTS - 1) * GROUPS // PARTS, GROUPS):
                    store(q, g)


def statistics(nc, residual, mean, rstd):
    with ExitStack() as ctx:
        def sb(name, shape, dt=F32):
            return ctx.enter_context(nc.sbuf_tensor(name, shape, dt))

        def sem(name):
            return ctx.enter_context(nc.semaphore(name))

        total = sb("total", [P, ALL_TILES])
        centred = sb("centred", [P, 2, TILES, CH])
        squared = sb("squared", [P, 2, TILES, CH])
        squares = sb("squares", [P, ALL_TILES])
        power = sb("power", [P, ALL_TILES])
        s_sum, s_mean, s_cent, s_sq, s_ss, s_var, s_pow = (
            sem(n) for n in ("s_sum", "s_mean", "s_cent", "s_sq", "s_ss", "s_var", "s_pow"))
        block = ctx.enter_context(nc.Block())

        def tiles(b):
            return slice(b * TILES, (b + 1) * TILES)

        @block.vector
        def _(dve):
            def square_sums(b):
                dve.wait_ge(s_sq, b + 1)
                nc.vector.tensor_reduce(squares[:, tiles(b)], squared[:, b % 2], AX.X, ALU.add).then_inc(s_ss, 1)

            for b in range(BATCH):
                nc.vector.tensor_reduce(total[:, tiles(b)], residual[:, tiles(b), :], AX.X, ALU.add).then_inc(s_sum, 1)
                dve.wait_ge(s_sum, b + 1)
                nc.vector.tensor_scalar(mean[:, tiles(b)], total[:, tiles(b)], 1.0 / CH, None,
                                        ALU.mult).then_inc(s_mean, 1)
                if b:
                    square_sums(b - 1)
            square_sums(BATCH - 1)
            dve.wait_ge(s_ss, BATCH)
            nc.vector.tensor_scalar(total[:], squares[:], 1.0 / CH, EPS, ALU.mult, ALU.add).then_inc(s_var, 1)

        @block.gpsimd
        def _(pool):
            nc.gpsimd.memset(power[:], -0.5).then_inc(s_pow, 1)
            for b in range(BATCH):
                pool.wait_ge(s_mean, b + 1)
                if b >= 2:
                    pool.wait_ge(s_sq, b - 1)
                nc.gpsimd.tensor_tensor(centred[:, b % 2], residual[:, tiles(b), :],
                                        mean[:, tiles(b)].unsqueeze(2).broadcast_to([P, TILES, CH]),
                                        ALU.subtract).then_inc(s_cent, 1)
            pool.wait_ge(s_pow, 1)
            pool.wait_ge(s_var, 1)
            nc.gpsimd.tensor_tensor(rstd[:], total[:], power[:], ALU.pow).then_inc(s_pow, 1)

        @block.scalar
        def _(act):
            for b in range(BATCH):
                act.wait_ge(s_cent, b + 1)
                if b >= 2:
                    act.wait_ge(s_ss, b - 1)
                nc.scalar.activation(squared[:, b % 2], centred[:, b % 2], ACT.Square).then_inc(s_sq, 1)


def attend(nc, d, residual, mean, rstd, eye):
    with ExitStack() as ctx:
        def sb(name, shape, dt=F32):
            return ctx.enter_context(nc.sbuf_tensor(name, shape, dt))

        def sem(name):
            return ctx.enter_context(nc.semaphore(name))

        def psum(name, shape):
            return ctx.enter_context(nc.psum_tensor(name, shape, F32))

        keys1 = sb("keys1", [P, 2 * SEQ], F32R)
        keys2 = sb("keys2", [P, 2 * SEQ], F32R)
        values = sb("values", [P, 2, TILES, CH])
        waves_q = sb("waves_q", [P, SEQ], F32R)
        next_q = sb("next_q", [P, CHUNK], F32R)
        query1 = sb("query1", [P, 2 * CHUNK], F32R)
        query2 = sb("query2", [P, 2 * CHUNK], F32R)
        normed = sb("normed", [P, CHUNK_TILES, CH])
        centred = sb("centred_x", [P, CHUNK_TILES, CH])
        probs = sb("probs", [P, P_SLOTS, 2, CHUNK])
        summed = sb("summed", [P, CHUNK])
        maxima = sb("maxima", [P, CHUNK_TILES, WHOLE + 1])
        maximum = sb("maximum", [P, CHUNK_TILES])
        recip = sb("recip", [P, CHUNK_TILES])
        update = sb("update", [P, CHUNK_TILES, CH])
        wq2 = sb("wq2", [CH, 2, CH])
        wkb = sb("wkb", [CH, CH + 1])
        bq = sb("bq", [CH, 1])
        wv = sb("wv", [CH, CH])
        wvd = sb("wvd", [CH, 2, CH])
        w_query = sb("w_query", [P, CH + 1])
        b_query = sb("b_query", [CH + 1, 1])
        w_value = sb("w_value", [P, CH + 1])
        beta_col = sb("beta_col", [P, 1])
        masks = sb("masks", [P, 4])

        scores = [psum(f"scores{i}", [P, 2, BANK]) for i in range(2)]
        acc = psum("acc", [P, BANK])
        misc = psum("misc", [P, BANK])
        tops = [psum(f"tops{i}", [P, BANK]) for i in range(2)]

        names = ("pe_passed", "pool_passed", "dve_passed", "par_in", "wave_in", "set_a", "set_b", "set_c", "set_w", "w_mm",
                 "x_centred", "x_ready", "v_ready", "ext_ready", "q_copied",
                 "t_ready", "t_high", "t_used", "g_ready", "g_high", "g_used",
                 "top_done", "top_used", "max_done", "row_mm", "row_used",
                 "s_done", "p_done", "pv_done", "acc_used", "o_ready", "o_used", "o_scaled", "o_mul", "o_rec")
        S = {n: sem(n) for n in names}
        block = ctx.enter_context(nc.Block())

        E0, E1 = CH, CH + EXTRA
        HALF = SEQ // 2

        def steps(eng, step):
            with eng.Fori(0, BATCH // 2 - 1) as i:
                for p in range(2):
                    n0 = i * (2 * CHUNKS) + p * CHUNKS
                    with eng.Fori(0, CHUNKS - 1) as c:
                        step(n0 + c, p, c, (p, c + 1), True)
                    step(n0 + (CHUNKS - 1), p, CHUNKS - 1, (1 - p, 0), True)
            for p in range(2):
                n0 = (BATCH - 2 + p) * CHUNKS
                with eng.Fori(0, CHUNKS - 1) as c:
                    step(n0 + c, p, c, (p, c + 1), p == 0)
                step(n0 + CHUNKS - 1, p, CHUNKS - 1, (1, 0) if p == 0 else None, p == 0)

        def unit_count(n, u):
            return n * UNITS + (u + 1 + UNITS)

        def before_unit(n, u, slot):
            others = [v for v in range(UNITS) if slot(v) == slot(u)]
            at = others.index(u)
            if at:
                return unit_count(n, others[at - 1])
            return n * UNITS + (others[-1] + 1)

        def score_slot(u):
            return u % 2

        def prob_slot(u):
            return u % (P_SLOTS - 1) if u < UNITS - 1 else P_SLOTS - 1

        def tiles_of(u):
            return [t for t in (2 * u, 2 * u + 1) if t < TILES]

        PAIRS = [(u, u + 1) for u in range(0, UNITS - 1, 2)] + [(UNITS - 1,)]
        QUERIES_AT, TURN_AT, ROW_AT = 0, 1, len(PAIRS) - 2
        TOPS_IN = [0, 4, 5, 4, 4, 4, 4, 0, 0]
        assert sum(TOPS_IN) == MAXES and len(TOPS_IN) == len(PAIRS)

        def tops_at(i):
            first = sum(TOPS_IN[:i])
            ks = list(range(first, first + TOPS_IN[i]))
            cut = max(1, len(ks) - 3)
            return ks[:cut], ks[cut:cut + 1], ks[cut + 1:]

        EARLY = 4
        T_LOW_AFTER = 6

        @block.sync
        def _(sp):
            sp.dma_start(wq2[:, 0, :], d["L0_attn_Wq"]).then_inc(S["par_in"], 16)
            sp.dma_start(wq2[:, 1, :], d["L0_attn_Wq"]).then_inc(S["par_in"], 16)
            sp.dma_start(wkb[:, 0:CH], d["L0_attn_Wk"]).then_inc(S["par_in"], 16)
            sp.dma_start(wkb[:, CH:CH + 1], col(d["L0_attn_bk"])).then_inc(S["par_in"], 16)
            sp.dma_start(bq[:], col(d["L0_attn_bq"])).then_inc(S["par_in"], 16)
            sp.dma_start(wv[:], d["L0_attn_Wv"]).then_inc(S["par_in"], 16)
            sp.dma_start(wvd[:, 0, CH - 1:CH], col(d["L0_attn_bv"])).then_inc(S["par_in"], 16)
            sp.dma_start(wvd[:, 1, CH - 1:CH], col(d["L0_attn_bv"])).then_inc(S["par_in"], 16)
            sp.dma_start(w_value[:, CH:CH + 1], d["sum_col"]).then_inc(S["par_in"], 16)
            sp.dma_start(masks[E0:E1, :], d["masks"]).then_inc(S["par_in"], 16)
            sp.dma_start(beta_col[E0:E0 + 1, :], d["waves"][0:1, 0:1]).then_inc(S["par_in"], 16)
            for r in range(3):
                for w in range(len(PERIODS)):
                    at = E0 + 1 + r * BIAS_ROWS + 2 * w
                    sp.dma_start(beta_col[at:at + 2, :],
                                 d["L0_attn_beta"][w:w + 1].partition_broadcast(2)).then_inc(S["par_in"], 16)
            raw = values[:].rearrange("p a t c -> p (a t c)")
            sp.dma_start(raw[E0:E1, :], d["waves"]).then_inc(S["wave_in"], 16)

        PARAMS = 16 * (11 + 3 * len(PERIODS))

        @block.gpsimd
        def _(pool):
            def normalise(j):
                stat = (ds(j * CHUNK_TILES, CHUNK_TILES))
                pool.wait_ge(S["t_ready"], j + 1)
                nc.gpsimd.tensor_tensor(centred[:], residual[:, stat, :],
                                        mean[:, stat].unsqueeze(2).broadcast_to([P, CHUNK_TILES, CH]),
                                        ALU.subtract).then_inc(S["x_centred"], 1)
                pool.wait_ge(S["x_centred"], j + 1)
                nc.gpsimd.tensor_tensor(normed[:], centred[:],
                                        rstd[:, stat].unsqueeze(2).broadcast_to([P, CHUNK_TILES, CH]),
                                        ALU.mult).then_inc(S["x_ready"], 1)
                pool.wait_ge(S["x_ready"], j + 1)

            def copy_values(j, p, c):
                stand_alone(pool, S["pool_passed"])
                nc.gpsimd.tensor_copy(values[:, p, ds(c * CHUNK_TILES, CHUNK_TILES), 0:CH - 1],
                                      normed[:, :, 0:CH - 1]).then_inc(S["v_ready"], 1)

            def next_extra_rows(r, c, prepared):
                pool.wait_ge(S["v_ready"], prepared)
                pool.wait_ge(S["row_used"], r + 1)
                stand_alone(pool, S["pool_passed"])
                nc.gpsimd.tensor_copy(next_q[E0:E1, :], waves_q[E0:E1, ds(c * CHUNK, CHUNK)]).then_inc(S["ext_ready"], 1)
                pool.wait_ge(S["ext_ready"], 2 * r + 1)

            def extra_rows(r, c):
                nc.gpsimd.tensor_copy(query1[E0:E1, ds((r % 2) * CHUNK, CHUNK)],
                                      waves_q[E0:E1, ds(c * CHUNK, CHUNK)]).then_inc(S["ext_ready"], 1)

            def high_rows(r):
                pool.wait_ge(S["ext_ready"], 2 * r + 2)
                pool.wait_ge(S["g_high"], r + 1)
                stand_alone(pool, S["pool_passed"])
                for to in (query1, query2):
                    nc.gpsimd.tensor_copy(to[0:CH, ds((r % 2) * CHUNK, CHUNK)],
                                          next_q[0:CH, :]).then_inc(S["q_copied"], 1)

            pool.wait_ge(S["set_c"], 2)
            nc.gpsimd.memset(values[:, :, :, CH - 1:CH], 1.0)
            with pool.Fori(0, CHUNKS) as c:
                normalise(c)
                copy_values(c, 0, c)
            next_extra_rows(0, 0, CHUNKS)
            extra_rows(0, 0)
            high_rows(0)

            def step(n, p, c, nxt, prep):
                if nxt:
                    next_extra_rows(n + 1, nxt[1], n + CHUNKS if prep else STEPS)
                if prep:
                    normalise(n + CHUNKS)
                if nxt:
                    pool.wait_ge(S["pv_done"], n * UNITS + UNITS)
                    stand_alone(pool, S["pool_passed"])
                    extra_rows(n + 1, nxt[1])
                    high_rows(n + 1)
                if prep:
                    copy_values(n + CHUNKS, 1 - p, c)

            steps(pool, step)

        @block.scalar
        def _(act):
            def keys_high(j, p, c):
                act.wait_ge(S["t_ready"], j + 2)
                at = ds(p * SEQ + c * CHUNK, CHUNK)
                nc.scalar.activation(keys1[0:CH, at], misc[0:CH, 0:CHUNK], ACT.Identity).then_inc(S["t_high"], 1)
                nc.scalar.activation(keys2[CH:P, at], misc[0:CH, 0:CHUNK], ACT.Identity).then_inc(S["t_high"], 1)

            def query_high(r):
                act.wait_ge(S["g_ready"], r + 1)
                act.wait_ge(S["ext_ready"], 2 * r + 1)
                nc.scalar.activation(next_q[0:CH + 1, :], misc[0:CH + 1, 0:CHUNK], ACT.Identity,
                                     bias=b_query[:, 0:1]).then_inc(S["g_high"], 1)

            def exponential(n, u):
                act.wait_ge(S["s_done"], n * UNITS + (u + 1))
                act.wait_ge(S["pv_done"], before_unit(n, u, prob_slot))
                k = len(tiles_of(u))
                nc.scalar.activation(probs[:, prob_slot(u), 0:k, :], scores[score_slot(u)][:, 0:k, 0:CHUNK],
                                     ACT.Exp).then_inc(S["p_done"], 1)

            def take_sums(n):
                act.wait_ge(S["pv_done"], unit_count(n, UNITS - 1))
                nc.scalar.activation(summed[:], acc[:, 0:CHUNK], ACT.Identity).then_inc(S["acc_used"], 1)

            act.wait_ge(S["set_b"], 4)
            with act.Fori(0, CHUNKS) as c:
                keys_high(c, 0, c)
            query_high(0)
            for u in range(2):
                exponential(0, u)

            def step(n, p, c, nxt, prep):
                for u in range(2, UNITS):
                    exponential(n, u)
                    if u == 2 * QUERIES_AT + 3 and nxt:
                        query_high(n + 1)
                    if u == 2 * TURN_AT + 3 and prep:
                        keys_high(n + CHUNKS, 1 - p, c)
                if nxt:
                    exponential(n + 1, 0)
                    exponential(n + 1, 1)
                take_sums(n)

            steps(act, step)

        @block.tensor
        def _(pe):
            pe.sem_inc(S["t_ready"], 1)
            pe.sem_inc(S["pv_done"], UNITS)

            pe.wait_ge(S["par_in"], PARAMS)
            nc.tensor.matmul(misc[:, 0:CH + 1], wq2[:].rearrange("e a j -> e (a j)"), wkb[:],
                             start=True, stop=True).then_inc(S["w_mm"], 1)
            nc.tensor.matmul(tops[0][0:CH + 1, 0:1], wkb[:], bq[:], start=True, stop=True).then_inc(S["w_mm"], 1)
            pe.wait_ge(S["set_a"], 3)
            nc.tensor.matmul(tops[1][:, 0:CH], wvd[:].rearrange("e a j -> e (a j)"), eye[0:CH, 0:CH],
                             start=True, stop=True).then_inc(S["w_mm"], 1)

            def turn(j):
                pe.wait_ge(S["x_ready"], j + 1)
                stand_alone(pe, S["pe_passed"])
                for t in range(CHUNK_TILES):
                    mm = nc.tensor.transpose(misc[0:CH, t * P:(t + 1) * P], normed[:, t, :], eye[:])
                mm.then_inc(S["t_ready"], 1)

            def queries(r, p, c):
                nc.tensor.matmul(misc[0:CH + 1, 0:CHUNK], w_query[:],
                                 keys2[:, ds(p * SEQ + c * CHUNK, CHUNK)].bitcast(F32),
                                 start=True, stop=True).then_inc(S["g_ready"], 1)

            def top(r, k, p):
                if k >= 2:
                    pe.wait_ge(S["top_used"], r * MAXES + (k - 1))
                for t in ([k // WHOLE] if k < WHOLE * CHUNK_TILES else range(CHUNK_TILES)):
                    a, n, to = (k % WHOLE * BANK, BANK, 0) if k < WHOLE * CHUNK_TILES else (WHOLE * BANK, REST, t * REST)
                    mm = nc.tensor.matmul(tops[k % 2][:, to:to + n], next_q[0:E1, t * P:(t + 1) * P],
                                          keys1[0:E1, p * SEQ + a:p * SEQ + a + n], start=True, stop=True)
                mm.then_inc(S["top_done"], 1)

            def next_tops(n, ks, nxt, prep):
                for k in ks if nxt else ():
                    if k == 0:
                        pe.wait_ge(S["g_high"], n + 2)
                        pe.wait_ge(S["o_used"], n + 1)
                    if k == 1:
                        pe.wait_ge(S["row_used"], n + 2)
                    if prep and k == WHOLE - 1:
                        pe.wait_ge(S["t_high"], (n + CHUNKS) * 2 + 2)
                    top(n + 1, k, nxt[0])

            def row(r):
                pe.wait_ge(S["max_done"], r + 1)
                for t in range(CHUNK_TILES):
                    mm = nc.tensor.matmul(tops[1][0:1, t * P:(t + 1) * P], maximum[:, t:t + 1], eye[:],
                                          start=True, stop=True)
                mm.then_inc(S["row_mm"], 1)

            def score(n, u, p):
                if u < 2:
                    pe.wait_ge(S["row_used"], n + 2)
                    pe.wait_ge(S["q_copied"], 2 * n + 2)
                    pe.wait_ge(S["g_used"], n + 1)
                pe.wait_ge(S["p_done"], before_unit(n, u, score_slot))
                at = ds((n % 2) * CHUNK, CHUNK)
                for i, t in enumerate(tiles_of(u)):
                    cols = slice(p * SEQ + t * P, p * SEQ + (t + 1) * P)
                    nc.tensor.matmul(scores[score_slot(u)][:, i, 0:CHUNK], keys1[0:E1, cols], query1[0:E1, at],
                                     start=True, stop=False)
                    mm = nc.tensor.matmul(scores[score_slot(u)][:, i, 0:CHUNK], keys2[:, cols], query2[:, at],
                                          start=False, stop=True)
                mm.then_inc(S["s_done"], 1)

            def weigh(n, u, p):
                pe.wait_ge(S["p_done"], unit_count(n, u))
                if u == 0:
                    pe.wait_ge(S["acc_used"], n + 1)
                for i, t in enumerate(tiles_of(u)):
                    mm = nc.tensor.matmul(acc[i * CH:(i + 1) * CH, 0:CHUNK], values[:, p, t, :],
                                          probs[:, prob_slot(u), i, :],
                                          start=(u == 0), stop=(t >= TILES - 2))
                mm.then_inc(S["pv_done"], 1)

            def project(n):
                pe.wait_ge(S["acc_used"], n + 2)
                pe.wait_ge(S["o_used"], n + 1)
                for t in range(CHUNK_TILES):
                    mm = nc.tensor.matmul(tops[0][:, t * (CH + 1):(t + 1) * (CH + 1)],
                                          summed[:, t * P:(t + 1) * P], w_value[:], start=True, stop=True)
                mm.then_inc(S["o_ready"], 1)

            pe.wait_ge(S["set_b"], 4)
            with pe.Fori(0, CHUNKS) as c:
                pe.wait_ge(S["t_used"], c + 1)
                turn(c)
            pe.wait_ge(S["t_used"], CHUNKS + 1)
            queries(0, 0, 0)
            pe.wait_ge(S["g_high"], 1)
            for k in range(MAXES):
                top(0, k, 0)
            pe.wait_ge(S["top_used"], MAXES)
            row(0)
            for u in range(EARLY):
                score(0, u, 0)

            def step(n, p, c, nxt, prep):
                for i, pair in enumerate(PAIRS):
                    before, between, after = tops_at(i)
                    if i == len(PAIRS) - 1:
                        ahead = [(n + 1, 0, nxt[0]), (n + 1, 1, nxt[0])] if nxt else []
                    else:
                        ahead = [(n, u, p) for u in PAIRS[i + 1] if u >= EARLY]
                    if nxt and i == ROW_AT:
                        row(n + 1)
                    next_tops(n, before, nxt, prep)
                    if ahead:
                        score(*ahead[0])
                    next_tops(n, between, nxt, prep)
                    if ahead[1:]:
                        score(*ahead[1])
                    next_tops(n, after, nxt, prep)
                    if nxt and i == QUERIES_AT:
                        pe.wait_ge(S["t_used"], (n + CHUNKS if prep else STEPS) + 1)
                        queries(n + 1, *nxt)
                    if prep and i == TURN_AT:
                        pe.wait_ge(S["g_used"], n + 2)
                        turn(n + CHUNKS)
                    for u in pair:
                        weigh(n, u, p)
                if nxt:
                    for u in range(2, EARLY):
                        score(n + 1, u, nxt[0])
                project(n)

            steps(pe, step)

        @block.vector
        def _(dve):
            dve.sem_inc(S["t_used"], 1)
            dve.sem_inc(S["row_used"], 1)
            dve.sem_inc(S["o_used"], 1)
            dve.sem_inc(S["p_done"], UNITS)
            dve.sem_inc(S["acc_used"], 1)

            dve.wait_ge(S["par_in"], PARAMS)
            for a in range(2):
                nc.vector.tensor_scalar(wvd[:, a, 0:CH - 1], wv[:, 0:CH - 1], wv[:, CH - 1:CH], None,
                                        ALU.subtract).then_inc(S["set_a"], 1)
            nc.vector.memset(maximum[:], 0.0).then_inc(S["set_a"], 1)
            dve.wait_ge(S["w_mm"], 1)
            nc.vector.tensor_scalar(w_query[:], misc[:, 0:CH + 1], CH ** -0.5, None, ALU.mult).then_inc(S["set_b"], 1)
            dve.wait_ge(S["w_mm"], 2)
            nc.vector.tensor_scalar(b_query[:], tops[0][0:CH + 1, 0:1], CH ** -0.5, None, ALU.mult).then_inc(S["set_b"], 1)
            dve.wait_ge(S["w_mm"], 3)
            nc.vector.tensor_copy(w_value[:, 0:CH], tops[1][:, 0:CH]).then_inc(S["set_b"], 1)

            raw = values[:].rearrange("p a t c -> p (a t c)")
            tmp = probs[:].rearrange("p a b c -> p (a b c)")
            dve.wait_ge(S["wave_in"], 16)
            count = [0]

            def link(ins):
                count[0] += 1
                ins.then_inc(S["set_w"], 1)
                dve.wait_ge(S["set_w"], count[0])

            rows = slice(E0, E1)
            for side in range(2):
                for h in range(2):
                    at = slice(h * HALF, (h + 1) * HALF)
                    target = keys1 if side else waves_q
                    if side:
                        link(nc.vector.tensor_scalar(raw[rows, at], raw[rows, at], beta_col[rows, 0:1], None, ALU.mult))
                    link(nc.vector.tensor_copy(target[rows, at], raw[rows, at]))
                    low = tmp[rows, 0:HALF]
                    link(nc.vector.tensor_tensor(low, raw[rows, at], target[rows, at].bitcast(F32), ALU.subtract))
                    m = 0 if side else 2
                    link(nc.vector.tensor_scalar(low, low, masks[rows, m + 1:m + 2], None, ALU.mult))
                    link(nc.vector.scalar_tensor_tensor(out=target[rows, at], in0=target[rows, at].bitcast(F32),
                                                        scalar=masks[rows, m:m + 1], in1=low,
                                                        op0=ALU.mult, op1=ALU.add))
                    if side:
                        link(nc.vector.tensor_copy(keys1[rows, SEQ + h * HALF:SEQ + (h + 1) * HALF],
                                                   keys1[rows, at].bitcast(F32)))
            nc.vector.memset(recip[:], 0.0).then_inc(S["set_c"], 1)
            nc.vector.memset(maxima[:], 0.0).then_inc(S["set_c"], 1)
            nc.vector.memset(update[:], 0.0).then_inc(S["set_b"], 1)

            def keys_low(j, p, c):
                at = ds(p * SEQ + c * CHUNK, CHUNK)
                dve.wait_ge(S["t_high"], j * 2 + 2)
                nc.vector.tensor_tensor(keys2[0:CH, at], misc[0:CH, 0:CHUNK], keys1[0:CH, at].bitcast(F32),
                                        ALU.subtract).then_inc(S["t_used"], 1)

            def query_low(r):
                dve.wait_ge(S["g_high"], r + 1)
                nc.vector.scalar_tensor_tensor(
                    out=query2[CH:P, ds((r % 2) * CHUNK, CHUNK)], in0=misc[0:CH, 0:CHUNK],
                    scalar=b_query[0:CH, 0:1], in1=next_q[0:CH, :].bitcast(F32),
                    op0=ALU.add, op1=ALU.subtract).then_inc(S["g_used"], 1)

            def reduce(r, k):
                dve.wait_ge(S["top_done"], r * MAXES + (k + 1))
                if k < WHOLE * CHUNK_TILES:
                    t, j = divmod(k, WHOLE)
                    ins = nc.vector.tensor_reduce(maxima[:, t, j:j + 1], tops[k % 2][:, :], AX.X, ALU.max)
                else:
                    ins = nc.vector.tensor_reduce(maxima[:, :, WHOLE],
                                                  tops[k % 2][:, 0:CHUNK_TILES * REST].rearrange("p (t n) -> p t n", n=REST),
                                                  AX.X, ALU.max)
                ins.then_inc(S["top_used"], 1)

            def shift_row(r):
                dve.wait_ge(S["top_used"], r * MAXES + MAXES)
                nc.vector.tensor_reduce(maximum[:], maxima[:], AX.X, ALU.max).then_inc(S["max_done"], 1)
                dve.wait_ge(S["row_mm"], r + 1)
                dve.wait_ge(S["ext_ready"], 2 * r + 2)
                nc.vector.tensor_tensor(query1[E0:E0 + 1, ds((r % 2) * CHUNK, CHUNK)],
                                        next_q[E0:E0 + 1, :].bitcast(F32), tops[1][0:1, 0:CHUNK],
                                        ALU.subtract).then_inc(S["row_used"], 1)

            def add_update(n):
                out = tops[0][:, 0:CHUNK_TILES * (CH + 1)].rearrange("p (t c) -> p t c", c=CH + 1)
                at = ds(n * CHUNK_TILES, CHUNK_TILES)
                dve.wait_ge(S["o_ready"], n + 1)
                nc.vector.reciprocal(recip[:], out[:, :, CH]).then_inc(S["o_rec"], 1)
                dve.wait_ge(S["o_rec"], n + 1)
                nc.vector.tensor_tensor(update[:], out[:, :, 0:CH],
                                        recip[:].unsqueeze(2).broadcast_to([P, CHUNK_TILES, CH]),
                                        ALU.mult).then_inc(S["o_used"], 1)
                dve.wait_ge(S["o_used"], n + 2)
                nc.vector.tensor_tensor(residual[:, at, :], residual[:, at, :], update[:], ALU.add).then_inc(S["o_mul"], 1)

            with dve.Fori(0, CHUNKS) as c:
                keys_low(c, 0, c)
            query_low(0)
            for k in range(MAXES):
                reduce(0, k)
            shift_row(0)

            def step(n, p, c, nxt, prep):
                if nxt:
                    query_low(n + 1)
                for k in range(MAXES):
                    if nxt:
                        reduce(n + 1, k)
                    if k == T_LOW_AFTER and prep:
                        keys_low(n + CHUNKS, 1 - p, c)
                if nxt:
                    shift_row(n + 1)
                add_update(n)

            steps(dve, step)


def experts(nc, d, residual, eye, out):
    GROUP = 4
    GROUPS = ALL_TILES // GROUP
    COLS = GROUP * P
    AHEAD = 4
    SLOTS = 8
    with ExitStack() as ctx:
        def sb(name, shape, dt=F32):
            return ctx.enter_context(nc.sbuf_tensor(name, shape, dt))

        def sem(name):
            return ctx.enter_context(nc.semaphore(name))

        w1_raw = sb("w1_raw", [P, EXPERTS, HIDDEN])
        w1_high = sb("w1_high", [P, EXPERTS, HIDDEN], F32R)
        w1_low = sb("w1_low", [P, EXPERTS, HIDDEN], F32R)
        b1 = sb("b1", [HIDDEN, EXPERTS])
        w2 = sb("w2", [HIDDEN, EXPERTS, CH])
        b2_raw = sb("b2_raw", [48, CH])
        b2_high = sb("b2_high", [48, P], F32R)
        b2_low = sb("b2_low", [48, P], F32R)
        gate_raw = sb("gate_raw", [P, EXPERTS])
        gate_high = sb("gate_high", [P, EXPERTS], F32R)
        gate_low = sb("gate_low", [P, EXPERTS], F32R)
        gate_bias = sb("gate_bias", [P, 1, EXPERTS])
        pick_raw = sb("pick_raw", [48, EXPERTS * P])
        pick = sb("pick", [48, EXPERTS * P], F32R)
        iota = sb("iota", [P, 1, EXPERTS])
        gamma = sb("gamma", [P, 1, CH])
        beta = sb("beta", [P, 1, CH])
        half = sb("half", [P, GROUP])

        z = sb("z", [P, GROUP, CH])
        both = sb("both", [P, P], F32R)
        halves = sb("halves", [P, 2, COLS], F32R)
        gates_t = sb("gates_t", [48, 2, COLS], F32R)
        hidden = sb("hidden", [P, SLOTS, COLS])
        gated = sb("gated", [P, SLOTS, COLS])
        moe = sb("moe", [P, COLS])
        n1 = {k: sb("n1_" + k, s) for k, s in (("sum", [P, GROUP]), ("mean", [P, GROUP]), ("cent", [P, GROUP, CH]),
                                             ("sq", [P, GROUP, CH]), ("ss", [P, GROUP]), ("var", [P, GROUP]), ("rstd", [P, GROUP]))}
        n2 = {k: sb("n2_" + k, s) for k, s in (("sum", [P, GROUP]), ("mean", [P, GROUP]), ("cent", [P, GROUP, CH]),
                                             ("sq", [P, GROUP, CH]), ("ss", [P, GROUP]), ("var", [P, GROUP]), ("rstd", [P, GROUP]))}
        y = sb("y", [P, GROUP, CH])
        o1, o2, o3 = (sb(f"o{i}", [P, GROUP, CH]) for i in (1, 2, 3))
        result = sb("result", [P, 2, GROUP, CH])
        logits = sb("logits", [P, GROUP, EXPERTS])
        best = sb("best", [P, GROUP, 8])
        where = sb("where", [P, GROUP, 8], U32)
        where_f = sb("where_f", [P, GROUP, 2])
        gap = sb("gap", [P, GROUP])
        ratio = sb("ratio", [P, GROUP])
        one_up = sb("one_up", [P, GROUP])
        weight = sb("weight", [P, 2, GROUP])
        is0 = sb("is0", [P, GROUP, EXPERTS])
        is1 = sb("is1", [P, GROUP, EXPERTS])
        by0 = sb("by0", [P, GROUP, EXPERTS])
        by1 = sb("by1", [P, GROUP, EXPERTS])
        gates = sb("gates", [P, GROUP, EXPERTS])

        def psum(name):
            return ctx.enter_context(nc.psum_tensor(name, [P, BANK], F32))

        ps_hid = [psum(f"ps_hid{i}") for i in range(2)]
        ps_gate = [psum(f"ps_gate{i}") for i in range(AHEAD)]
        ps_moe = psum("ps_moe")
        ps_misc = psum("ps_misc")

        names = ("pe_passed", "pool_passed", "dve_passed", "w_in", "w_cast", "b2_zero", "power_set",
                 "n_dve", "c_dve", "p_cent", "p_sq", "p_rstd", "z_ready", "z_turned", "z_high", "z_low", "log_ready",
                 "ratio_ready", "gates_turned", "g_high", "g_low",
                 "hid_ready", "relu_ready", "gate_ready", "gated_ready", "moe_done", "moe_used",
                 "q_dve", "q_cent", "q_sq", "q_rstd", "out_turned", "y_ready", "o_chain", "result_ready", "stored0", "stored1")
        S = {n: sem(n) for n in names}
        block = ctx.enter_context(nc.Block())

        N_OPS = Q_OPS = 4
        MASKS = 1 + 2 * GROUP + 4
        C_OPS = MASKS + 6

        PE_AT = {"z": 0, "logits": 2, "out": 4, "gates": 8}
        ACT_AT = {"moe": 3, "z": 5, "exp": 9, "gates": 13}
        DVE_AT = {"mean": 0, "z": 3, "var": 4, "choose": 5, "add": 7, "weights": 8, "post_var": 10, "gates": 11}

        def steps(eng, step):
            step(0, 0, True, False)
            with eng.Fori(0, (GROUPS - 2) // 2) as i:
                for k in range(2):
                    step(i * 2 + (1 + k), 1 - k, True, True)
            step(GROUPS - 1, 1, False, True)

        W_LOADS = 16 * 16

        @block.sync
        def _(sp):
            for k in range(2):
                rows = slice(k * CH, (k + 1) * CH)
                sp.dma_start(w1_raw[rows], d["L0_ffn_w1"].rearrange("e c f -> c e f")).then_inc(S["w_in"], 16)
                sp.dma_start(gate_raw[rows], d["L0_ffn_gate_w"]).then_inc(S["w_in"], 16)
            sp.dma_start(w2[:], d["L0_ffn_w2"].rearrange("e f c -> f e c")).then_inc(S["w_in"], 16)
            sp.dma_start(pick_raw[:], d["pick"]).then_inc(S["w_in"], 16)
            sp.dma_start(iota[:, 0, :], d["iota"]).then_inc(S["w_in"], 16)
            sp.dma_start(gate_bias[:, 0, :], d["L0_ffn_gate_b"].partition_broadcast(P)).then_inc(S["w_in"], 16)
            sp.dma_start(gamma[:, 0, :], d["L0_ffn_gamma"].partition_broadcast(P)).then_inc(S["w_in"], 16)
            sp.dma_start(beta[:, 0, :], d["L0_ffn_beta"].partition_broadcast(P)).then_inc(S["w_in"], 16)
            with nc.allow_non_contiguous_dma("a small transposed load"):
                for k in range(4):
                    sp.dma_start(b1[:, 4 * k:4 * k + 4],
                                 d["L0_ffn_b1"][4 * k:4 * k + 4].rearrange("e f -> f e")).then_inc(S["w_in"], 16)
            sp.wait_ge(S["b2_zero"], 1)
            for k in range(2):
                sp.dma_start(b2_raw[32 * k:32 * k + EXPERTS, :], d["L0_ffn_b2"]).then_inc(S["w_in"], 16)

            flat = out.rearrange("b (t p) c -> (b t) p c", p=P)

            def store(g, p):
                sp.wait_ge(S["result_ready"], g + 1)
                sp.dma_start(flat[ds(g * GROUP, GROUP)].rearrange("t p c -> p t c"),
                             result[:, p]).then_inc(S[f"stored{p}"], 16)

            def step(g, p, prep, post):
                if post:
                    store(g - 1, 1 - p)

            steps(sp, step)
            store(GROUPS - 1, 1)
            sp.wait_ge(S["stored0"], 16 * (GROUPS // 2))
            sp.wait_ge(S["stored1"], 16 * (GROUPS // 2) + 16)

        def norm_on_pool(pool, n, x, r, pre):
            dve, ops = (S["n_dve"], N_OPS) if pre else (S["q_dve"], Q_OPS)
            cent, sq = (S["p_cent"], S["p_sq"]) if pre else (S["q_cent"], S["q_sq"])
            pool.wait_ge(dve, r * ops + 2)
            nc.gpsimd.tensor_tensor(n["cent"][:], x, n["mean"][:].unsqueeze(2).broadcast_to([P, GROUP, CH]),
                                    ALU.subtract).then_inc(cent, 1)
            pool.wait_ge(cent, r + 1)
            nc.gpsimd.tensor_tensor(n["sq"][:], n["cent"][:], n["cent"][:], ALU.mult).then_inc(sq, 1)

        def root_on_pool(pool, n, r, pre):
            dve, ops = (S["n_dve"], N_OPS) if pre else (S["q_dve"], Q_OPS)
            rstd = S["p_rstd"] if pre else S["q_rstd"]
            pool.wait_ge(dve, r * ops + 4)
            nc.gpsimd.tensor_tensor(n["rstd"][:], n["var"][:], half[:], ALU.pow).then_inc(rstd, 1)
            pool.wait_ge(rstd, r + 1)

        @block.gpsimd
        def _(pool):
            nc.gpsimd.memset(b2_raw[:], 0.0).then_inc(S["b2_zero"], 1)
            nc.gpsimd.memset(half[:], -0.5).then_inc(S["power_set"], 1)
            pool.wait_ge(S["power_set"], 1)

            def rows_of(g):
                return residual[:, ds(g * GROUP, GROUP), :]

            def prep(r):
                norm_on_pool(pool, n1, rows_of(r % GROUPS), r, True)
                root_on_pool(pool, n1, r, True)
                if not (isinstance(r, int) and r == 0):
                    pool.wait_ge(S["z_turned"], r)
                nc.gpsimd.tensor_tensor(z[:], n1["cent"][:], n1["rstd"][:].unsqueeze(2).broadcast_to([P, GROUP, CH]),
                                        ALU.mult).then_inc(S["z_ready"], 1)

            def post_a(r):
                norm_on_pool(pool, n2, y[:], r, False)

            def post_b(r, p):
                root_on_pool(pool, n2, r, False)
                chain = [(o1, n2["cent"][:], n2["rstd"][:].unsqueeze(2), ALU.mult),
                         (o2, o1[:], gamma[:], ALU.mult),
                         (o3, o2[:], beta[:], ALU.add)]
                for k, (to, a, b, op) in enumerate(chain):
                    nc.gpsimd.tensor_tensor(to[:], a, b.broadcast_to([P, GROUP, CH]), op).then_inc(S["o_chain"], 1)
                    pool.wait_ge(S["o_chain"], r * 3 + (k + 1))
                pool.wait_ge(S[f"stored{p}"], (r // 2) * 16 + 16)
                nc.gpsimd.tensor_tensor(result[:, p], o3[:], rows_of(r), ALU.add).then_inc(S["result_ready"], 1)

            prep(0)
            prep(1)

            def step(g, p, nxt, post):
                if nxt:
                    prep(g + 2)
                if post:
                    post_a(g - 1)
                    post_b(g - 1, 1 - p)

            steps(pool, step)
            post_a(GROUPS - 1)
            post_b(GROUPS - 1, 1)

        @block.scalar
        def _(act):
            act.sem_inc(S["stored0"], 16)
            act.sem_inc(S["stored1"], 16)
            act.sem_inc(S["relu_ready"], EXPERTS)
            act.sem_inc(S["moe_used"], 1)

            def high_z(r, p):
                act.wait_ge(S["z_turned"], r + 1)
                nc.scalar.activation(halves[0:CH, p, :], ps_misc[0:CH, :], ACT.Identity).then_inc(S["z_high"], 1)

            def exp_gap(r):
                act.wait_ge(S["c_dve"], r * C_OPS + MASKS - 3)
                nc.scalar.activation(ratio[:], gap[:], ACT.Exp).then_inc(S["ratio_ready"], 1)

            def high_gates(r, p):
                act.wait_ge(S["gates_turned"], r + 1)
                nc.scalar.activation(gates_t[0:EXPERTS, p, :], ps_misc[0:EXPERTS, :], ACT.Identity).then_inc(S["g_high"], 1)

            def take_moe(g):
                act.wait_ge(S["moe_done"], (g + 1) * EXPERTS)
                nc.scalar.activation(moe[:], ps_moe[:], ACT.Identity).then_inc(S["moe_used"], 1)

            def relu(g, e):
                act.wait_ge(S["hid_ready"], g * EXPERTS + (e + 1))
                act.wait_ge(S["gated_ready"], g * EXPERTS + (e + 1 - SLOTS + EXPERTS))
                nc.scalar.activation(hidden[:, e % SLOTS, :], ps_hid[e % 2][:, :], ACT.Relu,
                                     bias=b1[:, e:e + 1]).then_inc(S["relu_ready"], 1)

            act.wait_ge(S["w_cast"], 14)
            high_z(0, 0)
            exp_gap(0)
            high_gates(0, 0)

            def step(g, p, prep, post):
                for e in range(EXPERTS):
                    relu(g, e)
                    if prep and e == ACT_AT["z"]:
                        high_z(g + 1, 1 - p)
                    if prep and e == ACT_AT["exp"]:
                        exp_gap(g + 1)
                    if prep and e == ACT_AT["gates"]:
                        high_gates(g + 1, 1 - p)
                    if post and e == ACT_AT["moe"]:
                        take_moe(g - 1)

            steps(act, step)
            take_moe(GROUPS - 1)

        @block.tensor
        def _(pe):
            pe.wait_ge(S["w_in"], W_LOADS)
            pe.wait_ge(S["w_cast"], 14)

            def turn_z(r):
                pe.wait_ge(S["z_ready"], r + 1)
                stand_alone(pe, S["pe_passed"])
                for t in range(GROUP):
                    mm = nc.tensor.transpose(ps_misc[0:CH, t * P:(t + 1) * P], z[:, t, :], eye[:])
                mm.then_inc(S["z_turned"], 1)

            def gate_logits(r, p):
                pe.wait_ge(S["z_low"], r + 1)
                for t in range(GROUP):
                    to = ps_misc[:, t * EXPERTS:(t + 1) * EXPERTS]
                    zt = halves[:, p, t * P:(t + 1) * P]
                    nc.tensor.matmul(to, zt, gate_high[:], start=True, stop=False)
                    mm = nc.tensor.matmul(to, zt, gate_low[:], start=False, stop=True)
                mm.then_inc(S["log_ready"], 1)

            def turn_gates(r):
                pe.wait_ge(S["c_dve"], (r + 1) * C_OPS)
                pe.wait_ge(S["y_ready"], r)
                for t in range(GROUP):
                    mm = nc.tensor.transpose(ps_misc[0:EXPERTS, t * P:(t + 1) * P], gates[:, t, :], eye[:])
                mm.then_inc(S["gates_turned"], 1)

            def hid(g, e, p):
                if e == 0:
                    pe.wait_ge(S["z_low"], g + 1)
                pe.wait_ge(S["relu_ready"], g * EXPERTS + (e - 1 + EXPERTS))
                nc.tensor.matmul(ps_hid[e % 2][:, :], w1_high[:, e, :], halves[:, p, :], start=True, stop=False)
                nc.tensor.matmul(ps_hid[e % 2][:, :], w1_low[:, e, :], halves[:, p, :],
                                 start=False, stop=True).then_inc(S["hid_ready"], 1)

            def gate(g, e, p):
                if e == 0:
                    pe.wait_ge(S["g_low"], g + 1)
                pe.wait_ge(S["gated_ready"], g * EXPERTS + (e + 1 - AHEAD + EXPERTS))
                nc.tensor.matmul(ps_gate[e % AHEAD][:, :], pick[:, e * P:(e + 1) * P], gates_t[:, p, :],
                                 start=True, stop=True).then_inc(S["gate_ready"], 1)

            def second(g, e, p):
                pe.wait_ge(S["gated_ready"], g * EXPERTS + (e + 2 + EXPERTS))
                if e == 0:
                    pe.wait_ge(S["moe_used"], g + 1)
                    nc.tensor.matmul(ps_moe[:, :], both[:], halves[:, p, :], start=True, stop=False,
                                     skip_group_check=True)
                    for part in (b2_high, b2_low):
                        nc.tensor.matmul(ps_moe[:, :], part[:], gates_t[:, p, :], start=False, stop=False,
                                         skip_group_check=True)
                for h in range(2):
                    mm = nc.tensor.matmul(ps_moe[h * CH:(h + 1) * CH, :], w2[:, e + h, :], gated[:, (e + h) % SLOTS, :],
                                          start=False, stop=(e == EXPERTS - 2), skip_group_check=True)
                mm.then_inc(S["moe_done"], 2)

            def turn_out(g, last=False):
                pe.wait_ge(S["moe_used"], g + 2)
                if last:
                    pe.wait_ge(S["y_ready"], g + 1)
                else:
                    pe.wait_ge(S["c_dve"], (g + 2) * C_OPS + 1)
                for t in range(GROUP):
                    mm = nc.tensor.transpose(ps_misc[:, t * P:(t + 1) * P], moe[:, t * P:(t + 1) * P], eye[:])
                mm.then_inc(S["out_turned"], 1)

            turn_z(0)
            gate_logits(0, 0)
            turn_gates(0)
            for e in range(AHEAD):
                hid(0, e, 0)
                gate(0, e, 0)

            def step(g, p, prep, post):
                for e in range(EXPERTS):
                    if e % 2 == 0:
                        for k in (e + AHEAD, e + AHEAD + 1):
                            if k < EXPERTS:
                                hid(g, k, p)
                                gate(g, k, p)
                            elif prep:
                                hid(g + 1, k - EXPERTS, 1 - p)
                                gate(g + 1, k - EXPERTS, 1 - p)
                    if post and e == PE_AT["out"]:
                        turn_out(g - 1, last=not prep)
                    if prep and e == PE_AT["z"]:
                        turn_z(g + 1)
                    if prep and e == PE_AT["logits"]:
                        gate_logits(g + 1, 1 - p)
                    if prep and e == PE_AT["gates"]:
                        turn_gates(g + 1)
                    if e % 2:
                        second(g, e - 1, p)

            steps(pe, step)
            turn_out(GROUPS - 1, last=True)

        @block.vector
        def _(dve):
            dve.sem_inc(S["gated_ready"], EXPERTS)
            dve.sem_inc(S["y_ready"], 1)
            dve.wait_ge(S["w_in"], W_LOADS)
            nc.vector.tensor_copy(w1_high[:], w1_raw[:]).then_inc(S["w_cast"], 1)
            nc.vector.tensor_copy(gate_high[:], gate_raw[:]).then_inc(S["w_cast"], 1)
            nc.vector.tensor_copy(pick[:], pick_raw[:]).then_inc(S["w_cast"], 1)
            dve.wait_ge(S["w_cast"], 2)
            nc.vector.tensor_tensor(w1_low[:], w1_raw[:], w1_high[:].bitcast(F32), ALU.subtract).then_inc(S["w_cast"], 1)
            nc.vector.tensor_tensor(gate_low[:], gate_raw[:], gate_high[:].bitcast(F32), ALU.subtract).then_inc(S["w_cast"], 1)
            for p in range(2):
                nc.vector.memset(gates_t[:, p, :].bitcast(F32), 0.0).then_inc(S["w_cast"], 1)
            for part in (b2_high, b2_low):
                nc.vector.memset(part[:].bitcast(F32), 0.0).then_inc(S["w_cast"], 1)
            dve.wait_ge(S["w_cast"], 9)
            nc.vector.tensor_copy(b2_high[:, 0:CH], b2_raw[:]).then_inc(S["w_cast"], 1)
            nc.vector.memset(both[:].bitcast(F32), 0.0).then_inc(S["w_cast"], 1)
            dve.wait_ge(S["w_cast"], 11)
            for h in range(2):
                rows = slice(h * CH, (h + 1) * CH)
                nc.vector.tensor_copy(both[rows, 0:CH], eye[rows, rows]).then_inc(S["w_cast"], 1)
            nc.vector.tensor_tensor(b2_low[:, 0:CH], b2_raw[:], b2_high[:, 0:CH].bitcast(F32),
                                    ALU.subtract).then_inc(S["w_cast"], 1)

            def linked(name, base):
                k = [0]

                def link(ins, wait=True):
                    k[0] += 1
                    ins.then_inc(S[name], 1)
                    if wait:
                        dve.wait_ge(S[name], base + k[0])
                return link

            def mean_of(link, n, x):
                link(nc.vector.tensor_reduce(n["sum"][:], x, AX.X, ALU.add))
                link(nc.vector.tensor_scalar(n["mean"][:], n["sum"][:], 1.0 / CH, None, ALU.mult), False)

            def prep_mean(r):
                link = linked("n_dve", r * N_OPS)
                if not (isinstance(r, int) and r == 0):
                    dve.wait_ge(S["z_ready"], r)
                mean_of(link, n1, residual[:, ds(r % GROUPS * GROUP, GROUP), :])

            def prep_var(r):
                dve.wait_ge(S["p_sq"], r + 1)
                link = linked("n_dve", r * N_OPS + 2)
                link(nc.vector.tensor_reduce(n1["ss"][:], n1["sq"][:], AX.X, ALU.add))
                link(nc.vector.tensor_scalar(n1["var"][:], n1["ss"][:], 1.0 / CH, EPS, ALU.mult, ALU.add), False)

            def low_z(r, p):
                dve.wait_ge(S["z_high"], r + 1)
                nc.vector.tensor_tensor(halves[CH:P, p, :], ps_misc[0:CH, :], halves[0:CH, p, :].bitcast(F32),
                                        ALU.subtract).then_inc(S["z_low"], 1)

            def choose(r):
                dve.wait_ge(S["log_ready"], r + 1)
                link = linked("c_dve", r * C_OPS)
                link(nc.vector.tensor_tensor(logits[:], ps_misc[:, 0:GROUP * EXPERTS].rearrange("p (t e) -> p t e", e=EXPERTS),
                                             gate_bias[:].broadcast_to([P, GROUP, EXPERTS]), ALU.add))
                stand_alone(dve, S["dve_passed"])
                for t in range(GROUP):
                    link(nc.vector.max(best[:, t, :], logits[:, t, :]), t == GROUP - 1)
                stand_alone(dve, S["dve_passed"])
                for t in range(GROUP):
                    link(nc.vector.max_index(where[:, t, :], best[:, t, :], logits[:, t, :]), False)
                link(nc.vector.tensor_tensor(gap[:], best[:, :, 1], best[:, :, 0], ALU.subtract))
                link(nc.vector.tensor_copy(where_f[:], where[:, :, 0:2]))
                full = [P, GROUP, EXPERTS]
                for k, to in enumerate((is0, is1)):
                    link(nc.vector.tensor_tensor(to[:], iota[:].broadcast_to(full),
                                                 where_f[:, :, k:k + 1].broadcast_to(full), ALU.is_equal), False)

            def fill_gates(r):
                full = [P, GROUP, EXPERTS]
                dve.wait_ge(S["ratio_ready"], r + 1)
                link = linked("c_dve", r * C_OPS + MASKS)
                link(nc.vector.tensor_scalar(one_up[:], ratio[:], 1.0, None, ALU.add))
                link(nc.vector.reciprocal(weight[:, 0, :], one_up[:]))
                link(nc.vector.tensor_tensor(weight[:, 1, :], weight[:, 0, :], ratio[:], ALU.mult))
                link(nc.vector.tensor_tensor(by0[:], is0[:], weight[:, 0, :].unsqueeze(2).broadcast_to(full), ALU.mult))
                link(nc.vector.tensor_tensor(by1[:], is1[:], weight[:, 1, :].unsqueeze(2).broadcast_to(full), ALU.mult))
                link(nc.vector.tensor_tensor(gates[:], by0[:], by1[:], ALU.add), False)

            def low_gates(r, p):
                dve.wait_ge(S["g_high"], r + 1)
                nc.vector.tensor_tensor(gates_t[32:32 + EXPERTS, p, :], ps_misc[0:EXPERTS, :],
                                        gates_t[0:EXPERTS, p, :].bitcast(F32), ALU.subtract).then_inc(S["g_low"], 1)

            def weigh(g, e):
                dve.wait_ge(S["relu_ready"], g * EXPERTS + (e + 1 + EXPERTS))
                dve.wait_ge(S["gate_ready"], g * EXPERTS + (e + 1))
                if not (isinstance(g, int) and g == 0 and e < SLOTS):
                    dve.wait_ge(S["moe_done"], g * EXPERTS + (e // 2 * 2 + 2 - SLOTS))
                nc.vector.tensor_tensor(gated[:, e % SLOTS, :], hidden[:, e % SLOTS, :], ps_gate[e % AHEAD][:, :],
                                        ALU.mult).then_inc(S["gated_ready"], 1)

            def add_halves(r):
                dve.wait_ge(S["out_turned"], r + 1)
                two = ps_misc[:].rearrange("p (t h c) -> p t c h", t=GROUP, h=2)
                nc.vector.tensor_reduce(y[:], two, AX.X, ALU.add).then_inc(S["y_ready"], 1)

            def post_mean(r):
                dve.wait_ge(S["y_ready"], r + 2)
                link = linked("q_dve", r * Q_OPS)
                mean_of(link, n2, y[:])

            def post_var(r):
                dve.wait_ge(S["q_sq"], r + 1)
                link = linked("q_dve", r * Q_OPS + 2)
                link(nc.vector.tensor_reduce(n2["ss"][:], n2["sq"][:], AX.X, ALU.add))
                link(nc.vector.tensor_scalar(n2["var"][:], n2["ss"][:], 1.0 / CH, EPS, ALU.mult, ALU.add), False)

            for r in range(2):
                prep_mean(r)
                prep_var(r)
            low_z(0, 0)
            choose(0)
            fill_gates(0)
            low_gates(0, 0)

            def step(g, p, prep, post):
                for e in range(EXPERTS):
                    weigh(g, e)
                    if prep and e == DVE_AT["mean"]:
                        prep_mean(g + 2)
                    if post and e == DVE_AT["add"]:
                        add_halves(g - 1)
                        post_mean(g - 1)
                    if prep and e == DVE_AT["var"]:
                        prep_var(g + 2)
                    if post and e == DVE_AT["post_var"]:
                        post_var(g - 1)
                    if prep and e == DVE_AT["z"]:
                        low_z(g + 1, 1 - p)
                    if prep and e == DVE_AT["choose"]:
                        choose(g + 1)
                    if prep and e == DVE_AT["weights"]:
                        fill_gates(g + 1)
                    if prep and e == DVE_AT["gates"]:
                        low_gates(g + 1, 1 - p)

            steps(dve, step)
            add_halves(GROUPS - 1)
            post_mean(GROUPS - 1)
            post_var(GROUPS - 1)


def early_fusion(nc, d, out, dump=None, stages=4):
    with ExitStack() as ctx:
        def sb(name, shape, dt=F32):
            return ctx.enter_context(nc.sbuf_tensor(name, shape, dt))

        residual = sb("residual", [P, ALL_TILES, CH])
        mean = sb("mean", [P, ALL_TILES])
        rstd = sb("rstd", [P, ALL_TILES])
        eye = sb("eye", [P, P])
        tokenise(nc, d, residual, eye)
        statistics(nc, residual, mean, rstd)
        if stages >= 2:
            attend(nc, d, residual, mean, rstd, eye)
        if stages >= 3:
            experts(nc, d, residual, eye, out)
        if dump is not None:
            with nc.semaphore("dumped") as dumped, nc.Block() as block:
                @block.sync
                def _(sp):
                    sp.dma_start(dump["h"], residual[:].rearrange("p t c -> p (t c)")).then_inc(dumped, 16)
                    sp.dma_start(dump["m"], mean[:]).then_inc(dumped, 16)
                    sp.dma_start(dump["r"], rstd[:]).then_inc(dumped, 16)
                    sp.wait_ge(dumped, 48)


def kernel(**inputs):
    import concourse.bacc as _bacc
    from concourse.bass_utils import run_bass_kernel_spmd as _run

    nc = _bacc.Bacc("TRN2", target_bir_lowering=False, num_devices=1)
    arrays, d = {}, {}
    for name, a in {**inputs, **constants()}.items():
        a = np.ascontiguousarray(a)
        arrays[f"in_{name}"] = a
        d[name] = nc.dram_tensor(f"in_{name}", a.shape, mybir.dt.from_np(a.dtype), kind="ExternalInput").ap()
    out = nc.dram_tensor("out_0", (BATCH, SEQ, CH), F32, kind="ExternalOutput").ap()
    early_fusion(nc, d, out)
    r = _run(nc, [arrays], core_ids=[0])
    return r.results[0]["out_0"]
```

```python
from contextlib import ExitStack

import concourse.bass as bass
import numpy as np
from concourse import mybir

F32 = mybir.dt.float32
F32R = mybir.dt.float32r
U32 = mybir.dt.uint32
ALU = mybir.AluOpType
ACT = mybir.ActivationFunctionType
AX = mybir.AxisListType

P = 128
BATCH, SIDE, CH = 8, 64, 64
IMAGE = SIDE * SIDE
TEXT = 128
SEQ = IMAGE + TEXT
TILES = SEQ // P
IMAGE_TILES = IMAGE // P
ALL_TILES = BATCH * TILES
EXPERTS, HIDDEN = 16, 128
EPS = 1e-5
PERIODS = (24.0, 720.0)
PAD = SIDE + 2
BANK = 512
ds = bass.ds

CHUNK_TILES = 3
CHUNK = CHUNK_TILES * P
CHUNKS = TILES // CHUNK_TILES
STEPS = BATCH * CHUNKS
UNITS = (TILES + 1) // 2
BIAS_ROWS = 2 * len(PERIODS)
EXTRA = 32 + BIAS_ROWS
P_SLOTS = 5
WHOLE, REST = divmod(SEQ, BANK)
MAXES = CHUNK_TILES * WHOLE + 1


def round12(x):
    bits = x.view(np.uint32).astype(np.uint64)
    half = np.uint64((1 << 11) - 1) + ((bits >> np.uint64(12)) & np.uint64(1))
    return ((bits + half) >> np.uint64(12) << np.uint64(12)).astype(np.uint32).view(np.float32)


def constants():
    s = np.arange(SEQ, dtype=np.float64)
    waves = []
    for period in PERIODS:
        waves += [np.cos(2 * np.pi * s / period), np.sin(2 * np.pi * s / period)]
    waves = np.stack(waves)
    high = round12(waves.astype(np.float32))
    low = waves.astype(np.float32) - high
    n = BIAS_ROWS
    waves_k, waves_q = np.zeros((2, EXTRA, SEQ), np.float32)
    waves_k[0] = waves_q[0] = 1
    for k, part in enumerate((high, low)):
        waves_k[1 + k * n:1 + (k + 1) * n] = waves
        waves_q[1 + k * n:1 + (k + 1) * n] = part
    waves_k[32:], waves_q[32:] = waves, high
    ones_col = np.zeros((P, 1), np.float32)
    ones_col[CH - 1] = ones_col[2 * CH - 1] = 1
    eye = np.eye(P, dtype=np.float32)
    pick = np.zeros((48, EXPERTS, P), np.float32)
    for e in range(EXPERTS):
        pick[e, e] = pick[32 + e, e] = 1
    iota = np.broadcast_to(np.arange(EXPERTS, dtype=np.float32), (P, EXPERTS)).copy()
    return {"ones": np.ones(P, np.float32), "waves_k": waves_k, "waves_q": waves_q, "sum_col": ones_col, "eye": eye,
            "pick": pick.reshape(48, EXPERTS * P), "iota": iota}


def col(ap):
    return ap.rearrange("(p a) -> p a", a=1)


def stand_alone(eng, passed):
    eng.sem_inc(passed, 1)


def tokenise(nc, d, weights, residual, mean, rstd, eye):
    PAIRS = BATCH // 2
    GROUP = 4
    GROUPS = IMAGE_TILES // GROUP
    ROWS = GROUP * P // SIDE
    PARTS = 4
    PART = IMAGE // PARTS
    QUARTERS = 4
    with ExitStack() as ctx:
        def sb(name, shape, dt=F32):
            return ctx.enter_context(nc.sbuf_tensor(name, shape, dt))

        def sem(name):
            return ctx.enter_context(nc.semaphore(name))

        tokens = sb("tokens", [P, 2, IMAGE_TILES, 2, CH])
        padded = sb("padded", [P, 2, PAD, PAD])
        conv = sb("conv", [P, 2, IMAGE])
        lin_rows = sb("lin_rows", [CH, CH])
        lin_both = sb("lin_both", [P, P])
        lin_bias = sb("lin_bias", [P, 2, CH])
        taps = sb("taps", [P, 9])
        vec = sb("vec", [P, 5])
        bn = sb("bn", [P, 4])
        shift = sb("shift", [P, 1])
        scale = sb("scale", [P, 1])
        ps_t = [ctx.enter_context(nc.psum_tensor(f"ps_t{i}", [P, BANK], F32)) for i in range(2)]
        ps_l = [ctx.enter_context(nc.psum_tensor(f"ps_l{i}", [P, BANK], F32)) for i in range(2)]
        ps_w = ctx.enter_context(nc.psum_tensor("ps_w", [P, BANK], F32))

        par_in, eye_in, text_in, bias_in = sem("par_in"), sem("eye_in"), sem("text_in"), sem("bias_in")
        x_in = [sem("x_in0"), sem("x_in1")]
        first_in = [sem(f"first_in{k}") for k in range(QUARTERS)]
        zeroed, bn_a, bn_b, bn_c = sem("zeroed"), sem("bn_a"), sem("bn_b"), sem("bn_c")
        lin_t, lin_c = sem("lin_t"), sem("lin_c")
        turned, padded_ready, conv_step = sem("turned"), sem("padded_ready"), sem("conv_step")
        lin_ready, lin_used = sem("lin_ready"), sem("lin_used")

        total = sb("total", [P, TILES])
        centred = sb("centred", [P, TILES, CH])
        squared = sb("squared", [P, TILES, CH])
        squares = sb("squares", [P, TILES])
        variance = sb("variance", [P, TILES])
        deviation = sb("deviation", [P, TILES])
        s_sum, s_mean, s_cent, s_sq, s_ss, s_var, s_dev = (
            sem(n) for n in ("s_sum", "s_mean", "s_cent", "s_sq", "s_ss", "s_var", "s_dev"))
        first = slice(0, TILES)

        block = ctx.enter_context(nc.Block())

        def parameters(eng, half):
            rows = slice(half * CH, half * CH + CH)
            for i, name in enumerate(["bn_gamma", "bn_beta", "bn_mean", "bn_var", "conv_b"]):
                eng.dma_start(vec[rows, i:i + 1], col(d["L0_tok_" + name])).then_inc(par_in, 16)
            eng.dma_start(taps[rows, :], d["L0_tok_conv_w"].rearrange("c a h w -> c (a h w)")).then_inc(par_in, 16)

        @block.sync
        def _(sp):
            sp.dma_start(lin_rows[:], d["L0_tok_lin_w"]).then_inc(par_in, 16)
            sp.dma_start(eye[:], d["eye"]).then_inc(eye_in, 16)
            parameters(sp, 1)
            for k in range(QUARTERS):
                tiles = slice(k * IMAGE_TILES // QUARTERS, (k + 1) * IMAGE_TILES // QUARTERS)
                for i in range(2):
                    src = d["x"][i].rearrange("(t r) w c -> (r w) t c", r=P // SIDE)
                    sp.dma_start(tokens[:, 0, tiles, i, :], src[:, tiles]).then_inc(first_in[k], 16)
            for q in range(1, PAIRS):
                if q >= 2:
                    sp.wait_ge(turned, (q - 1) * GROUPS)
                for i in range(2):
                    src = d["x"][2 * q + i].rearrange("(t r) w c -> (r w) t c", r=P // SIDE)
                    sp.dma_start(tokens[:, q % 2, :, i, :], src).then_inc(x_in[q % 2], 16)
                if q == 1:
                    for half in range(2):
                        sp.dma_start(lin_bias[:, half, :], d["L0_tok_lin_b"].partition_broadcast(P)).then_inc(bias_in, 16)
                    for b in range(BATCH):
                        sp.dma_start(residual[:, b * TILES + IMAGE_TILES, :], d["txt"][b]).then_inc(text_in, 16)
                    weights.load(sp, d)

        PARAMS = 16 * 13

        @block.gpsimd
        def _(pool):
            nc.gpsimd.memset(padded[:, 0], 0.0).then_inc(zeroed, 1)
            nc.gpsimd.memset(padded[:, 1], 0.0).then_inc(zeroed, 1)
            pool.wait_ge(s_mean, 1)
            nc.gpsimd.tensor_tensor(centred[:], residual[:, first, :],
                                    mean[:, first].unsqueeze(2).broadcast_to([P, TILES, CH]),
                                    ALU.subtract).then_inc(s_cent, 1)
            pool.wait_ge(s_cent, 1)
            nc.gpsimd.tensor_tensor(squared[:], centred[:], centred[:], ALU.mult).then_inc(s_sq, 1)

        @block.scalar
        def _(act):
            parameters(act, 0)
            act.wait_ge(bn_a, 1)
            nc.scalar.activation(bn[:, 1:2], bn[:, 0:1], ACT.Sqrt).then_inc(bn_b, 1)
            act.wait_ge(bn_c, 3)
            act.wait_ge(zeroed, 2)
            for q in range(PAIRS):
                for g in range(GROUPS):
                    k = q * GROUPS + g
                    act.wait_ge(turned, k + 1)
                    if g == 0 and q >= 2:
                        act.wait_ge(conv_step, (q - 1) * PARTS * 9)
                    nc.scalar.activation(
                        padded[:, q % 2, 1 + g * ROWS:1 + (g + 1) * ROWS, 1:1 + SIDE],
                        ps_t[k % 2][:, :].rearrange("p (r w) -> p r w", w=SIDE),
                        ACT.Identity, bias=shift[:, 0:1], scale=scale[:, 0:1]).then_inc(padded_ready, 1)
            act.wait_ge(s_var, 1)
            nc.scalar.activation(deviation[:], variance[:], ACT.Sqrt).then_inc(s_dev, 1)

        @block.tensor
        def _(pe):
            pe.wait_ge(eye_in, 16)
            pe.wait_ge(par_in, PARAMS)
            nc.tensor.transpose(ps_w[0:CH, 0:CH], lin_rows[:], eye[0:CH, 0:CH]).then_inc(lin_t, 1)

            def turn(q):
                if q:
                    pe.wait_ge(x_in[q % 2], 32 * ((q + 1) // 2))
                for g in range(GROUPS):
                    if q == 0 and g % (GROUPS // QUARTERS) == 0:
                        pe.wait_ge(first_in[g * QUARTERS // GROUPS], 32)
                    k = q * GROUPS + g
                    if k >= 2:
                        pe.wait_ge(padded_ready, k - 1)
                    for j in range(GROUP):
                        mm = nc.tensor.transpose(ps_t[k % 2][:, j * P:(j + 1) * P],
                                                 tokens[:, q % 2, g * GROUP + j, :, :], eye[:])
                    mm.then_inc(turned, 1)

            def linear(q):
                for g in range(GROUPS):
                    k = q * GROUPS + g
                    part = g * PARTS // GROUPS
                    pe.wait_ge(conv_step, (q * PARTS + part // 2 * 2) * 9 + 17 + part % 2)
                    if k >= 2:
                        pe.wait_ge(lin_used, k - 1)
                    for j in range(GROUP):
                        t = g * GROUP + j
                        mm = nc.tensor.matmul(ps_l[k % 2][:, j * P:(j + 1) * P],
                                              conv[:, q % 2, t * P:(t + 1) * P], lin_both[:],
                                              start=True, stop=True)
                    mm.then_inc(lin_ready, 1)

            turn(0)
            pe.wait_ge(lin_c, 3)
            for q in range(PAIRS):
                if q + 1 < PAIRS:
                    turn(q + 1)
                linear(q)

        @block.vector
        def _(dve):
            dve.wait_ge(par_in, PARAMS)
            nc.vector.tensor_scalar(bn[:, 0:1], vec[:, 3:4], EPS, None, ALU.add).then_inc(bn_a, 1)
            nc.vector.memset(lin_both[:], 0.0).then_inc(lin_c, 1)
            dve.wait_ge(lin_t, 1)
            dve.wait_ge(lin_c, 1)
            for h in range(2):
                nc.vector.tensor_copy(lin_both[h * CH:h * CH + CH, h * CH:h * CH + CH],
                                      ps_w[0:CH, 0:CH]).then_inc(lin_c, 1)
            dve.wait_ge(bn_b, 1)
            nc.vector.reciprocal(bn[:, 2:3], bn[:, 1:2]).then_inc(bn_c, 1)
            dve.wait_ge(bn_c, 1)
            nc.vector.tensor_tensor(scale[:], bn[:, 2:3], vec[:, 0:1], ALU.mult).then_inc(bn_c, 1)
            dve.wait_ge(bn_c, 2)
            nc.vector.scalar_tensor_tensor(out=bn[:, 3:4], in0=vec[:, 2:3], scalar=scale[:, 0:1],
                                           in1=vec[:, 1:2], op0=ALU.mult, op1=ALU.subtract).then_inc(bn_a, 1)
            dve.wait_ge(bn_a, 2)
            nc.vector.tensor_scalar(shift[:], bn[:, 3:4], -1.0, None, ALU.mult).then_inc(bn_c, 1)

            taken = [0]

            def convolve(q, parts):
                for k in range(9):
                    for part in parts:
                        r0 = part * SIDE // PARTS
                        n = SIDE // PARTS
                        acc = conv[:, q % 2, part * PART:(part + 1) * PART].rearrange("p (r w) -> p r w", w=SIDE)
                        window = padded[:, q % 2, r0 + k // 3:r0 + k // 3 + n, k % 3:k % 3 + SIDE]
                        if k == 0:
                            dve.wait_ge(padded_ready, q * GROUPS + min(GROUPS, (r0 + n) // ROWS + 1))
                            if q >= 2 and part == 0:
                                dve.wait_ge(lin_ready, (q - 1) * GROUPS)
                            ins = nc.vector.tensor_scalar(acc, window, taps[:, 0:1], vec[:, 4:5], ALU.mult, ALU.add)
                        else:
                            dve.wait_ge(conv_step, taken[0] - 1)
                            ins = nc.vector.scalar_tensor_tensor(out=acc, in0=window, scalar=taps[:, k:k + 1],
                                                                 in1=acc, op0=ALU.mult, op1=ALU.add)
                        taken[0] += 1
                        ins.then_inc(conv_step, 1)

            def store(q, g):
                k = q * GROUPS + g
                dve.wait_ge(lin_ready, k + 1)
                if k == 0:
                    dve.wait_ge(bias_in, 32)
                for i in range(2):
                    t0 = (2 * q + i) * TILES + g * GROUP
                    ins = nc.vector.tensor_tensor(
                        residual[:, t0:t0 + GROUP, :],
                        ps_l[k % 2][:, :].rearrange("p (t i c) -> p i t c", t=GROUP, i=2)[:, i],
                        lin_bias[:, i:i + 1, :].broadcast_to([P, GROUP, CH]), ALU.add)
                ins.then_inc(lin_used, 1)

            for q in range(PAIRS):
                convolve(q, (0, 1))
                if q:
                    for g in range(GROUPS // 2, GROUPS):
                        store(q - 1, g)
                convolve(q, (2, 3))
                for g in range(GROUPS // 2):
                    store(q, g)
                if q == PAIRS - 1:
                    for g in range(GROUPS // 2, GROUPS):
                        store(q, g)
                if q == 1:
                    dve.wait_ge(lin_used, GROUPS)
                    dve.wait_ge(text_in, 16 * BATCH)
                    nc.vector.tensor_reduce(total[:], residual[:, first, :], AX.X, ALU.add).then_inc(s_sum, 1)
                    dve.wait_ge(s_sum, 1)
                    nc.vector.tensor_scalar(mean[:, first], total[:], 1.0 / CH, None, ALU.mult).then_inc(s_mean, 1)
                if q == 2:
                    dve.wait_ge(s_sq, 1)
                    nc.vector.tensor_reduce(squares[:], squared[:], AX.X, ALU.add).then_inc(s_ss, 1)
                    dve.wait_ge(s_ss, 1)
                    nc.vector.tensor_scalar(variance[:], squares[:], 1.0 / CH, EPS, ALU.mult, ALU.add).then_inc(s_var, 1)
            dve.wait_ge(s_dev, 1)
            nc.vector.reciprocal(rstd[:, first], deviation[:])


class AttentionWeights:

    def __init__(self, nc, ctx):
        def sb(name, shape):
            return ctx.enter_context(nc.sbuf_tensor(name, shape, F32))

        self.wq2 = sb("wq2", [CH, 2, CH])
        self.wkb = sb("wkb", [CH, CH + 1])
        self.bq = sb("bq", [CH, 1])
        self.wv = sb("wv", [CH, CH])
        self.wvd = sb("wvd", [CH, 2, CH])
        self.w_value = sb("w_value", [P, CH + 1])
        self.beta_col = sb("beta_col", [P, 1])
        self.loaded = ctx.enter_context(nc.semaphore("weights_loaded"))
        self.ones_in = ctx.enter_context(nc.semaphore("ones_in"))

    LOADS = 16 * (9 + 3 * len(PERIODS))

    def load(self, sp, d):
        sp.dma_start(self.beta_col[CH:CH + EXTRA, :], col(d["ones"])[0:EXTRA]).then_inc(self.ones_in, 16)
        sp.dma_start(self.wq2[:, 0, :], d["L0_attn_Wq"]).then_inc(self.loaded, 16)
        sp.dma_start(self.wq2[:, 1, :], d["L0_attn_Wq"]).then_inc(self.loaded, 16)
        sp.dma_start(self.wkb[:, 0:CH], d["L0_attn_Wk"]).then_inc(self.loaded, 16)
        sp.dma_start(self.wkb[:, CH:CH + 1], col(d["L0_attn_bk"])).then_inc(self.loaded, 16)
        sp.dma_start(self.bq[:], col(d["L0_attn_bq"])).then_inc(self.loaded, 16)
        sp.dma_start(self.wv[:], d["L0_attn_Wv"]).then_inc(self.loaded, 16)
        sp.dma_start(self.wvd[:, 0, CH - 1:CH], col(d["L0_attn_bv"])).then_inc(self.loaded, 16)
        sp.dma_start(self.wvd[:, 1, CH - 1:CH], col(d["L0_attn_bv"])).then_inc(self.loaded, 16)
        sp.dma_start(self.w_value[:, CH:CH + 1], d["sum_col"]).then_inc(self.loaded, 16)
        sp.wait_ge(self.ones_in, 16)
        for first in (1, 1 + BIAS_ROWS, 32):
            for w in range(len(PERIODS)):
                at = CH + first + 2 * w
                sp.dma_start(self.beta_col[at:at + 2, :],
                             d["L0_attn_beta"][w:w + 1].partition_broadcast(2)).then_inc(self.loaded, 16)
        sp.wait_ge(self.loaded, self.LOADS)


def attend(nc, d, weights, residual, mean, rstd, eye):
    with ExitStack() as ctx:
        def sb(name, shape, dt=F32):
            return ctx.enter_context(nc.sbuf_tensor(name, shape, dt))

        def sem(name):
            return ctx.enter_context(nc.semaphore(name))

        def psum(name, shape):
            return ctx.enter_context(nc.psum_tensor(name, shape, F32))

        keys1 = sb("keys1", [P, 2 * SEQ], F32R)
        keys2 = sb("keys2", [P, 2 * SEQ], F32R)
        values = sb("values", [P, 2, TILES, CH])
        waves_q = sb("waves_q", [P, SEQ])
        next_q = sb("next_q", [P, CHUNK], F32R)
        query1 = sb("query1", [P, 2 * CHUNK], F32R)
        query2 = sb("query2", [P, 2 * CHUNK], F32R)
        normed = sb("normed", [P, 2, CHUNK_TILES, CH])
        centred = sb("centred_x", [P, CHUNK_TILES, CH])
        probs = sb("probs", [P, P_SLOTS, 2, CHUNK])
        summed = sb("summed", [P, CHUNK])
        maxima = sb("maxima", [P, CHUNK_TILES, WHOLE + 1])
        maximum = sb("maximum", [P, CHUNK_TILES])
        recip = sb("recip", [P, CHUNK_TILES])
        update = sb("update", [P, CHUNK_TILES, CH])
        wq2, wkb, bq, wv, wvd = weights.wq2, weights.wkb, weights.bq, weights.wv, weights.wvd
        w_value, beta_col = weights.w_value, weights.beta_col
        w_query = sb("w_query", [P, CH + 1])
        b_query = sb("b_query", [CH + 1, 1])
        total = sb("total_x", [P, CHUNK_TILES])
        squared = sb("squared_x", [P, CHUNK_TILES, CH])
        squares = sb("squares_x", [P, CHUNK_TILES])
        variance = sb("variance_x", [P, CHUNK_TILES])
        half = sb("half_x", [P, CHUNK_TILES])

        scores = [psum(f"scores{i}", [P, 2, BANK]) for i in range(2)]
        turned = psum("turned", [P, 2, BANK])
        misc, acc = turned[:, 0], turned[:, 1]
        tops = [psum(f"tops{i}", [P, BANK]) for i in range(2)]

        names = ("pe_passed", "act_passed", "pool_passed", "dve_passed", "wave_in", "wave_high", "set_a", "set_b", "set_c",
                 "set_w", "w_mm", "m_sum", "m_mean", "m_sq", "m_ss", "m_var", "m_pow", "m_set",
                 "x_centred", "x_ready", "v_ready", "ext_ready", "q_copied",
                 "t_ready", "t_high", "t_used", "g_ready", "g_high", "g_used",
                 "top_done", "top_used", "max_done", "row_mm", "row_used",
                 "s_done", "p_done", "pv_done", "acc_used", "o_ready", "o_used", "o_mul", "o_rec")
        S = {n: sem(n) for n in names}
        block = ctx.enter_context(nc.Block())

        E0, E1 = CH, CH + EXTRA

        def steps(eng, step):
            with eng.Fori(0, BATCH // 2 - 1) as i:
                for p in range(2):
                    n0 = i * (2 * CHUNKS) + p * CHUNKS
                    with eng.Fori(0, CHUNKS - 1) as c:
                        step(n0 + c, p, c, (p, c + 1), True)
                    step(n0 + (CHUNKS - 1), p, CHUNKS - 1, (1 - p, 0), True)
            for p in range(2):
                n0 = (BATCH - 2 + p) * CHUNKS
                with eng.Fori(0, CHUNKS - 1) as c:
                    step(n0 + c, p, c, (p, c + 1), p == 0)
                step(n0 + CHUNKS - 1, p, CHUNKS - 1, (1, 0) if p == 0 else None, p == 0)

        def unit_count(n, u):
            return n * UNITS + (u + 1 + UNITS)

        def before_unit(n, u, slot):
            others = [v for v in range(UNITS) if slot(v) == slot(u)]
            at = others.index(u)
            if at:
                return unit_count(n, others[at - 1])
            return n * UNITS + (others[-1] + 1)

        def score_slot(u):
            return u % 2

        def prob_slot(u):
            return u % (P_SLOTS - 1) if u < UNITS - 1 else P_SLOTS - 1

        def first_batch(eng, chunk):
            with eng.Fori(0, CHUNKS // 2) as i:
                for slot in range(2):
                    chunk(i * 2 + slot, slot)
            chunk(CHUNKS - 1, 0)

        def tiles_of(u):
            return [t for t in (2 * u, 2 * u + 1) if t < TILES]

        PAIRS = [(u, u + 1) for u in range(0, UNITS - 1, 2)] + [(UNITS - 1,)]
        QUERIES_AT, TURN_AT, ROW_AT = 0, 3, len(PAIRS) - 2
        TOPS_IN = [0, 4, 5, 4, 4, 4, 4, 0, 0]
        assert sum(TOPS_IN) == MAXES and len(TOPS_IN) == len(PAIRS)

        def tops_at(i):
            first = sum(TOPS_IN[:i])
            places = (0, 1, 2, 4, 4) if TOPS_IN[i] == 5 else (0, 1, 3, 4)
            return {first + k: places[k] for k in range(TOPS_IN[i])}

        EARLY = 4
        SQUARES_AFTER = sum(TOPS_IN[:TURN_AT]) - 1
        T_LOW_AFTER = sum(TOPS_IN[:TURN_AT + 1]) - 1
        assert SQUARES_AFTER < T_LOW_AFTER

        @block.sync
        def _(sp):
            sp.dma_start(waves_q[0:EXTRA, :], d["waves_k"]).then_inc(S["wave_in"], 16)
            sp.dma_start(waves_q[E0:E1, :], d["waves_q"]).then_inc(S["wave_in"], 16)

        @block.gpsimd
        def _(pool):
            def whole(stat):
                return stat.unsqueeze(2).broadcast_to([P, CHUNK_TILES, CH])

            def centre(j):
                stat = ds(j * CHUNK_TILES, CHUNK_TILES)
                nc.gpsimd.tensor_tensor(centred[:], residual[:, stat, :], whole(mean[:, stat]),
                                        ALU.subtract).then_inc(S["x_centred"], 1)
                pool.wait_ge(S["x_centred"], j + 1)

            def square():
                nc.gpsimd.tensor_tensor(squared[:], centred[:], centred[:], ALU.mult).then_inc(S["m_sq"], 1)

            def scale(j, slot=0, before=1):
                pool.wait_ge(S["t_ready"], j + 3 - before)
                stand_alone(pool, S["pool_passed"])
                nc.gpsimd.tensor_tensor(normed[:, slot], centred[:], whole(rstd[:, ds(j * CHUNK_TILES, CHUNK_TILES)]),
                                        ALU.mult).then_inc(S["x_ready"], 1)
                pool.wait_ge(S["x_ready"], j + 2)

            def copy_values(j, p, c):
                stand_alone(pool, S["pool_passed"])
                nc.gpsimd.tensor_copy(values[:, p, ds(c * CHUNK_TILES, CHUNK_TILES), 0:CH - 1],
                                      normed[:, 0, :, 0:CH - 1]).then_inc(S["v_ready"], 1)

            def next_extra_rows(r, c, prepared):
                pool.wait_ge(S["v_ready"], prepared + 2)
                pool.wait_ge(S["row_used"], r + 1)
                stand_alone(pool, S["pool_passed"])
                nc.gpsimd.tensor_copy(next_q[E0:E1, :], waves_q[E0:E1, ds(c * CHUNK, CHUNK)]).then_inc(S["ext_ready"], 1)
                pool.wait_ge(S["ext_ready"], 2 * r + 1)

            def extra_rows(r, c):
                nc.gpsimd.tensor_copy(query1[E0:E1, ds((r % 2) * CHUNK, CHUNK)],
                                      waves_q[E0:E1, ds(c * CHUNK, CHUNK)]).then_inc(S["ext_ready"], 1)

            def high_rows(r):
                pool.wait_ge(S["ext_ready"], 2 * r + 2)
                pool.wait_ge(S["g_high"], r + 1)
                stand_alone(pool, S["pool_passed"])
                for to in (query1, query2):
                    nc.gpsimd.tensor_copy(to[0:CH, ds((r % 2) * CHUNK, CHUNK)],
                                          next_q[0:CH, :]).then_inc(S["q_copied"], 1)

            pool.sem_inc(S["x_ready"], 1)
            pool.sem_inc(S["v_ready"], 2)
            nc.gpsimd.memset(half[:], -0.5).then_inc(S["m_set"], 1)
            nc.gpsimd.memset(values[:, :, :, CH - 1:CH], 1.0)

            def chunk(j, slot):
                centre(j)
                pool.wait_ge(S["v_ready"], j + 1)
                scale(j, slot, before=2)

            first_batch(pool, chunk)
            pool.wait_ge(S["wave_in"], 32)
            pool.wait_ge(S["m_set"], 1)
            next_extra_rows(0, 0, CHUNKS)
            extra_rows(0, 0)
            high_rows(0)

            def step(n, p, c, nxt, prep):
                if nxt:
                    next_extra_rows(n + 1, nxt[1], n + CHUNKS if prep else STEPS)
                if prep:
                    pool.wait_ge(S["m_mean"], n + 1)
                    stand_alone(pool, S["pool_passed"])
                    centre(n + CHUNKS)
                    square()
                    pool.wait_ge(S["m_sq"], n + 1)
                if nxt:
                    pool.wait_ge(S["pv_done"], n * UNITS + UNITS)
                    stand_alone(pool, S["pool_passed"])
                    extra_rows(n + 1, nxt[1])
                    high_rows(n + 1)
                if prep:
                    pool.wait_ge(S["q_copied"], 2 * n + 4)
                    pool.wait_ge(S["m_var"], n + 1)
                    stand_alone(pool, S["pool_passed"])
                    nc.gpsimd.tensor_tensor(rstd[:, ds((n + CHUNKS) * CHUNK_TILES, CHUNK_TILES)], variance[:], half[:],
                                            ALU.pow).then_inc(S["m_pow"], 1)
                    pool.wait_ge(S["m_pow"], n + 1)
                    scale(n + CHUNKS)
                    copy_values(n + CHUNKS, 1 - p, c)

            steps(pool, step)

        @block.scalar
        def _(act):
            def keys_high(j, p, c, slot=0):
                act.wait_ge(S["t_ready"], j + 3)
                at = ds(p * SEQ + c * CHUNK, CHUNK)
                nc.scalar.activation(keys1[0:CH, at], turned[0:CH, slot, 0:CHUNK], ACT.Identity).then_inc(S["t_high"], 1)
                nc.scalar.activation(keys2[CH:P, at], turned[0:CH, slot, 0:CHUNK], ACT.Identity).then_inc(S["t_high"], 1)

            def query_high(r):
                act.wait_ge(S["g_ready"], r + 1)
                act.wait_ge(S["ext_ready"], 2 * r + 1)
                nc.scalar.activation(next_q[0:CH + 1, :], misc[0:CH + 1, 0:CHUNK], ACT.Identity,
                                     bias=b_query[:, 0:1]).then_inc(S["g_high"], 1)

            def exponential(n, u):
                act.wait_ge(S["s_done"], n * UNITS + (u + 1))
                act.wait_ge(S["pv_done"], before_unit(n, u, prob_slot))
                k = len(tiles_of(u))
                nc.scalar.activation(probs[:, prob_slot(u), 0:k, :], scores[score_slot(u)][:, 0:k, 0:CHUNK],
                                     ACT.Exp).then_inc(S["p_done"], 1)

            def take_sums(n):
                act.wait_ge(S["pv_done"], unit_count(n, UNITS - 1))
                nc.scalar.activation(summed[:], acc[:, 0:CHUNK], ACT.Identity).then_inc(S["acc_used"], 1)

            act.wait_ge(S["wave_in"], 32)
            nc.scalar.activation(keys1[E0:E1, 0:SEQ], waves_q[0:EXTRA, :], ACT.Identity,
                                 scale=beta_col[E0:E1, 0:1]).then_inc(S["wave_high"], 1)
            act.wait_ge(S["set_b"], 3)

            def chunk(j, slot):
                act.wait_ge(S["x_ready"], j + 2)
                stand_alone(act, S["act_passed"])
                nc.scalar.activation(values[:, 0, ds(j * CHUNK_TILES, CHUNK_TILES), 0:CH - 1], normed[:, slot, :, 0:CH - 1],
                                     ACT.Identity).then_inc(S["v_ready"], 1)
                keys_high(j, 0, j, slot)

            first_batch(act, chunk)
            query_high(0)
            act.wait_ge(S["set_w"], 1)
            nc.scalar.activation(keys1[E0:E1, SEQ:], keys1[E0:E1, 0:SEQ].bitcast(F32), ACT.Identity).then_inc(S["set_c"], 1)
            for u in range(2):
                exponential(0, u)

            def step(n, p, c, nxt, prep):
                for u in range(2, UNITS):
                    exponential(n, u)
                    if u == 2 * QUERIES_AT + 3 and nxt:
                        query_high(n + 1)
                    if u == 2 * TURN_AT + 3 and prep:
                        keys_high(n + CHUNKS, 1 - p, c)
                if nxt:
                    exponential(n + 1, 0)
                    exponential(n + 1, 1)
                take_sums(n)

            steps(act, step)

        @block.tensor
        def _(pe):
            pe.sem_inc(S["t_ready"], 2)
            pe.sem_inc(S["pv_done"], UNITS)

            nc.tensor.matmul(misc[:, 0:CH + 1], wq2[:].rearrange("e a j -> e (a j)"), wkb[:],
                             start=True, stop=True).then_inc(S["w_mm"], 1)
            nc.tensor.matmul(tops[0][0:CH + 1, 0:1], wkb[:], bq[:], start=True, stop=True).then_inc(S["w_mm"], 1)
            pe.wait_ge(S["set_a"], 2)
            nc.tensor.matmul(tops[1][:, 0:CH], wvd[:].rearrange("e a j -> e (a j)"), eye[0:CH, 0:CH],
                             start=True, stop=True).then_inc(S["w_mm"], 1)

            def turn(j, slot=0):
                pe.wait_ge(S["x_ready"], j + 2)
                stand_alone(pe, S["pe_passed"])
                for t in range(CHUNK_TILES):
                    mm = nc.tensor.transpose(turned[0:CH, slot, t * P:(t + 1) * P], normed[:, slot, t, :], eye[:])
                mm.then_inc(S["t_ready"], 1)

            def queries(r, p, c):
                nc.tensor.matmul(misc[0:CH + 1, 0:CHUNK], w_query[:],
                                 keys2[:, ds(p * SEQ + c * CHUNK, CHUNK)].bitcast(F32),
                                 start=True, stop=True).then_inc(S["g_ready"], 1)

            def top(r, k, p):
                if k >= 2:
                    pe.wait_ge(S["top_used"], r * MAXES + (k - 1))
                whole = k < WHOLE * CHUNK_TILES
                for t in ([k % CHUNK_TILES] if whole else range(CHUNK_TILES)):
                    a, n, to = (k // CHUNK_TILES * BANK, BANK, 0) if whole else (WHOLE * BANK, REST, t * REST)
                    mm = nc.tensor.matmul(tops[k % 2][:, to:to + n], next_q[0:E1, t * P:(t + 1) * P],
                                          keys1[0:E1, p * SEQ + a:p * SEQ + a + n], start=True, stop=True)
                mm.then_inc(S["top_done"], 1)

            def next_tops(n, ks, nxt, prep):
                for k in ks if nxt else ():
                    if k == 0:
                        pe.wait_ge(S["g_high"], n + 2)
                        pe.wait_ge(S["o_used"], n + 1)
                    if k == 1:
                        pe.wait_ge(S["row_used"], n + 2)
                    if prep and k == (WHOLE - 1) * CHUNK_TILES:
                        pe.wait_ge(S["t_high"], (n + CHUNKS) * 2 + 2)
                    top(n + 1, k, nxt[0])

            def row(r):
                pe.wait_ge(S["max_done"], r + 1)
                for t in range(CHUNK_TILES):
                    mm = nc.tensor.matmul(tops[1][0:1, t * P:(t + 1) * P], maximum[:, t:t + 1], eye[:],
                                          start=True, stop=True)
                mm.then_inc(S["row_mm"], 1)

            def score(n, u, p, only=None):
                tiles = tiles_of(u)
                at = ds((n % 2) * CHUNK, CHUNK)
                for i, t in enumerate(tiles):
                    if only is not None and i != only:
                        continue
                    if i == 0:
                        if u < 2:
                            pe.wait_ge(S["row_used"], n + 2)
                            pe.wait_ge(S["q_copied"], 2 * n + 2)
                            pe.wait_ge(S["g_used"], n + 1)
                        pe.wait_ge(S["p_done"], before_unit(n, u, score_slot))
                    cols = slice(p * SEQ + t * P, p * SEQ + (t + 1) * P)
                    nc.tensor.matmul(scores[score_slot(u)][:, i, 0:CHUNK], keys1[0:E1, cols], query1[0:E1, at],
                                     start=True, stop=False)
                    mm = nc.tensor.matmul(scores[score_slot(u)][:, i, 0:CHUNK], keys2[:, cols], query2[:, at],
                                          start=False, stop=True)
                    if i == len(tiles) - 1:
                        mm.then_inc(S["s_done"], 1)

            def weigh(n, u, p):
                pe.wait_ge(S["p_done"], unit_count(n, u))
                if u == 0:
                    pe.wait_ge(S["acc_used"], n + 1)
                for i, t in enumerate(tiles_of(u)):
                    mm = nc.tensor.matmul(acc[i * CH:(i + 1) * CH, 0:CHUNK], values[:, p, t, :],
                                          probs[:, prob_slot(u), i, :],
                                          start=(u == 0), stop=(t >= TILES - 2))
                mm.then_inc(S["pv_done"], 1)

            def project(n):
                pe.wait_ge(S["acc_used"], n + 2)
                pe.wait_ge(S["o_used"], n + 1)
                for t in range(CHUNK_TILES):
                    mm = nc.tensor.matmul(tops[0][:, t * (CH + 1):(t + 1) * (CH + 1)],
                                          summed[:, t * P:(t + 1) * P], w_value[:], start=True, stop=True)
                mm.then_inc(S["o_ready"], 1)

            pe.wait_ge(S["set_b"], 3)

            def chunk(j, slot):
                pe.wait_ge(S["t_used"], j + 1)
                turn(j, slot)

            first_batch(pe, chunk)
            pe.wait_ge(S["t_used"], CHUNKS + 2)
            queries(0, 0, 0)
            pe.wait_ge(S["g_high"], 1)
            pe.wait_ge(S["set_w"], 1)
            for k in range(MAXES):
                top(0, k, 0)
            pe.wait_ge(S["top_used"], MAXES)
            row(0)
            pe.wait_ge(S["set_c"], 1)
            for u in range(EARLY):
                score(0, u, 0)

            def step(n, p, c, nxt, prep):
                for i, pair in enumerate(PAIRS):
                    if i == len(PAIRS) - 1:
                        ahead = [(n + 1, u, nxt[0]) for u in PAIRS[0]] if nxt else []
                    else:
                        ahead = [(n, u, p) for u in PAIRS[i + 1] if u >= EARLY]
                    tiles = [(*job, k) for job in ahead for k in range(len(tiles_of(job[1])))]
                    if nxt and i == ROW_AT:
                        row(n + 1)
                    for place in range(5):
                        next_tops(n, [k for k, at in tops_at(i).items() if at == place], nxt, prep)
                        if place < len(tiles):
                            score(*tiles[place])
                    if nxt and i == QUERIES_AT:
                        pe.wait_ge(S["t_used"], (n + CHUNKS if prep else STEPS) + 2)
                        queries(n + 1, *nxt)
                    if prep and i == TURN_AT:
                        pe.wait_ge(S["g_used"], n + 2)
                        turn(n + CHUNKS)
                    for u in pair:
                        weigh(n, u, p)
                if nxt:
                    for u in range(2, EARLY):
                        score(n + 1, u, nxt[0])
                project(n)

            steps(pe, step)

        @block.vector
        def _(dve):
            dve.sem_inc(S["t_used"], 2)
            dve.sem_inc(S["row_used"], 1)
            dve.sem_inc(S["o_used"], 1)
            dve.sem_inc(S["p_done"], UNITS)
            dve.sem_inc(S["acc_used"], 1)

            for a in range(2):
                nc.vector.tensor_scalar(wvd[:, a, 0:CH - 1], wv[:, 0:CH - 1], wv[:, CH - 1:CH], None,
                                        ALU.subtract).then_inc(S["set_a"], 1)
            dve.wait_ge(S["w_mm"], 1)
            nc.vector.tensor_scalar(w_query[:], misc[:, 0:CH + 1], CH ** -0.5, None, ALU.mult).then_inc(S["set_b"], 1)
            dve.wait_ge(S["w_mm"], 2)
            nc.vector.tensor_scalar(b_query[:], tops[0][0:CH + 1, 0:1], CH ** -0.5, None, ALU.mult).then_inc(S["set_b"], 1)
            dve.wait_ge(S["w_mm"], 3)
            nc.vector.tensor_copy(w_value[:, 0:CH], tops[1][:, 0:CH]).then_inc(S["set_b"], 1)


            low = slice(E0 + 32, E1)
            dve.wait_ge(S["wave_high"], 1)
            nc.vector.scalar_tensor_tensor(out=keys1[low, 0:SEQ], in0=waves_q[32:EXTRA, :], scalar=beta_col[low, 0:1],
                                           in1=keys1[low, 0:SEQ].bitcast(F32), op0=ALU.mult,
                                           op1=ALU.subtract).then_inc(S["set_w"], 1)
            def chunk_mean(n):
                stat = ds((n + CHUNKS) * CHUNK_TILES, CHUNK_TILES)
                nc.vector.tensor_reduce(total[:], residual[:, stat, :], AX.X, ALU.add).then_inc(S["m_sum"], 1)
                dve.wait_ge(S["m_sum"], n + 1)
                nc.vector.tensor_scalar(mean[:, stat], total[:], 1.0 / CH, None, ALU.mult).then_inc(S["m_mean"], 1)

            def chunk_variance(n):
                dve.wait_ge(S["m_sq"], n + 1)
                nc.vector.tensor_reduce(squares[:], squared[:], AX.X, ALU.add).then_inc(S["m_ss"], 1)
                dve.wait_ge(S["m_ss"], n + 1)
                nc.vector.tensor_scalar(variance[:], squares[:], 1.0 / CH, EPS, ALU.mult, ALU.add).then_inc(S["m_var"], 1)

            def keys_low(j, p, c, slot=0):
                at = ds(p * SEQ + c * CHUNK, CHUNK)
                dve.wait_ge(S["t_high"], j * 2 + 2)
                nc.vector.tensor_tensor(keys2[0:CH, at], turned[0:CH, slot, 0:CHUNK], keys1[0:CH, at].bitcast(F32),
                                        ALU.subtract).then_inc(S["t_used"], 1)

            def query_low(r):
                dve.wait_ge(S["g_high"], r + 1)
                nc.vector.scalar_tensor_tensor(
                    out=query2[CH:P, ds((r % 2) * CHUNK, CHUNK)], in0=misc[0:CH, 0:CHUNK],
                    scalar=b_query[0:CH, 0:1], in1=next_q[0:CH, :].bitcast(F32),
                    op0=ALU.add, op1=ALU.subtract).then_inc(S["g_used"], 1)

            def reduce(r, k):
                dve.wait_ge(S["top_done"], r * MAXES + (k + 1))
                if k < WHOLE * CHUNK_TILES:
                    j, t = divmod(k, CHUNK_TILES)
                    ins = nc.vector.tensor_reduce(maxima[:, t, j:j + 1], tops[k % 2][:, :], AX.X, ALU.max)
                else:
                    ins = nc.vector.tensor_reduce(maxima[:, :, WHOLE],
                                                  tops[k % 2][:, 0:CHUNK_TILES * REST].rearrange("p (t n) -> p t n", n=REST),
                                                  AX.X, ALU.max)
                ins.then_inc(S["top_used"], 1)

            def shift_row(r):
                dve.wait_ge(S["top_used"], r * MAXES + MAXES)
                nc.vector.tensor_reduce(maximum[:], maxima[:], AX.X, ALU.max).then_inc(S["max_done"], 1)
                dve.wait_ge(S["row_mm"], r + 1)
                dve.wait_ge(S["ext_ready"], 2 * r + 2)
                nc.vector.tensor_tensor(query1[E0:E0 + 1, ds((r % 2) * CHUNK, CHUNK)],
                                        next_q[E0:E0 + 1, :].bitcast(F32), tops[1][0:1, 0:CHUNK],
                                        ALU.subtract).then_inc(S["row_used"], 1)

            def add_update(n):
                out = tops[0][:, 0:CHUNK_TILES * (CH + 1)].rearrange("p (t c) -> p t c", c=CH + 1)
                at = ds(n * CHUNK_TILES, CHUNK_TILES)
                dve.wait_ge(S["o_ready"], n + 1)
                nc.vector.reciprocal(recip[:], out[:, :, CH]).then_inc(S["o_rec"], 1)
                dve.wait_ge(S["o_rec"], n + 1)
                nc.vector.tensor_tensor(update[:], out[:, :, 0:CH],
                                        recip[:].unsqueeze(2).broadcast_to([P, CHUNK_TILES, CH]),
                                        ALU.mult).then_inc(S["o_used"], 1)
                dve.wait_ge(S["o_used"], n + 2)
                nc.vector.tensor_tensor(residual[:, at, :], residual[:, at, :], update[:], ALU.add).then_inc(S["o_mul"], 1)

            first_batch(dve, lambda j, slot: keys_low(j, 0, j, slot))
            query_low(0)
            for k in range(MAXES):
                reduce(0, k)
            shift_row(0)

            def step(n, p, c, nxt, prep):
                if prep:
                    chunk_mean(n)
                if nxt:
                    query_low(n + 1)
                for k in range(MAXES):
                    if nxt:
                        reduce(n + 1, k)
                    if k == SQUARES_AFTER and prep:
                        chunk_variance(n)
                    if k == T_LOW_AFTER and prep:
                        keys_low(n + CHUNKS, 1 - p, c)
                if nxt:
                    shift_row(n + 1)
                add_update(n)

            steps(dve, step)


def experts(nc, d, residual, eye, out):
    GROUP = 4
    GROUPS = ALL_TILES // GROUP
    COLS = GROUP * P
    AHEAD = 4
    SLOTS = 8
    with ExitStack() as ctx:
        def sb(name, shape, dt=F32):
            return ctx.enter_context(nc.sbuf_tensor(name, shape, dt))

        def sem(name):
            return ctx.enter_context(nc.semaphore(name))

        w1_raw = sb("w1_raw", [P, EXPERTS, HIDDEN])
        w1_high = sb("w1_high", [P, EXPERTS, HIDDEN], F32R)
        w1_low = sb("w1_low", [P, EXPERTS, HIDDEN], F32R)
        b1 = sb("b1", [HIDDEN, EXPERTS])
        w2 = sb("w2", [HIDDEN, EXPERTS, CH])
        b2_raw = sb("b2_raw", [48, CH])
        b2_high = sb("b2_high", [48, P], F32R)
        b2_low = sb("b2_low", [48, P], F32R)
        gate_raw = sb("gate_raw", [P, EXPERTS])
        gate_w = sb("gate_w", [P, 2, EXPERTS], F32R)
        gate_bias = sb("gate_bias", [P, 1, EXPERTS])
        pick_raw = sb("pick_raw", [48, EXPERTS * P])
        pick = sb("pick", [48, EXPERTS * P], F32R)
        iota = sb("iota", [P, 1, EXPERTS])
        gamma = sb("gamma", [P, 1, CH])
        beta = sb("beta", [P, 1, CH])
        half = sb("half", [P, GROUP])

        z = sb("z", [P, GROUP, CH])
        both = sb("both", [P, P], F32R)
        halves = sb("halves", [P, 2, COLS], F32R)
        gates_t = sb("gates_t", [48, 2, COLS], F32R)
        hidden = sb("hidden", [P, SLOTS, COLS])
        gated = sb("gated", [P, SLOTS, COLS])
        moe = sb("moe", [P, COLS])
        n1 = {k: sb("n1_" + k, s) for k, s in (("sum", [P, GROUP]), ("mean", [P, GROUP]), ("cent", [P, GROUP, CH]),
                                             ("sq", [P, GROUP, CH]), ("ss", [P, GROUP]), ("var", [P, GROUP]), ("rstd", [P, GROUP]))}
        n2 = {k: sb("n2_" + k, s) for k, s in (("sum", [P, GROUP]), ("mean", [P, GROUP]), ("cent", [P, GROUP, CH]),
                                             ("sq", [P, GROUP, CH]), ("ss", [P, GROUP]), ("var", [P, GROUP]), ("rstd", [P, GROUP]))}
        y = sb("y", [P, GROUP, CH])
        o1, o2, o3 = (sb(f"o{i}", [P, GROUP, CH]) for i in (1, 2, 3))
        result = sb("result", [P, 2, GROUP, CH])
        biased = sb("biased", [P, GROUP, EXPERTS])
        logits = sb("logits", [P, GROUP, EXPERTS])
        best = sb("best", [P, GROUP, 8])
        where = sb("where", [P, GROUP, 8], U32)
        where_f = sb("where_f", [P, GROUP, 2])
        gap = sb("gap", [P, GROUP])
        ratio = sb("ratio", [P, GROUP])
        one_up = sb("one_up", [P, GROUP])
        weight = sb("weight", [P, 2, GROUP])
        is0 = sb("is0", [P, GROUP, EXPERTS])
        is1 = sb("is1", [P, GROUP, EXPERTS])
        by0 = sb("by0", [P, GROUP, EXPERTS])
        by1 = sb("by1", [P, GROUP, EXPERTS])
        gates = sb("gates", [P, GROUP, EXPERTS])

        def psum(name):
            return ctx.enter_context(nc.psum_tensor(name, [P, BANK], F32))

        ps_hid = [psum(f"ps_hid{i}") for i in range(2)]
        ps_gate = [psum(f"ps_gate{i}") for i in range(AHEAD)]
        ps_moe = psum("ps_moe")
        ps_misc = psum("ps_misc")

        names = ("pe_passed", "pool_passed", "dve_passed", "w_in", "w_cast", "w1_high", "w1_low", "b2_zero", "power_set",
                 "n_dve", "c_dve", "p_cent", "p_sq", "p_rstd", "z_ready", "z_turned", "z_high", "z_low", "log_ready",
                 "ratio_ready", "gates_turned", "g_high", "g_low",
                 "hid_ready", "relu_ready", "gate_ready", "gated_ready", "moe_done", "moe_used",
                 "q_dve", "q_cent", "q_sq", "q_rstd", "out_turned", "y_ready", "o_chain", "result_ready", "stored0", "stored1")
        S = {n: sem(n) for n in names}
        block = ctx.enter_context(nc.Block())

        N_OPS = Q_OPS = 4
        MASKS = 2 + 2 * GROUP + 4
        C_OPS = MASKS + 6

        QUAD = AHEAD
        PE_AT = {"z": 0, "logits": 0, "out": 4, "gates": 8}
        ACT_AT = {"z": 3, "moe": 5, "exp": 8, "gates": 13}
        DVE_AT = {"z": 2, "choose": 5, "mean": 7, "weights": 8, "var": 9, "add": 9, "gates": 12, "post_var": 14}

        def steps(eng, step):
            step(0, 0, True, False)
            with eng.Fori(0, (GROUPS - 2) // 2) as i:
                for k in range(2):
                    step(i * 2 + (1 + k), 1 - k, True, True)
            step(GROUPS - 1, 1, False, True)

        W_LOADS = 16 * 16

        @block.sync
        def _(sp):
            for k in range(2):
                rows = slice(k * CH, (k + 1) * CH)
                sp.dma_start(w1_raw[rows], d["L0_ffn_w1"].rearrange("e c f -> c e f")).then_inc(S["w_in"], 16)
                sp.dma_start(gate_raw[rows], d["L0_ffn_gate_w"]).then_inc(S["w_in"], 16)
            sp.dma_start(w2[:], d["L0_ffn_w2"].rearrange("e f c -> f e c")).then_inc(S["w_in"], 16)
            sp.dma_start(pick_raw[:], d["pick"]).then_inc(S["w_in"], 16)
            sp.dma_start(iota[:, 0, :], d["iota"]).then_inc(S["w_in"], 16)
            sp.dma_start(gate_bias[:, 0, :], d["L0_ffn_gate_b"].partition_broadcast(P)).then_inc(S["w_in"], 16)
            sp.dma_start(gamma[:, 0, :], d["L0_ffn_gamma"].partition_broadcast(P)).then_inc(S["w_in"], 16)
            sp.dma_start(beta[:, 0, :], d["L0_ffn_beta"].partition_broadcast(P)).then_inc(S["w_in"], 16)
            with nc.allow_non_contiguous_dma("a small transposed load"):
                for k in range(4):
                    sp.dma_start(b1[:, 4 * k:4 * k + 4],
                                 d["L0_ffn_b1"][4 * k:4 * k + 4].rearrange("e f -> f e")).then_inc(S["w_in"], 16)
            sp.wait_ge(S["b2_zero"], 1)
            for k in range(2):
                sp.dma_start(b2_raw[32 * k:32 * k + EXPERTS, :], d["L0_ffn_b2"]).then_inc(S["w_in"], 16)

            flat = out.rearrange("b (t p) c -> (b t) p c", p=P)

            def store(g, p):
                sp.wait_ge(S["result_ready"], g + 1)
                sp.dma_start(flat[ds(g * GROUP, GROUP)].rearrange("t p c -> p t c"),
                             result[:, p]).then_inc(S[f"stored{p}"], 16)

            def step(g, p, prep, post):
                if post:
                    store(g - 1, 1 - p)

            steps(sp, step)
            store(GROUPS - 1, 1)
            sp.wait_ge(S["stored0"], 16 * (GROUPS // 2))
            sp.wait_ge(S["stored1"], 16 * (GROUPS // 2) + 16)

        def norm_on_pool(pool, n, x, r, pre):
            dve, ops = (S["n_dve"], N_OPS) if pre else (S["q_dve"], Q_OPS)
            cent, sq = (S["p_cent"], S["p_sq"]) if pre else (S["q_cent"], S["q_sq"])
            pool.wait_ge(dve, r * ops + 2)
            nc.gpsimd.tensor_tensor(n["cent"][:], x, n["mean"][:].unsqueeze(2).broadcast_to([P, GROUP, CH]),
                                    ALU.subtract).then_inc(cent, 1)
            pool.wait_ge(cent, r + 1)
            nc.gpsimd.tensor_tensor(n["sq"][:], n["cent"][:], n["cent"][:], ALU.mult).then_inc(sq, 1)

        def root_on_pool(pool, n, r, pre):
            dve, ops = (S["n_dve"], N_OPS) if pre else (S["q_dve"], Q_OPS)
            rstd = S["p_rstd"] if pre else S["q_rstd"]
            pool.wait_ge(dve, r * ops + 4)
            nc.gpsimd.tensor_tensor(n["rstd"][:], n["var"][:], half[:], ALU.pow).then_inc(rstd, 1)
            pool.wait_ge(rstd, r + 1)

        @block.gpsimd
        def _(pool):
            nc.gpsimd.memset(b2_raw[:], 0.0).then_inc(S["b2_zero"], 1)
            nc.gpsimd.memset(half[:], -0.5).then_inc(S["power_set"], 1)
            pool.wait_ge(S["power_set"], 1)

            def rows_of(g):
                return residual[:, ds(g * GROUP, GROUP), :]

            def prep(r):
                norm_on_pool(pool, n1, rows_of(r % GROUPS), r, True)
                root_on_pool(pool, n1, r, True)
                if not (isinstance(r, int) and r == 0):
                    pool.wait_ge(S["z_turned"], r)
                nc.gpsimd.tensor_tensor(z[:], n1["cent"][:], n1["rstd"][:].unsqueeze(2).broadcast_to([P, GROUP, CH]),
                                        ALU.mult).then_inc(S["z_ready"], 1)

            def post_a(r):
                norm_on_pool(pool, n2, y[:], r, False)

            def post_b(r, p):
                root_on_pool(pool, n2, r, False)
                chain = [(o1, n2["cent"][:], n2["rstd"][:].unsqueeze(2), ALU.mult),
                         (o2, o1[:], gamma[:], ALU.mult),
                         (o3, o2[:], beta[:], ALU.add)]
                for k, (to, a, b, op) in enumerate(chain):
                    nc.gpsimd.tensor_tensor(to[:], a, b.broadcast_to([P, GROUP, CH]), op).then_inc(S["o_chain"], 1)
                    pool.wait_ge(S["o_chain"], r * 3 + (k + 1))
                pool.wait_ge(S[f"stored{p}"], (r // 2) * 16 + 16)
                nc.gpsimd.tensor_tensor(result[:, p], o3[:], rows_of(r), ALU.add).then_inc(S["result_ready"], 1)

            prep(0)
            prep(1)

            def step(g, p, nxt, post):
                if nxt:
                    prep(g + 2)
                if post:
                    post_a(g - 1)
                    post_b(g - 1, 1 - p)

            steps(pool, step)
            post_a(GROUPS - 1)
            post_b(GROUPS - 1, 1)

        @block.scalar
        def _(act):
            act.sem_inc(S["stored0"], 16)
            act.sem_inc(S["stored1"], 16)
            act.sem_inc(S["relu_ready"], EXPERTS)
            act.sem_inc(S["moe_used"], 1)

            def high_z(r, p):
                act.wait_ge(S["z_turned"], r + 1)
                nc.scalar.activation(halves[0:CH, p, :], ps_misc[0:CH, :], ACT.Identity).then_inc(S["z_high"], 1)

            def exp_gap(r):
                act.wait_ge(S["c_dve"], r * C_OPS + MASKS - 3)
                nc.scalar.activation(ratio[:], gap[:], ACT.Exp).then_inc(S["ratio_ready"], 1)

            def high_gates(r, p):
                act.wait_ge(S["gates_turned"], r + 1)
                nc.scalar.activation(gates_t[0:EXPERTS, p, :], ps_misc[0:EXPERTS, :], ACT.Identity).then_inc(S["g_high"], 1)

            def take_moe(g):
                act.wait_ge(S["moe_done"], (g + 1) * EXPERTS)
                nc.scalar.activation(moe[:], ps_moe[:], ACT.Identity).then_inc(S["moe_used"], 1)

            def relu(g, e):
                act.wait_ge(S["hid_ready"], g * EXPERTS + (e + 1))
                act.wait_ge(S["gated_ready"], g * EXPERTS + (e + 1 - SLOTS + EXPERTS))
                nc.scalar.activation(hidden[:, e % SLOTS, :], ps_hid[e % 2][:, :], ACT.Relu,
                                     bias=b1[:, e:e + 1]).then_inc(S["relu_ready"], 1)

            high_z(0, 0)
            act.wait_ge(S["w_in"], W_LOADS)
            nc.scalar.activation(w1_high[:], w1_raw[:], ACT.Identity).then_inc(S["w1_high"], 1)
            nc.scalar.activation(pick[:], pick_raw[:], ACT.Identity).then_inc(S["w1_high"], 1)
            exp_gap(0)
            high_gates(0, 0)

            def step(g, p, prep, post):
                for e in range(EXPERTS):
                    relu(g, e)
                    if prep and e == ACT_AT["z"]:
                        high_z(g + 1, 1 - p)
                    if prep and e == ACT_AT["exp"]:
                        exp_gap(g + 1)
                    if prep and e == ACT_AT["gates"]:
                        high_gates(g + 1, 1 - p)
                    if post and e == ACT_AT["moe"]:
                        take_moe(g - 1)

            steps(act, step)
            take_moe(GROUPS - 1)

        @block.tensor
        def _(pe):

            def turn_z(r):
                pe.wait_ge(S["z_ready"], r + 1)
                stand_alone(pe, S["pe_passed"])
                for t in range(GROUP):
                    mm = nc.tensor.transpose(ps_misc[0:CH, t * P:(t + 1) * P], z[:, t, :], eye[:])
                mm.then_inc(S["z_turned"], 1)

            def gate_logits(r, p):
                pe.wait_ge(S["z_low"], r + 1)
                for t in range(GROUP):
                    mm = nc.tensor.matmul(ps_misc[:, 2 * t * EXPERTS:2 * (t + 1) * EXPERTS],
                                          halves[:, p, t * P:(t + 1) * P], gate_w[:].rearrange("p h e -> p (h e)"),
                                          start=True, stop=True)
                mm.then_inc(S["log_ready"], 1)

            def turn_gates(r):
                pe.wait_ge(S["c_dve"], (r + 1) * C_OPS)
                pe.wait_ge(S["y_ready"], r)
                for t in range(GROUP):
                    mm = nc.tensor.transpose(ps_misc[0:EXPERTS, t * P:(t + 1) * P], gates[:, t, :], eye[:])
                mm.then_inc(S["gates_turned"], 1)

            def hid(g, e, p):
                if e == 0:
                    pe.wait_ge(S["z_low"], g + 1)
                pe.wait_ge(S["relu_ready"], g * EXPERTS + (e - 1 + EXPERTS))
                nc.tensor.matmul(ps_hid[e % 2][:, :], w1_high[:, e, :], halves[:, p, :], start=True, stop=False)
                nc.tensor.matmul(ps_hid[e % 2][:, :], w1_low[:, e, :], halves[:, p, :],
                                 start=False, stop=True).then_inc(S["hid_ready"], 1)

            def gate(g, e, p):
                if e == 0:
                    pe.wait_ge(S["g_low"], g + 1)
                pe.wait_ge(S["gated_ready"], g * EXPERTS + (e + 1 - AHEAD + EXPERTS))
                nc.tensor.matmul(ps_gate[e % AHEAD][:, :], pick[:, e * P:(e + 1) * P], gates_t[:, p, :],
                                 start=True, stop=True).then_inc(S["gate_ready"], 1)

            def second(g, e, p):
                pe.wait_ge(S["gated_ready"], g * EXPERTS + (e + 2 + EXPERTS))
                if e == 0:
                    pe.wait_ge(S["moe_used"], g + 1)
                    nc.tensor.matmul(ps_moe[:, :], both[:], halves[:, p, :], start=True, stop=False,
                                     skip_group_check=True)
                    for part in (b2_high, b2_low):
                        nc.tensor.matmul(ps_moe[:, :], part[:], gates_t[:, p, :], start=False, stop=False,
                                         skip_group_check=True)
                for h in range(2):
                    mm = nc.tensor.matmul(ps_moe[h * CH:(h + 1) * CH, :], w2[:, e + h, :], gated[:, (e + h) % SLOTS, :],
                                          start=False, stop=(e == EXPERTS - 2), skip_group_check=True)
                mm.then_inc(S["moe_done"], 2)

            def turn_out(g, last=False):
                pe.wait_ge(S["moe_used"], g + 2)
                if last:
                    pe.wait_ge(S["y_ready"], g + 1)
                else:
                    pe.wait_ge(S["c_dve"], (g + 2) * C_OPS + 2)
                for t in range(GROUP):
                    mm = nc.tensor.transpose(ps_misc[:, t * P:(t + 1) * P], moe[:, t * P:(t + 1) * P], eye[:])
                mm.then_inc(S["out_turned"], 1)

            turn_z(0)
            pe.wait_ge(S["w_in"], W_LOADS)
            pe.wait_ge(S["w_cast"], 11)
            gate_logits(0, 0)
            turn_gates(0)
            pe.wait_ge(S["w1_high"], 2)
            pe.wait_ge(S["w1_low"], 1)
            for e in range(AHEAD):
                hid(0, e, 0)
                gate(0, e, 0)

            def step(g, p, prep, post):
                for e in range(0, EXPERTS, QUAD):
                    if prep and e == PE_AT["z"]:
                        turn_z(g + 1)
                    def layers(*order):
                        for layer, k in order:
                            if e + AHEAD < EXPERTS:
                                layer(g, e + AHEAD + k, p)
                            elif prep:
                                layer(g + 1, k, 1 - p)

                    layers((hid, 0), (hid, 1), (gate, 0), (gate, 1))
                    if prep and e == PE_AT["logits"]:
                        gate_logits(g + 1, 1 - p)
                    if post and e == PE_AT["out"]:
                        turn_out(g - 1, last=not prep)
                    if prep and e == PE_AT["gates"]:
                        turn_gates(g + 1)
                    layers((hid, 2), (gate, 2), (hid, 3), (gate, 3))
                    for k in range(e, e + QUAD, 2):
                        second(g, k, p)

            steps(pe, step)
            turn_out(GROUPS - 1, last=True)

        @block.vector
        def _(dve):
            dve.sem_inc(S["gated_ready"], EXPERTS)
            dve.sem_inc(S["y_ready"], 1)
            for p in range(2):
                nc.vector.memset(gates_t[:, p, :].bitcast(F32), 0.0).then_inc(S["w_cast"], 1)
            for part in (b2_high, b2_low, both):
                nc.vector.memset(part[:].bitcast(F32), 0.0).then_inc(S["w_cast"], 1)

            def small_weights():
                dve.wait_ge(S["w_in"], W_LOADS)
                nc.vector.tensor_copy(gate_w[:, 0], gate_raw[:]).then_inc(S["w_cast"], 1)
                dve.wait_ge(S["w_cast"], 6)
                nc.vector.tensor_tensor(gate_w[:, 1], gate_raw[:], gate_w[:, 0].bitcast(F32), ALU.subtract).then_inc(S["w_cast"], 1)
                nc.vector.tensor_copy(b2_high[:, 0:CH], b2_raw[:]).then_inc(S["w_cast"], 1)
                for h in range(2):
                    rows = slice(h * CH, (h + 1) * CH)
                    nc.vector.tensor_copy(both[rows, 0:CH], eye[rows, rows]).then_inc(S["w_cast"], 1)
                dve.wait_ge(S["w_cast"], 8)
                nc.vector.tensor_tensor(b2_low[:, 0:CH], b2_raw[:], b2_high[:, 0:CH].bitcast(F32),
                                        ALU.subtract).then_inc(S["w_cast"], 1)

            def linked(name, base):
                k = [0]

                def link(ins, wait=True):
                    k[0] += 1
                    ins.then_inc(S[name], 1)
                    if wait:
                        dve.wait_ge(S[name], base + k[0])
                return link

            def mean_of(link, n, x):
                link(nc.vector.tensor_reduce(n["sum"][:], x, AX.X, ALU.add))
                link(nc.vector.tensor_scalar(n["mean"][:], n["sum"][:], 1.0 / CH, None, ALU.mult), False)

            def prep_mean(r):
                link = linked("n_dve", r * N_OPS)
                if not (isinstance(r, int) and r == 0):
                    dve.wait_ge(S["z_ready"], r)
                mean_of(link, n1, residual[:, ds(r % GROUPS * GROUP, GROUP), :])

            def prep_var(r):
                dve.wait_ge(S["p_sq"], r + 1)
                link = linked("n_dve", r * N_OPS + 2)
                link(nc.vector.tensor_reduce(n1["ss"][:], n1["sq"][:], AX.X, ALU.add))
                link(nc.vector.tensor_scalar(n1["var"][:], n1["ss"][:], 1.0 / CH, EPS, ALU.mult, ALU.add), False)

            def low_z(r, p):
                dve.wait_ge(S["z_high"], r + 1)
                nc.vector.tensor_tensor(halves[CH:P, p, :], ps_misc[0:CH, :], halves[0:CH, p, :].bitcast(F32),
                                        ALU.subtract).then_inc(S["z_low"], 1)

            def choose(r):
                dve.wait_ge(S["log_ready"], r + 1)
                link = linked("c_dve", r * C_OPS)
                parts = ps_misc[:, 0:2 * GROUP * EXPERTS].rearrange("p (t h e) -> p h t e", h=2, e=EXPERTS)
                link(nc.vector.tensor_tensor(biased[:], parts[:, 1], gate_bias[:].broadcast_to([P, GROUP, EXPERTS]), ALU.add))
                link(nc.vector.tensor_tensor(logits[:], parts[:, 0], biased[:], ALU.add))
                stand_alone(dve, S["dve_passed"])
                for t in range(GROUP):
                    link(nc.vector.max(best[:, t, :], logits[:, t, :]), t == GROUP - 1)
                stand_alone(dve, S["dve_passed"])
                for t in range(GROUP):
                    link(nc.vector.max_index(where[:, t, :], best[:, t, :], logits[:, t, :]), False)
                link(nc.vector.tensor_tensor(gap[:], best[:, :, 1], best[:, :, 0], ALU.subtract))
                link(nc.vector.tensor_copy(where_f[:], where[:, :, 0:2]))
                full = [P, GROUP, EXPERTS]
                for k, to in enumerate((is0, is1)):
                    link(nc.vector.tensor_tensor(to[:], iota[:].broadcast_to(full),
                                                 where_f[:, :, k:k + 1].broadcast_to(full), ALU.is_equal), False)

            def fill_gates(r):
                full = [P, GROUP, EXPERTS]
                dve.wait_ge(S["ratio_ready"], r + 1)
                link = linked("c_dve", r * C_OPS + MASKS)
                link(nc.vector.tensor_scalar(one_up[:], ratio[:], 1.0, None, ALU.add))
                link(nc.vector.reciprocal(weight[:, 0, :], one_up[:]))
                link(nc.vector.tensor_tensor(weight[:, 1, :], weight[:, 0, :], ratio[:], ALU.mult))
                link(nc.vector.tensor_tensor(by0[:], is0[:], weight[:, 0, :].unsqueeze(2).broadcast_to(full), ALU.mult))
                link(nc.vector.tensor_tensor(by1[:], is1[:], weight[:, 1, :].unsqueeze(2).broadcast_to(full), ALU.mult))
                link(nc.vector.tensor_tensor(gates[:], by0[:], by1[:], ALU.add), False)

            def low_gates(r, p):
                dve.wait_ge(S["g_high"], r + 1)
                nc.vector.tensor_tensor(gates_t[32:32 + EXPERTS, p, :], ps_misc[0:EXPERTS, :],
                                        gates_t[0:EXPERTS, p, :].bitcast(F32), ALU.subtract).then_inc(S["g_low"], 1)

            def weigh(g, e):
                dve.wait_ge(S["relu_ready"], g * EXPERTS + (e + 1 + EXPERTS))
                dve.wait_ge(S["gate_ready"], g * EXPERTS + (e + 1))
                if not (isinstance(g, int) and g == 0 and e < SLOTS):
                    dve.wait_ge(S["moe_done"], g * EXPERTS + (e // 2 * 2 + 2 - SLOTS))
                nc.vector.tensor_tensor(gated[:, e % SLOTS, :], hidden[:, e % SLOTS, :], ps_gate[e % AHEAD][:, :],
                                        ALU.mult).then_inc(S["gated_ready"], 1)

            def add_halves(r):
                dve.wait_ge(S["out_turned"], r + 1)
                two = ps_misc[:].rearrange("p (t h c) -> p t c h", t=GROUP, h=2)
                nc.vector.tensor_reduce(y[:], two, AX.X, ALU.add).then_inc(S["y_ready"], 1)

            def post_mean(r):
                dve.wait_ge(S["y_ready"], r + 2)
                link = linked("q_dve", r * Q_OPS)
                mean_of(link, n2, y[:])

            def post_var(r):
                dve.wait_ge(S["q_sq"], r + 1)
                link = linked("q_dve", r * Q_OPS + 2)
                link(nc.vector.tensor_reduce(n2["ss"][:], n2["sq"][:], AX.X, ALU.add))
                link(nc.vector.tensor_scalar(n2["var"][:], n2["ss"][:], 1.0 / CH, EPS, ALU.mult, ALU.add), False)

            for r in range(2):
                prep_mean(r)
                prep_var(r)
            small_weights()
            low_z(0, 0)
            dve.wait_ge(S["w1_high"], 1)
            nc.vector.tensor_tensor(w1_low[:], w1_raw[:], w1_high[:].bitcast(F32), ALU.subtract).then_inc(S["w1_low"], 1)
            choose(0)
            fill_gates(0)
            low_gates(0, 0)

            def step(g, p, prep, post):
                for e in range(EXPERTS):
                    weigh(g, e)
                    if prep and e == DVE_AT["mean"]:
                        prep_mean(g + 2)
                    if post and e == DVE_AT["add"]:
                        add_halves(g - 1)
                        post_mean(g - 1)
                    if prep and e == DVE_AT["var"]:
                        prep_var(g + 2)
                    if post and e == DVE_AT["post_var"]:
                        post_var(g - 1)
                    if prep and e == DVE_AT["z"]:
                        low_z(g + 1, 1 - p)
                    if prep and e == DVE_AT["choose"]:
                        choose(g + 1)
                    if prep and e == DVE_AT["weights"]:
                        fill_gates(g + 1)
                    if prep and e == DVE_AT["gates"]:
                        low_gates(g + 1, 1 - p)

            steps(dve, step)
            add_halves(GROUPS - 1)
            post_mean(GROUPS - 1)
            post_var(GROUPS - 1)


def early_fusion(nc, d, out):
    with ExitStack() as ctx:
        def sb(name, shape, dt=F32):
            return ctx.enter_context(nc.sbuf_tensor(name, shape, dt))

        residual = sb("residual", [P, ALL_TILES, CH])
        mean = sb("mean", [P, ALL_TILES])
        rstd = sb("rstd", [P, ALL_TILES])
        eye = sb("eye", [P, P])
        weights = AttentionWeights(nc, ctx)
        tokenise(nc, d, weights, residual, mean, rstd, eye)
        attend(nc, d, weights, residual, mean, rstd, eye)
        experts(nc, d, residual, eye, out)


def kernel(**inputs):
    import concourse.bacc as _bacc
    from concourse.bass_utils import run_bass_kernel_spmd as _run

    nc = _bacc.Bacc("TRN2", target_bir_lowering=False, num_devices=1)
    arrays, d = {}, {}
    for name, a in {**inputs, **constants()}.items():
        a = np.ascontiguousarray(a)
        arrays[f"in_{name}"] = a
        d[name] = nc.dram_tensor(f"in_{name}", a.shape, mybir.dt.from_np(a.dtype), kind="ExternalInput").ap()
    out = nc.dram_tensor("out_0", (BATCH, SEQ, CH), F32, kind="ExternalOutput").ap()
    early_fusion(nc, d, out)
    r = _run(nc, [arrays], core_ids=[0])
    return r.results[0]["out_0"]
```
